# Optimizing a Trainium2 kernel written in Bass

```python
import numpy as np
import jax
import jax.numpy as jnp

def _softmax(x, axis=-1):
    return jax.nn.softmax(x, axis=axis)

def _gelu(x):
    return jax.nn.gelu(x, approximate=True)

def _silu(x):
    return jax.nn.silu(x)

def _sigmoid(x):
    return jax.nn.sigmoid(x)

def _layernorm(x, axis=-1, eps=1e-05):
    m = jnp.mean(x, axis=axis, keepdims=True)
    v = jnp.var(x, axis=axis, keepdims=True)
    return (x - m) / jnp.sqrt(v + eps)

def _scatter_add(tgt, idx, src, axis=0):
    return tgt.at[idx].add(src)

def _segment_sum(src, seg, n):
    return jax.ops.segment_sum(src, seg, n)
kernel_name = 'mk_vit_tower_cls_d1_tok_img768_r4_ca2e52'

def setup_inputs(seed: int=0):
    np.random.seed(seed)
    _w = jnp.asarray

    def _rec_inputs():
        import jax
        import jax.numpy as jnp
        _rk = jax.random.key(seed)
        x = 7.57192e-06 + 1.00007 * jax.random.normal(jax.random.fold_in(_rk, 1), (16, 3, 128, 128), jnp.float32)
        cls_tok = 0.02 * jax.random.normal(jax.random.fold_in(_rk, 5), (1, 1, 192), jnp.float32)
        return (x, cls_tok)
    x, cls_tok = _rec_inputs()

    def _L0_tok_setup():
        import jax, jax.numpy as jnp
        import numpy as np
        B, IN, IMG = (64, 3, 224)
        PATCH, LEVELS, D = (16, 4, 192)
        ISQ2 = 0.7071067811865476
        DN = ('NCHW', 'OIHW', 'NCHW')

        def conv(x, w, b=None, stride=1, pad=((0, 0), (0, 0)), groups=1):
            y = jax.lax.conv_general_dilated(x, w, (stride, stride), pad, dimension_numbers=DN, feature_group_count=groups)
            return y if b is None else y + b[None, :, None, None]

        def dwconv(x, wd, wp, bp):
            y = conv(x, wd, pad=((1, 1), (1, 1)), groups=x.shape[1])
            return conv(y, wp, bp)

        def haar_dwt2(x):
            xe, xo = (x[..., ::2], x[..., 1::2])
            lo_w, hi_w = ((xe + xo) * ISQ2, (xe - xo) * ISQ2)

            def split_h(t):
                te, to = (t[..., ::2, :], t[..., 1::2, :])
                return ((te + to) * ISQ2, (te - to) * ISQ2)
            ll, lh = split_h(lo_w)
            hl, hh = split_h(hi_w)
            return (ll, lh, hl, hh)

        def wavelet_packet(x):
            f = x
            for _ in range(LEVELS):
                b, k, h, w = f.shape
                ll, lh, hl, hh = haar_dwt2(f)
                bands = jnp.stack([ll, lh, hl, hh], axis=1)
                bands = bands.reshape(b, 4, k // IN, IN, h // 2, w // 2)
                f = jnp.transpose(bands, (0, 2, 1, 3, 4, 5)).reshape(b, 4 * k, h // 2, w // 2)
            return f

        def gelu(x):
            return jax.nn.gelu(x, approximate=False)

        def forward(x, pl_w, pl_b, pl_dw, pl_pw, pl_pwb, pg_w1, pg_b1, pg_dw, pg_pw, pg_pwb, pg_w2, pg_b2, alpha, f1_dw, f1_pw, f1_pwb, f2_dw, f2_pw, f2_pwb, f3_dw, f3_pw, f3_pwb, ln_g, ln_b, cls):
            loc = conv(x, pl_w, pl_b, stride=PATCH)
            loc = dwconv(gelu(loc), pl_dw, pl_pw, pl_pwb)
            g = wavelet_packet(x)
            g = gelu(conv(g, pg_w1, pg_b1))
            g = gelu(dwconv(g, pg_dw, pg_pw, pg_pwb))
            glob = conv(g, pg_w2, pg_b2)
            gate = 0.5 * (jnp.tanh(alpha) + 1.0)
            h = (1.0 - gate) * loc + gate * glob
            h = jax.nn.relu(dwconv(h, f1_dw, f1_pw, f1_pwb))
            h = jax.nn.relu(dwconv(h, f2_dw, f2_pw, f2_pwb))
            h = dwconv(loc + h, f3_dw, f3_pw, f3_pwb)
            t = jnp.transpose(h.reshape(h.shape[0], D, -1), (0, 2, 1))
            mu = jnp.mean(t, -1, keepdims=True)
            var = jnp.mean((t - mu) ** 2, -1, keepdims=True)
            t = (t - mu) / jnp.sqrt(var + 1e-05) * ln_g + ln_b
            cls_tok = jnp.broadcast_to(cls, (t.shape[0], 1, D))
            return jnp.concatenate([cls_tok, t], axis=1)
        key = jax.random.key(seed)
        ks = jax.random.split(key, 32)

        def rn(i, shape, s=0.02):
            return jax.random.normal(ks[i], shape, jnp.float32) * s
        KW = IN * 4 ** LEVELS
        return {'x': jax.random.normal(ks[0], (B, IN, IMG, IMG), jnp.float32), 'pl_w': rn(1, (D, IN, PATCH, PATCH)), 'pl_b': rn(2, (D,)), 'pl_dw': rn(3, (D, 1, 3, 3)), 'pl_pw': rn(4, (D, D, 1, 1)), 'pl_pwb': rn(5, (D,)), 'pg_w1': rn(6, (D, KW, 1, 1)), 'pg_b1': rn(7, (D,)), 'pg_dw': rn(8, (D, 1, 3, 3)), 'pg_pw': rn(9, (D, D, 1, 1)), 'pg_pwb': rn(10, (D,)), 'pg_w2': rn(11, (D, D, 1, 1)), 'pg_b2': rn(12, (D,)), 'alpha': jnp.zeros((1, D, 1, 1), jnp.float32), 'f1_dw': rn(13, (D, 1, 3, 3)), 'f1_pw': rn(14, (D, D, 1, 1)), 'f1_pwb': rn(15, (D,)), 'f2_dw': rn(16, (D, 1, 3, 3)), 'f2_pw': rn(17, (D, D, 1, 1)), 'f2_pwb': rn(18, (D,)), 'f3_dw': rn(19, (D, 1, 3, 3)), 'f3_pw': rn(20, (D, D, 1, 1)), 'f3_pwb': rn(21, (D,)), 'ln_g': jnp.ones((D,), jnp.float32), 'ln_b': jnp.zeros((D,), jnp.float32), 'cls': rn(22, (1, 1, D))}
    _L0_tok_all = _L0_tok_setup()
    _L0_tok_in = {k: v for k, v in _L0_tok_all.items() if k in ('pl_w', 'pl_b', 'pl_dw', 'pl_pw', 'pl_pwb', 'pg_w1', 'pg_b1', 'pg_dw', 'pg_pw', 'pg_pwb', 'pg_w2', 'pg_b2', 'alpha', 'f1_dw', 'f1_pw', 'f1_pwb', 'f2_dw', 'f2_pw', 'f2_pwb', 'f3_dw', 'f3_pw', 'f3_pwb', 'ln_g', 'ln_b', 'cls')}
    del _L0_tok_all

    def _L0_attn_setup():
        import jax, jax.numpy as jnp
        import numpy as np
        HEADS = 12
        DIM_HEAD = 64
        SCALE = DIM_HEAD ** (-0.5)
        LN_EPS = 1e-05

        def _ternary(w):
            s = jnp.mean(jnp.abs(w))
            return jnp.clip(jnp.round(w / (s + 1e-08)), -1.0, 1.0) * s

        def _sparsify(x, sparsity):
            thr = jnp.quantile(jnp.abs(x), sparsity, axis=-1, keepdims=True)
            return jnp.where(jnp.abs(x) >= thr, x, 0.0)
        key = jax.random.key(seed)
        ks = jax.random.split(key, 4)
        b, n, dim = (16, 256, 192)
        inner = HEADS * DIM_HEAD
        return {'x': jax.random.normal(ks[0], (b, n, dim), dtype=jnp.float32), 'gamma': jnp.ones((dim,), jnp.float32), 'beta': jnp.zeros((dim,), jnp.float32), 'w_qkv': jax.random.normal(ks[1], (3 * inner, dim), jnp.float32) * 0.02, 'w_out': jax.random.normal(ks[2], (dim, inner), jnp.float32) * 0.02, 'b_out': jnp.zeros((dim,), jnp.float32), 'sparsity': jnp.float32(0.5)}
    _L0_attn_all = _L0_attn_setup()
    _L0_attn_in = {k: v for k, v in _L0_attn_all.items() if k in ('gamma', 'beta', 'w_qkv', 'w_out', 'b_out', 'sparsity')}
    del _L0_attn_all

    def _L0_ffn_setup():
        import jax, jax.numpy as jnp
        import numpy as np
        B, T, D, E, K = (4, 512, 192, 8, 2)
        H = 4 * D
        key = jax.random.key(seed)
        k0, k1, k2, k3, k4 = jax.random.split(key, 5)
        s = 0.02
        return {'x': jax.random.normal(k0, (B, T, D), jnp.float32), 'router_w': jax.random.uniform(k1, (E, D), jnp.float32, -s * 0.1, s * 0.1), 'Wg': jax.random.uniform(k2, (E, H, D), jnp.float32, -s * 0.4, s * 0.4), 'Wu': jax.random.uniform(k3, (E, H, D), jnp.float32, -s * 0.4, s * 0.4), 'Wd': jax.random.normal(k4, (E, D, H), jnp.float32) * 0.01}
    _L0_ffn_all = _L0_ffn_setup()
    _L0_ffn_in = {k: v for k, v in _L0_ffn_all.items() if k in ('router_w', 'Wg', 'Wu', 'Wd')}
    del _L0_ffn_all
    return {'x': x, 'cls_tok': cls_tok, 'L0_tok_pl_w': _L0_tok_in['pl_w'], 'L0_tok_pl_b': _L0_tok_in['pl_b'], 'L0_tok_pl_dw': _L0_tok_in['pl_dw'], 'L0_tok_pl_pw': _L0_tok_in['pl_pw'], 'L0_tok_pl_pwb': _L0_tok_in['pl_pwb'], 'L0_tok_pg_w1': _L0_tok_in['pg_w1'], 'L0_tok_pg_b1': _L0_tok_in['pg_b1'], 'L0_tok_pg_dw': _L0_tok_in['pg_dw'], 'L0_tok_pg_pw': _L0_tok_in['pg_pw'], 'L0_tok_pg_pwb': _L0_tok_in['pg_pwb'], 'L0_tok_pg_w2': _L0_tok_in['pg_w2'], 'L0_tok_pg_b2': _L0_tok_in['pg_b2'], 'L0_tok_alpha': _L0_tok_in['alpha'], 'L0_tok_f1_dw': _L0_tok_in['f1_dw'], 'L0_tok_f1_pw': _L0_tok_in['f1_pw'], 'L0_tok_f1_pwb': _L0_tok_in['f1_pwb'], 'L0_tok_f2_dw': _L0_tok_in['f2_dw'], 'L0_tok_f2_pw': _L0_tok_in['f2_pw'], 'L0_tok_f2_pwb': _L0_tok_in['f2_pwb'], 'L0_tok_f3_dw': _L0_tok_in['f3_dw'], 'L0_tok_f3_pw': _L0_tok_in['f3_pw'], 'L0_tok_f3_pwb': _L0_tok_in['f3_pwb'], 'L0_tok_ln_g': _L0_tok_in['ln_g'], 'L0_tok_ln_b': _L0_tok_in['ln_b'], 'L0_tok_cls': _L0_tok_in['cls'], 'L0_attn_gamma': _L0_attn_in['gamma'], 'L0_attn_beta': _L0_attn_in['beta'], 'L0_attn_w_qkv': _L0_attn_in['w_qkv'], 'L0_attn_w_out': _L0_attn_in['w_out'], 'L0_attn_b_out': _L0_attn_in['b_out'], 'L0_attn_sparsity': _L0_attn_in['sparsity'], 'L0_ffn_router_w': _L0_ffn_in['router_w'], 'L0_ffn_Wg': _L0_ffn_in['Wg'], 'L0_ffn_Wu': _L0_ffn_in['Wu'], 'L0_ffn_Wd': _L0_ffn_in['Wd']}

def reference(x, cls_tok, L0_tok_pl_w, L0_tok_pl_b, L0_tok_pl_dw, L0_tok_pl_pw, L0_tok_pl_pwb, L0_tok_pg_w1, L0_tok_pg_b1, L0_tok_pg_dw, L0_tok_pg_pw, L0_tok_pg_pwb, L0_tok_pg_w2, L0_tok_pg_b2, L0_tok_alpha, L0_tok_f1_dw, L0_tok_f1_pw, L0_tok_f1_pwb, L0_tok_f2_dw, L0_tok_f2_pw, L0_tok_f2_pwb, L0_tok_f3_dw, L0_tok_f3_pw, L0_tok_f3_pwb, L0_tok_ln_g, L0_tok_ln_b, L0_tok_cls, L0_attn_gamma, L0_attn_beta, L0_attn_w_qkv, L0_attn_w_out, L0_attn_b_out, L0_attn_sparsity, L0_ffn_router_w, L0_ffn_Wg, L0_ffn_Wu, L0_ffn_Wd):
    import jax
    import jax.numpy as jnp

    def _L0_tok_ref(x, pl_w, pl_b, pl_dw, pl_pw, pl_pwb, pg_w1, pg_b1, pg_dw, pg_pw, pg_pwb, pg_w2, pg_b2, alpha, f1_dw, f1_pw, f1_pwb, f2_dw, f2_pw, f2_pwb, f3_dw, f3_pw, f3_pwb, ln_g, ln_b, cls):
        import jax, jax.numpy as jnp
        import numpy as np
        B, IN, IMG = (64, 3, 224)
        PATCH, LEVELS, D = (16, 4, 192)
        ISQ2 = 0.7071067811865476
        DN = ('NCHW', 'OIHW', 'NCHW')

        def conv(x, w, b=None, stride=1, pad=((0, 0), (0, 0)), groups=1):
            y = jax.lax.conv_general_dilated(x, w, (stride, stride), pad, dimension_numbers=DN, feature_group_count=groups)
            return y if b is None else y + b[None, :, None, None]

        def dwconv(x, wd, wp, bp):
            y = conv(x, wd, pad=((1, 1), (1, 1)), groups=x.shape[1])
            return conv(y, wp, bp)

        def haar_dwt2(x):
            xe, xo = (x[..., ::2], x[..., 1::2])
            lo_w, hi_w = ((xe + xo) * ISQ2, (xe - xo) * ISQ2)

            def split_h(t):
                te, to = (t[..., ::2, :], t[..., 1::2, :])
                return ((te + to) * ISQ2, (te - to) * ISQ2)
            ll, lh = split_h(lo_w)
            hl, hh = split_h(hi_w)
            return (ll, lh, hl, hh)

        def wavelet_packet(x):
            f = x
            for _ in range(LEVELS):
                b, k, h, w = f.shape
                ll, lh, hl, hh = haar_dwt2(f)
                bands = jnp.stack([ll, lh, hl, hh], axis=1)
                bands = bands.reshape(b, 4, k // IN, IN, h // 2, w // 2)
                f = jnp.transpose(bands, (0, 2, 1, 3, 4, 5)).reshape(b, 4 * k, h // 2, w // 2)
            return f

        def gelu(x):
            return jax.nn.gelu(x, approximate=False)

        def forward(x, pl_w, pl_b, pl_dw, pl_pw, pl_pwb, pg_w1, pg_b1, pg_dw, pg_pw, pg_pwb, pg_w2, pg_b2, alpha, f1_dw, f1_pw, f1_pwb, f2_dw, f2_pw, f2_pwb, f3_dw, f3_pw, f3_pwb, ln_g, ln_b, cls):
            loc = conv(x, pl_w, pl_b, stride=PATCH)
            loc = dwconv(gelu(loc), pl_dw, pl_pw, pl_pwb)
            g = wavelet_packet(x)
            g = gelu(conv(g, pg_w1, pg_b1))
            g = gelu(dwconv(g, pg_dw, pg_pw, pg_pwb))
            glob = conv(g, pg_w2, pg_b2)
            gate = 0.5 * (jnp.tanh(alpha) + 1.0)
            h = (1.0 - gate) * loc + gate * glob
            h = jax.nn.relu(dwconv(h, f1_dw, f1_pw, f1_pwb))
            h = jax.nn.relu(dwconv(h, f2_dw, f2_pw, f2_pwb))
            h = dwconv(loc + h, f3_dw, f3_pw, f3_pwb)
            t = jnp.transpose(h.reshape(h.shape[0], D, -1), (0, 2, 1))
            mu = jnp.mean(t, -1, keepdims=True)
            var = jnp.mean((t - mu) ** 2, -1, keepdims=True)
            t = (t - mu) / jnp.sqrt(var + 1e-05) * ln_g + ln_b
            cls_tok = jnp.broadcast_to(cls, (t.shape[0], 1, D))
            return jnp.concatenate([cls_tok, t], axis=1)
        return forward(x, pl_w, pl_b, pl_dw, pl_pw, pl_pwb, pg_w1, pg_b1, pg_dw, pg_pw, pg_pwb, pg_w2, pg_b2, alpha, f1_dw, f1_pw, f1_pwb, f2_dw, f2_pw, f2_pwb, f3_dw, f3_pw, f3_pwb, ln_g, ln_b, cls)

    def _L0_attn_ref(x, gamma, beta, w_qkv, w_out, b_out, sparsity):
        import jax, jax.numpy as jnp
        import numpy as np
        HEADS = 12
        DIM_HEAD = 64
        SCALE = DIM_HEAD ** (-0.5)
        LN_EPS = 1e-05

        def _ternary(w):
            s = jnp.mean(jnp.abs(w))
            return jnp.clip(jnp.round(w / (s + 1e-08)), -1.0, 1.0) * s

        def _sparsify(x, sparsity):
            thr = jnp.quantile(jnp.abs(x), sparsity, axis=-1, keepdims=True)
            return jnp.where(jnp.abs(x) >= thr, x, 0.0)
        b, n, dim = x.shape
        mu = jnp.mean(x, axis=-1, keepdims=True)
        var = jnp.mean((x - mu) ** 2, axis=-1, keepdims=True)
        xn = (x - mu) * jax.lax.rsqrt(var + LN_EPS) * gamma + beta
        qkv = jnp.einsum('bnd,ed->bne', _sparsify(xn, sparsity), _ternary(w_qkv))
        q, k, v = jnp.split(qkv, 3, axis=-1)

        def heads(t):
            return t.reshape(b, n, HEADS, DIM_HEAD).transpose(0, 2, 1, 3)
        q, k, v = (heads(q), heads(k), heads(v))
        dots = jnp.einsum('bhid,bhjd->bhij', q, k) * SCALE
        attn = jax.nn.softmax(dots, axis=-1)
        out = jnp.einsum('bhij,bhjd->bhid', attn, v)
        out = out.transpose(0, 2, 1, 3).reshape(b, n, HEADS * DIM_HEAD)
        out = jnp.einsum('bne,de->bnd', _sparsify(out, sparsity), _ternary(w_out)) + b_out
        return out

    def _L0_ffn_ref(x, router_w, Wg, Wu, Wd):
        import jax, jax.numpy as jnp
        import numpy as np
        B, T, D, E, K = (4, 512, 192, 8, 2)
        H = 4 * D
        Bv, Tv, Dv = x.shape
        N = Bv * Tv
        xf = x.reshape(N, Dv)
        logits = (xf @ router_w.T).astype(jnp.float32)
        top_logits, top_idx = jax.lax.top_k(logits, K)
        top_w = jax.nn.softmax(top_logits, axis=-1).astype(x.dtype)
        out = jnp.zeros_like(xf)
        for e in range(E):
            w_e = jnp.sum(top_w * (top_idx == e), axis=-1)
            h = jax.nn.silu(xf @ Wg[e].T) * (xf @ Wu[e].T)
            out = out + h @ Wd[e].T * w_e[:, None]
        return out.reshape(Bv, Tv, Dv)
    h = _L0_tok_ref(x, L0_tok_pl_w, L0_tok_pl_b, L0_tok_pl_dw, L0_tok_pl_pw, L0_tok_pl_pwb, L0_tok_pg_w1, L0_tok_pg_b1, L0_tok_pg_dw, L0_tok_pg_pw, L0_tok_pg_pwb, L0_tok_pg_w2, L0_tok_pg_b2, L0_tok_alpha, L0_tok_f1_dw, L0_tok_f1_pw, L0_tok_f1_pwb, L0_tok_f2_dw, L0_tok_f2_pw, L0_tok_f2_pwb, L0_tok_f3_dw, L0_tok_f3_pw, L0_tok_f3_pwb, L0_tok_ln_g, L0_tok_ln_b, L0_tok_cls)
    h = jnp.concatenate([jnp.broadcast_to(cls_tok, (h.shape[0], 1, h.shape[2])), h], axis=1)
    h = h + _L0_attn_ref(_layernorm(h, axis=-1), L0_attn_gamma, L0_attn_beta, L0_attn_w_qkv, L0_attn_w_out, L0_attn_b_out, L0_attn_sparsity)
    h = h + _L0_ffn_ref(_layernorm(h, axis=-1), L0_ffn_router_w, L0_ffn_Wg, L0_ffn_Wu, L0_ffn_Wd)
    return h

_drawn_inputs = setup_inputs


def setup_inputs(seed=0):
    import zlib

    import numpy as np

    out = dict(_drawn_inputs(seed))
    spreads = {'L0_tok_alpha': (0.0, 0.8),
     'L0_tok_ln_g': (1.0, 0.2),
     'L0_tok_ln_b': (0.0, 0.1),
     'L0_attn_gamma': (1.0, 0.6),
     'L0_attn_beta': (0.0, 0.506),
     'L0_attn_b_out': (0.0, 0.1)}
    factors = {'x': 8.0,
     'cls_tok': 8.0,
     'L0_tok_pl_w': 8.0,
     'L0_tok_pl_b': 27.292,
     'L0_tok_pl_dw': 8.0,
     'L0_tok_pl_pw': 8.0,
     'L0_tok_pl_pwb': 20.875,
     'L0_tok_pg_w1': 8.0,
     'L0_tok_pg_b1': 104.023,
     'L0_tok_pg_dw': 8.0,
     'L0_tok_pg_pw': 8.0,
     'L0_tok_pg_pwb': 46.677,
     'L0_tok_pg_w2': 8.0,
     'L0_tok_pg_b2': 64.0,
     'L0_tok_f1_dw': 8.0,
     'L0_tok_f1_pw': 8.0,
     'L0_tok_f1_pwb': 47.526,
     'L0_tok_f2_dw': 8.0,
     'L0_tok_f2_pw': 8.0,
     'L0_tok_f2_pwb': 28.284,
     'L0_tok_f3_pw': 2.811,
     'L0_tok_cls': 8.0,
     'L0_ffn_router_w': 8.0,
     'L0_ffn_Wg': 8.0,
     'L0_ffn_Wu': 8.0,
     'L0_ffn_Wd': 8.0}
    for name, (base, spread) in spreads.items():
        noise = np.random.default_rng([zlib.crc32(name.encode()), seed]).standard_normal(out[name].shape)
        drawn = base * np.exp(spread * noise) if base else spread * noise
        out[name] = jnp.asarray(drawn.astype(out[name].dtype))
    for name, factor in factors.items():
        out[name] = (out[name] * factor).astype(out[name].dtype)
    return out
```

```python
from contextlib import ExitStack

import concourse.bass as bass
from concourse import mybir

F32 = mybir.dt.float32
F32R = mybir.dt.float32r
BF16 = mybir.dt.bfloat16
I32 = mybir.dt.int32
U32 = mybir.dt.uint32
ALU = mybir.AluOpType
ACT = mybir.ActivationFunctionType
AX = mybir.AxisListType

B, C, IMG, PATCH = 16, 3, 128, 16
G = IMG // PATCH
S = G * G
D = 192
HD = D // 2
NP_ = B * S
NT = NP_ + 2 * B
BH = B // 2
HALF = NP_ // 2
KC = C * PATCH * PATCH // 128
HEADS, DH = 12, 64
INNER = HEADS * DH
KEYS = S + 2
TT = 9
E, HID = 8, 4 * D
HC = HID // 128
EPS = 1e-5
PASSES = 5
ROWS = [128] * 8 + [NT - NP_]
FREE0, FREE1 = 16512, 229344

PL_B, PL_PWB, PG_B1, PG_PWB, PG_B2, ALPHA, F1_PWB, F2_PWB = range(8)
F3_PWB, LN_G, LN_B, GAMMA, BETA, B_OUT, CLS0, CLS1 = range(8)
DW_PL, DW_PG, DW_F1, DW_F2, DW_F3 = range(5)
PW_PL, PW_PG, PW_G2, PW_F1, PW_F2, PW_F3 = range(6)

BLOCKS = [(0, 3, 384), (3, 3, 384), (6, 3, NT - 768)]


def build_tower(nc, patches, plw, w1t, haar, ident_d, vecs_d, dws_d, pws_d, rows_d, sparsity, wqkv_d, wout_d,
                router_d, iota_d, wgu_d, wd_d, out):
    ctx = ExitStack()
    with ctx:
        o_scr = nc.dram_tensor("o_scratch", (NT, INNER), F32, kind="Internal").ap()

        plan = {}

        def place(zone, name, shape, dt):
            n = 1
            for k in shape[1:]:
                n *= k
            n *= 2 if dt == BF16 else 4
            at = (plan[zone] + 31) // 32 * 32
            plan[zone] = at + n
            assert plan[zone] <= FREE1, (name, plan[zone])
            return nc.alloc_sbuf_tensor_at(name, list(shape), dt, offset=at)

        def sem(name):
            return ctx.enter_context(nc.semaphore(name))

        def due(v):
            return not (isinstance(v, int) and v <= 0)

        plan["kept"] = FREE0
        ident = place("kept", "ident", [128, 128], F32)
        ones = place("kept", "ones", [128, 128], F32)
        rows = place("kept", "rows", [128, 6, D], F32)
        H = place("kept", "H", [128, TT, D], F32)
        vecs = place("kept", "vecs", [HD, 8, 2], F32)
        dws = place("kept", "dws", [HD, 2, 5, 9], F32)
        router = place("kept", "router", [128, 2, E], F32)
        below = place("kept", "below", [128, 2, INNER], F32)
        iota = place("kept", "iota", [128, E], F32)
        gate = place("kept", "gate", [HD, 4, 2], F32)
        bn = place("kept", "bn", [128, TT, 6], F32)
        mv = place("kept", "mv", [128, TT, 2], F32)
        rstd = place("kept", "rstd", [128, 4, TT], F32)
        wsum = place("kept", "wsum", [128, 2, 96], F32)
        wabs = place("kept", "wabs", [128, 2], F32)
        wscale = place("kept", "wscale", [128, 8], F32)
        qrank = place("kept", "qrank", [128, 5], F32)
        thr = place("kept", "thr", [128, TT], I32)
        cand = place("kept", "cand", [128, TT], I32)
        biti = place("kept", "biti", [128, TT], I32)
        bitf = place("kept", "bitf", [128, TT], F32)
        hitb = place("kept", "hitb", [128, TT], I32)
        cnt = place("kept", "cnt", [128, TT], F32)
        asum = place("kept", "asum", [128, TT], F32)
        lev = place("kept", "lev", [128, TT], F32)
        inv = place("kept", "inv", [128, TT], F32)
        err = place("kept", "err", [128, TT], F32)
        work = place("kept", "work", [128, 4, TT], F32)
        far = place("kept", "far", [128, 1], F32)
        far_i = place("kept", "far_i", [128, 1], I32)
        pick = place("kept", "pick", [128, TT, 8], F32)
        junk = place("kept", "junk", [128, 2, INNER], BF16)
        logit = place("kept", "logit", [128, TT, E], F32)
        top8 = place("kept", "top8", [128, TT, 8], F32)
        idx8 = place("kept", "idx8", [128, TT, 8], U32)
        idxf = place("kept", "idxf", [128, TT, 2], F32)
        topw = place("kept", "topw", [128, 4, TT], F32)
        wsel = place("kept", "wsel", [128, 2, TT, E], F32)
        wE = place("kept", "wE", [128, TT, E], F32)
        Tqkv = place("kept", "Tqkv", [HD, 2, 3 * INNER], F32R)
        Tout = place("kept", "Tout", [128, HC, D], F32R)
        W0 = plan["kept"]

        plan["tok"] = W0
        patch = place("tok", "patch", [128, KC, NP_], F32)
        plw_sb = place("tok", "plw_sb", [128, KC, D], F32)
        wf_sb = place("tok", "wf_sb", [128, KC, D], F32)
        w1_sb = place("tok", "w1_sb", [128, 2, C * D], F32)
        haar_sb = place("tok", "haar_sb", [128, 2, 256], F32)
        padA = place("tok", "padA", [HD, 2, 2, G + 2, G + 2, BH], F32)
        padB = place("tok", "padB", [HD, 2, 2, G + 2, G + 2, BH], F32)
        dwA = place("tok", "dwA", [HD, 2, NP_], F32)
        dwB = place("tok", "dwB", [HD, 2, NP_], F32)
        loc = place("tok", "loc", [HD, 2, NP_], F32)
        g2 = place("tok", "g2", [HD, 2, NP_], F32)
        t1 = place("tok", "t1", [HD, 2, NP_], F32)
        pws = place("tok", "pws", [HD, 6, 2, D], F32)
        wq_raw = place("tok", "wq_raw", [HD, 2, 3 * INNER], F32)
        wo_raw = place("tok", "wo_raw", [128, HC, D], F32)
        neg1 = place("tok", "neg1", [128, 3 * INNER], F32)

        plan["att"] = W0
        Z = place("att", "Z", [128, TT, D], F32)
        AB = place("att", "AB", [128, TT, D], F32)
        XH = place("att", "XH", [HD, 2, NT], F32R)
        XL = place("att", "XL", [HD, 2, NT], F32R)
        QKT = place("att", "QKT", [128, 12, NT], F32)
        qk_b = [place("att", f"qk_b{r}", [128, 12, KEYS], F32) for r in range(2)]
        xh_b = [place("att", f"xh_b{r}", [HD, 2, KEYS], F32R) for r in range(2)]
        xl_b = [place("att", f"xl_b{r}", [HD, 2, KEYS], F32R) for r in range(2)]
        v_b = [place("att", f"v_b{r}", [KEYS, HEADS, DH + 1], F32) for r in range(2)]
        s_sb = place("att", "s_sb", [KEYS, HEADS, KEYS], F32)
        p_sb = [place("att", f"p_sb{r}", [KEYS, HEADS, KEYS], F32) for r in range(2)]
        pT_sb = place("att", "pT_sb", [KEYS, HEADS, KEYS], F32)
        o_b = [place("att", f"o_b{r}", [KEYS, HEADS, DH], F32) for r in range(2)]
        mx = place("att", "mx", [KEYS, 2, HEADS], F32)
        O = place("att", "O", [128, TT, INNER], F32)
        plan["out"] = W0
        OA = place("out", "OA", [128, TT, INNER], F32)
        OH = place("out", "OH", [128, HC, NT], F32R)
        OL = place("out", "OL", [128, HC, NT], F32R)
        assert plan["out"] <= plan["att"] - TT * INNER * 4
        plan["moe"] = plan["out"]
        plan["wgt"] = plan["att"]
        raw_a = place("wgt", "raw_a", [128, 2 * HID], F32)
        plan["moe"] = W0
        X6 = place("moe", "X6", [128, TT, 256], F32)
        XFh = place("moe", "XFh", [128, 2, NT], F32R)
        XFl = place("moe", "XFl", [128, 2, NT], F32R)
        raw_b = place("moe", "raw_b", [128, 2 * HID], F32)
        raw_d = place("moe", "raw_d", [128, HC, D], F32)
        Wh = [place("moe", f"Wh{r}", [128, 2 * HID], F32R) for r in range(2)]
        Wl = [place("moe", f"Wl{r}", [128, 2 * HID], F32R) for r in range(2)]
        Wm = [place("moe", f"Wm{r}", [128, 2 * HID], F32R) for r in range(2)]
        Dh_ = [place("moe", f"Dh{r}", [128, HC, D], F32R) for r in range(2)]
        Dl_ = [place("moe", f"Dl{r}", [128, HC, D], F32R) for r in range(2)]
        hH = [place("moe", f"hH{r}", [128, HC, 384], F32R) for r in range(2)]
        hL = [place("moe", f"hL{r}", [128, HC, 384], F32R) for r in range(2)]
        sg = [place("moe", f"sg{r}", [128, 384], F32) for r in range(2)]
        hp = [place("moe", f"hp{r}", [128, 384], F32) for r in range(2)]

        PS = ctx.enter_context(nc.psum_tensor("PS", [128, 8, 512], F32))

        l_fold, l_plw, l_vecs, l_dws, l_pws = (sem(n) for n in ("l_fold", "l_plw", "l_vecs", "l_dws", "l_pws"))
        l_patch = [sem(f"l_patch{k}") for k in range(KC)]
        l_wqkv, l_wout, l_ident, l_rows, l_cls, l_small = (
            sem(n) for n in ("l_wqkv", "l_wout", "l_ident", "l_rows", "l_cls", "l_small"))
        l_o = [sem(f"l_o{t}") for t in range(TT)]
        l_exp = sem("l_exp")
        pads_zero, h8_zero = sem("pads_zero"), sem("h8_zero")
        fold_done, fold_copied = sem("fold_done"), sem("fold_copied")
        tanh_done, gate_done = sem("tanh_done"), sem("gate_done")
        job_done, job_copied = sem("job_done"), sem("job_copied")
        tap_done, mix_done = sem("tap_done"), sem("mix_done")
        wsum_ready, wmean_ready, wmean_read = sem("wsum_ready"), sem("wmean_ready"), sem("wmean_read")
        dve_done = sem("dve_done")
        var_ready, std_ready = sem("var_ready"), sem("std_ready")
        abs_in, abs_done = sem("abs_in"), sem("abs_done")
        asum_set, far_ready, far_summed, below_done = (sem(n) for n in ("asum_set", "far_ready", "far_summed", "below_done"))
        count_done = [[sem(f"count_done{w}{p}") for p in range(PASSES)] for w in range(2)]
        bit_step = [sem("bit_step0"), sem("bit_step1")]
        masked1, xT_done, xh_done, xl_done = (sem(n) for n in ("masked1", "xT_done", "xh_done", "xl_done"))
        qk_done, qk_copied_a, qk_copied_d = sem("qk_done"), sem("qk_copied_a"), sem("qk_copied_d")
        qkb_ready, xb_ready = sem("qkb_ready"), sem("xb_ready")
        scores_done, v_done, pT_done, pv_done = (sem(n) for n in ("scores_done", "v_done", "pT_done", "pv_done"))
        max_done, shifted, exp_done = sem("max_done"), sem("shifted"), sem("exp_done")
        pT_copied, v_copied, recip_done, o_ready = (sem(n) for n in ("pT_copied", "v_copied", "recip_done", "o_ready"))
        o_stored = [sem("o_stored0"), sem("o_stored1")]
        masked2, oT_done, oh_done, ol_done = (sem(n) for n in ("masked2", "oT_done", "oh_done", "ol_done"))
        proj_done, proj_added = sem("proj_done"), sem("proj_added")
        x6_ready, xfT_done, xfh_done, xfl_done = (sem(n) for n in ("x6_ready", "xfT_done", "xfh_done", "xfl_done"))
        logits_done, diff_ready, exp2_done = sem("logits_done"), sem("diff_ready"), sem("exp2_done")
        w_hi, w_lo = sem("w_hi"), sem("w_lo")
        gu_done, silu_done, hp_done, hh_done, hl_done = (
            sem(n) for n in ("gu_done", "silu_done", "hp_done", "hh_done", "hl_done"))
        down_done, down_added = sem("down_done"), sem("down_added")
        stored = sem("stored")

        block = ctx.enter_context(nc.Block())

        JOBS = [("loc", 0), ("loc", 1), ("g", 0), ("g", 1), (PW_PL, 0), (PW_PL, 1), (PW_PG, 0), (PW_PG, 1),
                (PW_G2, 0), (PW_G2, 1), (PW_F1, 0), (PW_F1, 1), (PW_F2, 0), (PW_F2, 1), (PW_F3, 0), (PW_F3, 1)]
        DWS = [(DW_PL, 0), (DW_PL, 1), (DW_PG, 0), (DW_PG, 1), (DW_F1, 0), (DW_F1, 1), (DW_F2, 0), (DW_F2, 1),
               (DW_F3, 0), (DW_F3, 1)]
        dw_pad = {DW_PL: padA, DW_PG: padB, DW_F1: padA, DW_F2: padB, DW_F3: padA}
        dw_out = {DW_PL: dwA, DW_PG: dwB, DW_F1: dwA, DW_F2: dwB, DW_F3: dwA}
        pw_of = {PW_PL: DW_PL, PW_PG: DW_PG, PW_F1: DW_F1, PW_F2: DW_F2, PW_F3: DW_F3}

        def window(pad, m, h, dy, dx):
            return pad[:, m, h, dy:dy + G, dx:dx + G, :].rearrange("p y x b -> p y (x b)")

        def inside(pad, m, h):
            return window(pad, m, h, 1, 1)

        def cols(t, m, h):
            return t[:, m, h * HALF:(h + 1) * HALF].rearrange("p (y n) -> p y n", y=G)

        def slot(h):
            return h % 2 * (HEADS // 2) + h // 2

        def patch_rows(b):
            return bass.DynSlice(b + (b // BH) * (HALF - BH), S, step=BH)

        def batch_cols(t, b):
            return t[:, :, patch_rows(b)], t[:, :, NP_:NT].rearrange("p c (k b) -> p c k b", k=2)[:, :, :, bass.ts(b, 1)]

        def moe_columns(n):
            t0, nt, w = BLOCKS[n]
            return slice(t0 * 128, t0 * 128 + w)

        @block.sync
        def _(sp):
            sp.dma_start(haar_sb[:], haar).then_inc(l_fold, 16)
            sp.dma_start(w1_sb[:], w1t).then_inc(l_fold, 16)
            sp.dma_start(plw_sb[:], plw).then_inc(l_plw, 16)
            for k in range(KC):
                sp.dma_start(patch[:, k, :], patches[:, k, :]).then_inc(l_patch[k], 16)

            def store_o(b, r):
                sp.wait_ge(o_ready, b + 1)
                sp.dma_start(o_scr[patch_rows(b), :], o_b[r][0:S].rearrange("p h d -> p (h d)")).then_inc(o_stored[r], 16)
                sp.dma_start(o_scr[NP_:NT, :].rearrange("(k b) n -> k b n", k=2)[:, bass.ts(b, 1), :],
                             o_b[r][S:KEYS].rearrange("p h d -> p (h d)").unsqueeze(1)).then_inc(o_stored[r], 16)

            with sp.Fori(0, B // 2) as j:
                store_o(2 * j, 0)
                store_o(2 * j + 1, 1)
            sp.wait_ge(o_stored[0], 16 * B)
            sp.wait_ge(o_stored[1], 16 * B)
            for t in range(TT):
                sp.dma_start(O[0:ROWS[t], t, :], o_scr[t * 128:t * 128 + ROWS[t], :]).then_inc(l_o[t], 16)

            sp.wait_ge(xfl_done, TT)
            def load_expert(e):
                if due(3 * e):
                    sp.wait_ge(w_lo, 3 * e)
                sp.dma_start(raw_a[:], wgu_d[bass.ts(e, 1), 0:128, :].rearrange("e p n -> (e p) n")).then_inc(l_exp, 16)
                for half in range(2):
                    sp.dma_start(raw_b[64 * half:64 * half + 64, :],
                                 wgu_d[bass.ts(e, 1), 128:D, :].rearrange("e p n -> (e p) n")).then_inc(l_exp, 16)
                sp.dma_start(raw_d[:], wd_d[bass.ts(e, 1)].rearrange("e p c n -> (e p) c n")).then_inc(l_exp, 16)

            load_expert(0)
            with sp.Fori(1, E) as e:
                load_expert(e)
            sp.wait_ge(down_added, E * TT)
            for b in range(B):
                h, i = b // BH, b % BH
                sp.dma_start(out[b, 2:KEYS, :].rearrange("(t s) d -> s t d", t=4), H[i::BH, 4 * h:4 * h + 4, :])\
                    .then_inc(stored, 16)
            for k in range(2):
                sp.dma_start(out[:, k, :], H[16 * k:16 * k + 16, 8, :]).then_inc(stored, 16)
            sp.wait_ge(stored, 18 * 16)

        @block.gpsimd
        def _(pool):
            pool.dma_start(ident[:], ident_d).then_inc(l_ident, 16)
            pool.memset(padA[:], 0.0).then_inc(pads_zero, 1)
            pool.memset(padB[:], 0.0).then_inc(pads_zero, 1)
            pool.memset(H[:, 8, :], 0.0).then_inc(h8_zero, 1)
            pool.dma_start(rows[:], rows_d[0:6, :].partition_broadcast(128)).then_inc(l_rows, 16)
            pool.dma_start(qrank[:, 0:1], sparsity.partition_broadcast(128)).then_inc(l_small, 16)
            pool.dma_start(iota[:], iota_d).then_inc(l_small, 16)
            pool.dma_start(router[:, 0, :], router_d[0:128, :]).then_inc(l_small, 16)
            pool.dma_start(router[0:64, 1, :], router_d[128:D, :]).then_inc(l_small, 16)
            pool.wait_ge(h8_zero, 1)
            for k in range(2):
                pool.dma_start(H[16 * k:16 * k + 16, 8, :], rows_d[CLS0 + k, :].partition_broadcast(16)).then_inc(l_cls, 16)

            def x_copies(b, r):
                if due(b - 1):
                    pool.wait_ge(v_done, b - 1)
                for src, dst in ((XH, xh_b[r]), (XL, xl_b[r])):
                    a, c = batch_cols(src.bitcast(F32), b)
                    pool.tensor_copy(dst[:, :, 0:S], a)
                    last = pool.tensor_copy(dst[:, :, S:KEYS].unsqueeze(3), c)
                last.then_inc(xb_ready, 1)

            pool.wait_ge(xh_done, 6)
            pool.wait_ge(xl_done, 6)
            x_copies(0, 0)
            x_copies(1, 1)
            with pool.Fori(1, B // 2) as j:
                x_copies(2 * j, 0)
                x_copies(2 * j + 1, 1)

            def rests(e, r):
                pool.wait_ge(w_hi, 3 * (e + 1))
                if not (isinstance(e, int) and e < 2):
                    if due(TT * (e - 1)):
                        pool.wait_ge(down_done, TT * (e - 1))
                pool.tensor_tensor(Wl[r][:], raw_a[:], Wh[r].bitcast(F32)[:], ALU.subtract).then_inc(w_lo, 1)
                pool.wait_ge(w_lo, 3 * e + 1)
                pool.tensor_tensor(Wm[r][64:128, :], raw_b[64:128, :], Wm[r].bitcast(F32)[64:128, :],
                                   ALU.subtract).then_inc(w_lo, 1)
                pool.wait_ge(w_lo, 3 * e + 2)
                pool.tensor_tensor(Dl_[r][:], raw_d[:], Dh_[r].bitcast(F32)[:], ALU.subtract).then_inc(w_lo, 1)

            rests(0, 0)
            rests(1, 1)
            with pool.Fori(1, E // 2) as j:
                rests(2 * j, 0)
                rests(2 * j + 1, 1)

        @block.scalar
        def _(act):
            act.dma_start(vecs[:], vecs_d).then_inc(l_vecs, 16)
            act.dma_start(dws[:], dws_d).then_inc(l_dws, 16)
            act.dma_start(wq_raw[:], wqkv_d).then_inc(l_wqkv, 16)
            act.dma_start(wo_raw[:], wout_d).then_inc(l_wout, 16)
            act.dma_start(pws[:], pws_d).then_inc(l_pws, 16)
            act.wait_ge(l_vecs, 16)
            act.activation(gate[:, 0, :], vecs[:, ALPHA, :], ACT.Tanh).then_inc(tanh_done, 1)
            act.wait_ge(fold_done, 1)
            for pc in range(2):
                act.activation(wf_sb[:, pc:pc + 3:2, :],
                               PS[:, 4 + 2 * pc, 0:2 * D].rearrange("p (c d) -> p c d", c=2), ACT.Copy).then_inc(fold_copied, 1)
                act.activation(wf_sb[:, 4 + pc, :], PS[:, 5 + 2 * pc, 0:D], ACT.Copy).then_inc(fold_copied, 1)
            act.wait_ge(pads_zero, 2)
            for j, (kind, h) in enumerate(JOBS[:14]):
                act.wait_ge(job_done, j + 1)
                if kind == PW_G2:
                    act.wait_ge(gate_done, 3)
                for m in range(2):
                    ps = PS[0:HD, 2 * (j % 4) + m, :]
                    psv = ps.rearrange("p (y n) -> p y n", y=G)
                    c = slice(h * HALF, (h + 1) * HALF)
                    bias = {"loc": PL_B, "g": PG_B1, PW_PL: PL_PWB, PW_PG: PG_PWB, PW_F1: F1_PWB, PW_F2: F2_PWB}.get(kind)
                    bias = gate[:, 3, m:m + 1] if bias is None else vecs[:, bias, m:m + 1]
                    if kind == "loc":
                        ins = act.activation(inside(padA, m, h), psv, ACT.Gelu, bias=bias)
                    elif kind == "g":
                        ins = act.activation(inside(padB, m, h), psv, ACT.Gelu, bias=bias)
                    elif kind == PW_PL:
                        ins = act.activation(loc[:, m, c], ps, ACT.Identity, bias=bias)
                    elif kind == PW_PG:
                        ins = act.activation(g2[:, m, c], ps, ACT.Gelu, bias=bias)
                    elif kind == PW_G2:
                        ins = act.activation(t1[:, m, c], ps, ACT.Identity, bias=bias, scale=gate[:, 1, m:m + 1])
                    elif kind == PW_F1:
                        ins = act.activation(inside(padB, m, h), psv, ACT.Relu, bias=bias)
                    else:
                        ins = act.activation(t1[:, m, c], ps, ACT.Relu, bias=bias)
                ins.then_inc(job_copied, 1)

            def sqrt(n):
                if due(n):
                    act.wait_ge(var_ready, n)
                act.activation(rstd[:, 1, :], rstd[:, 0, :], ACT.Sqrt).then_inc(std_ready, 1)

            for n in range(3):
                sqrt(n + 1)
            act.wait_ge(abs_in, 1)
            act.wait_ge(asum_set, 1)
            for t in range(TT):
                act.activation(AB[0:ROWS[t], t, :], Z[0:ROWS[t], t, :], ACT.Abs,
                               accum_out=asum[0:ROWS[t], t:t + 1]).then_inc(abs_done, 1)
            for n in range(6):
                g, c = n // 2, n % 2
                w = 512 if g < 2 else 32
                act.wait_ge(xT_done, n + 1)
                act.activation(XH[:, c, 512 * g:512 * g + w], PS[0:HD, 3 * c + g, 0:w], ACT.Copy).then_inc(xh_done, 1)
            for q in range(0, 36, 2):
                act.wait_ge(qk_done, q + 1)
                act.activation(QKT[:, q // 3, 352 * (q % 3):352 * (q % 3) + 352], PS[:, (6 + q) % 8, 0:352],
                               ACT.Copy).then_inc(qk_copied_a, 1)

            def copy_pT(b):
                act.wait_ge(pT_done, b + 1)
                if due(b):
                    act.wait_ge(pv_done, b)
                act.activation(pT_sb[:].rearrange("p (k h) n -> p k h n", k=2),
                               PS[0:KEYS, 4:6, 0:6 * KEYS].rearrange("p k (h n) -> p k h n", h=6),
                               ACT.Copy).then_inc(pT_copied, 1)

            def copy_v(b, r):
                act.wait_ge(v_done, b + 1)
                if due(b - 1):
                    act.wait_ge(pv_done, b - 1)
                act.activation(v_b[r][:, :, 0:DH].rearrange("p (k h) d -> p k h d", k=2),
                               PS[0:KEYS, 2:4, 0:384].rearrange("p k (h d) -> p k h d", h=6),
                               ACT.Copy).then_inc(v_copied, 1)

            def exp(b, r):
                act.wait_ge(shifted, b + 1)
                if due(b - 1):
                    act.wait_ge(pT_done, b - 1)
                act.activation(p_sb[r][:], s_sb[:], ACT.Exp, scale=wscale[0:KEYS, 4:5]).then_inc(exp_done, 1)

            copy_v(0, 0)
            exp(0, 0)
            copy_pT(0)
            copy_v(1, 1)
            exp(1, 1)
            with act.Fori(1, B // 2) as j:
                for k in range(2):
                    copy_pT(2 * j + (k - 1))
                    copy_v(2 * j + k, k)
                    exp(2 * j + k, k)
            copy_pT(B - 1)

            for t in range(TT):
                act.wait_ge(l_o[t], 16)
                act.activation(OA[0:ROWS[t], t, :], O[0:ROWS[t], t, :], ACT.Abs,
                               accum_out=asum[0:ROWS[t], t:t + 1]).then_inc(abs_done, 1)
            for t in range(TT):
                act.wait_ge(oT_done, t + 1)
                act.activation(OH[:, :, t * 128:t * 128 + ROWS[t]].rearrange("p (k c) n -> p k c n", k=2),
                               PS[:, 2 * (t % 3):2 * (t % 3) + 2, 0:384].rearrange("p k (c n) -> p k c n", c=3)[:, :, :, 0:ROWS[t]],
                               ACT.Copy).then_inc(oh_done, 1)
            sqrt(4)
            for t in range(TT):
                act.wait_ge(xfT_done, t + 1)
                act.activation(XFh[:, :, t * 128:t * 128 + ROWS[t]],
                               PS[:, t % 4, 0:256].rearrange("p (c n) -> p c n", c=2)[:, :, 0:ROWS[t]],
                               ACT.Copy).then_inc(xfh_done, 1)
            act.wait_ge(diff_ready, 1)
            act.activation(topw[:, 1, :], topw[:, 0, :], ACT.Exp).then_inc(exp2_done, 1)

            def highs(e, r):
                act.wait_ge(l_exp, 64 * (e + 1))
                if not (isinstance(e, int) and e < 2):
                    if due(TT * (e - 1)):
                        act.wait_ge(down_done, TT * (e - 1))
                act.activation(Wh[r][:], raw_a[:], ACT.Copy).then_inc(w_hi, 1)
                act.activation(Wm[r][:], raw_b[:], ACT.Copy).then_inc(w_hi, 1)
                act.activation(Dh_[r][:], raw_d[:], ACT.Copy).then_inc(w_hi, 1)

            def act_block(e2, k):
                n, w = k % 3, BLOCKS[k % 3][2]
                for m in range(HC + 1):
                    if m < HC:
                        i = 6 * k + m
                        act.wait_ge(gu_done, 36 * e2 + i + 1)
                        if due(36 * e2 + i - 1):
                            act.wait_ge(hp_done, 36 * e2 + i - 1)
                        act.activation(sg[m % 2][:, 0:w], PS[:, 2 * (i % 3), 0:w], ACT.Silu).then_inc(silu_done, 1)
                    if m > 0:
                        i = 6 * k + m - 1
                        act.wait_ge(hp_done, 36 * e2 + i + 1)
                        if k >= 2 or not isinstance(e2, int):
                            if due(18 * e2 + 3 * (k - 1)):
                                act.wait_ge(down_done, 18 * e2 + 3 * (k - 1))
                        act.activation(hH[k % 2][:, m - 1, 0:w], hp[(m - 1) % 2][:, 0:w], ACT.Copy).then_inc(hh_done, 1)

            highs(0, 0)
            for k in range(6):
                act_block(0, k)
                if k == 0:
                    highs(1, 1)
                if k == 4:
                    highs(2, 0)
            with act.Fori(1, E // 2 - 1) as e2:
                for k in range(6):
                    act_block(e2, k)
                    if k == 0:
                        highs(2 * e2 + 1, 1)
                    if k == 4:
                        highs(2 * e2 + 2, 0)
            for k in range(6):
                act_block(E // 2 - 1, k)
                if k == 0:
                    highs(E - 1, 1)

        @block.tensor
        def _(pe):
            pe.wait_ge(l_fold, 32)
            for pc in range(2):
                for bank, c0, n in ((4 + 2 * pc, 0, 2 * D), (5 + 2 * pc, 2 * D, D)):
                    for k in range(2):
                        mm = pe.matmul(PS[:, bank, 0:n], haar_sb[:, k, 128 * pc:128 * pc + 128],
                                       w1_sb[:, k, c0:c0 + n], start=(k == 0), stop=(k == 1))
            mm.then_inc(fold_done, 1)
            pe.wait_ge(l_plw, 16)
            for j, (kind, h) in enumerate(JOBS):
                b0 = 2 * (j % 4)
                c = slice(h * HALF, (h + 1) * HALF)
                if kind == "g":
                    pe.wait_ge(fold_copied, 4)
                if j == 3:
                    pe.wait_ge(wmean_read, 2)
                if j >= 4:
                    if due(j - 3):
                        pe.wait_ge(job_copied, j - 3)
                    pe.wait_ge(l_pws, 16)
                if kind in pw_of:
                    pe.wait_ge(tap_done, 18 * (DWS.index((pw_of[kind], h)) + 1))
                if kind == PW_G2:
                    pe.wait_ge(job_copied, 7 + h)
                if kind == PW_F3:
                    src = dw_out[DW_F3]
                    for i in range(4):
                        t = 4 * h + i
                        for k in range(2):
                            mm = pe.matmul(PS[:, b0 + i // 2, (i % 2) * D:(i % 2) * D + D],
                                           src[:, k, t * 128:t * 128 + 128], pws[:, PW_F3, k, :],
                                           start=(k == 0), stop=(k == 1))
                elif kind in ("loc", "g"):
                    w = plw_sb if kind == "loc" else wf_sb
                    for k in range(KC):
                        if j == 0:
                            pe.wait_ge(l_patch[k], 16)
                        for m in range(2):
                            mm = pe.matmul(PS[0:HD, b0 + m, :], w[:, k, m * HD:m * HD + HD], patch[:, k, c],
                                           start=(k == 0), stop=(k == KC - 1))
                else:
                    src = g2 if kind == PW_G2 else dw_out[pw_of[kind]]
                    for m in range(2):
                        for k in range(2):
                            mm = pe.matmul(PS[0:HD, b0 + m, :], pws[:, kind, k, m * HD:m * HD + HD], src[:, k, c],
                                           start=(k == 0), stop=(k == 1))
                mm.then_inc(job_done, 1)
                if j == 0:
                    pe.wait_ge(wsum_ready, 2)
                    pe.wait_ge(fold_copied, 4)
                    pe.matmul(PS[:, 7, 0:1], ones[0:HD, :], wabs[0:HD, 0:1], start=True, stop=True)
                    pe.matmul(PS[:, 7, 1:2], ones[:, :], wabs[:, 1:2], start=True, stop=True).then_inc(wmean_ready, 1)
            def sum_far(which):
                pe.wait_ge(far_ready, which + 1)
                pe.matmul(PS[:, 0, 0:1], ones[:], far[:], start=True, stop=True).then_inc(far_summed, 1)

            sum_far(0)
            pe.wait_ge(l_ident, 16)
            for g in range(3):
                for c in range(2):
                    for t in range(4 * g, min(4 * g + 4, TT)):
                        pe.wait_ge(masked1, t + 1)
                        tr = pe.transpose(PS[0:HD, 3 * c + g, (t % 4) * 128:(t % 4) * 128 + ROWS[t]],
                                          Z[0:ROWS[t], t, c * HD:c * HD + HD], ident[0:ROWS[t], 0:ROWS[t]])
                    tr.then_inc(xT_done, 1)
            pe.wait_ge(xh_done, 6)
            pe.wait_ge(xl_done, 6)
            for q in range(36):
                m, n = q // 3, q % 3
                if due((q - 8) // 2 + 1):
                    pe.wait_ge(qk_copied_a if q % 2 == 0 else qk_copied_d, (q - 8) // 2 + 1)
                for c in range(2):
                    for x in (XH, XL):
                        mm = pe.matmul(PS[:, (6 + q) % 8, 0:352], Tqkv[:, c, 128 * m:128 * m + 128],
                                       x[:, c, 352 * n:352 * n + 352], start=(c == 0 and x is XH), stop=(c == 1 and x is XL))
                mm.then_inc(qk_done, 1)

            def scores(b, r):
                pe.wait_ge(qkb_ready, b + 1)
                if due(b):
                    pe.wait_ge(shifted, b)
                for h in range(HEADS):
                    p = 64 * (h % 2)
                    mm = pe.matmul(PS[0:KEYS, h % 2, (h // 2) * KEYS:(h // 2 + 1) * KEYS],
                                   qk_b[r][p:p + 64, h // 2, :], qk_b[r][p:p + 64, 6 + h // 2, :],
                                   start=True, stop=True)
                mm.then_inc(scores_done, 1)

            def values(b, r):
                pe.wait_ge(xb_ready, b + 1)
                if due(b):
                    pe.wait_ge(v_copied, b)
                for k in range(2):
                    for c in range(2):
                        for x in (xh_b, xl_b):
                            mm = pe.matmul(PS[0:KEYS, 2 + k, 0:384], x[r][:, c, :],
                                           Tqkv[:, c, 2 * INNER + 384 * k:2 * INNER + 384 * k + 384],
                                           start=(c == 0 and x is xh_b), stop=(c == 1 and x is xl_b))
                mm.then_inc(v_done, 1)

            def transposed(b, r):
                pe.wait_ge(exp_done, b + 1)
                if due(b):
                    pe.wait_ge(pT_copied, b)
                for h in range(HEADS):
                    tr = pe.transpose(PS[0:KEYS, 4 + h // 6, (h % 6) * KEYS:(h % 6 + 1) * KEYS], p_sb[r][:, h, :],
                                      ident[0:KEYS, 0:KEYS])
                tr.then_inc(pT_done, 1)

            def weighted(b, r):
                pe.wait_ge(pT_copied, b + 1)
                pe.wait_ge(v_copied, b + 1)
                if due(b):
                    pe.wait_ge(o_ready, b)
                for h in range(HEADS):
                    mm = pe.matmul(PS[0:KEYS, 6 + h // 6, (h % 6) * (DH + 1):(h % 6 + 1) * (DH + 1)], pT_sb[:, slot(h), :],
                                   v_b[r][:, h, :], start=True, stop=True)
                mm.then_inc(pv_done, 1)

            pe.wait_ge(qk_copied_a, 18)
            pe.wait_ge(qk_copied_d, 18)
            scores(0, 0)
            values(0, 0)
            scores(1, 1)
            transposed(0, 0)
            values(1, 1)
            weighted(0, 0)
            with pe.Fori(1, B // 2) as j:
                for k in range(2):
                    scores(2 * j + k, k)
                    transposed(2 * j + (k - 1), 1 - k)
                    values(2 * j + k, k)
                    weighted(2 * j + (k - 1), 1 - k)
            transposed(B - 1, 1)
            weighted(B - 1, 1)
            pe.wait_ge(o_ready, B)

            def turn_o(t):
                pe.wait_ge(masked2, t + 1)
                if due(t - 2):
                    pe.wait_ge(ol_done, t - 2)
                for c in range(HC):
                    tr = pe.transpose(PS[:, 2 * (t % 3) + c // 3, (c % 3) * 128:(c % 3) * 128 + ROWS[t]],
                                      O[0:ROWS[t], t, 128 * c:128 * c + 128], ident[0:ROWS[t], 0:ROWS[t]])
                tr.then_inc(oT_done, 1)

            def project(t):
                pe.wait_ge(oh_done, t + 1)
                pe.wait_ge(ol_done, t + 1)
                if due(t - 1):
                    pe.wait_ge(proj_added, t - 1)
                for c in range(HC):
                    for x in (OH, OL):
                        mm = pe.matmul(PS[0:ROWS[t], 6 + t % 2, 0:D], x[:, c, t * 128:t * 128 + ROWS[t]], Tout[:, c, :],
                                       start=(c == 0 and x is OH), stop=(c == HC - 1 and x is OL))
                mm.then_inc(proj_done, 1)

            sum_far(1)
            turn_o(0)
            turn_o(1)
            for t in range(TT):
                if t + 2 < TT:
                    turn_o(t + 2)
                project(t)
            pe.wait_ge(x6_ready, 1)
            for t in range(TT):
                if due(t - 3):
                    pe.wait_ge(xfl_done, t - 3)
                for c in range(2):
                    tr = pe.transpose(PS[:, t % 4, 128 * c:128 * c + ROWS[t]], X6[0:ROWS[t], t, 128 * c:128 * c + 128],
                                      ident[0:ROWS[t], 0:ROWS[t]])
                tr.then_inc(xfT_done, 1)
            pe.wait_ge(xfl_done, TT)
            pe.wait_ge(xfh_done, TT)
            pe.wait_ge(l_small, 64)
            for t in range(TT):
                for c, p in ((0, 128), (1, 64)):
                    for x in (XFh, XFl):
                        mm = pe.matmul(PS[0:ROWS[t], 4, E * t:E * t + E],
                                       x.bitcast(F32)[0:p, c, t * 128:t * 128 + ROWS[t]], router[0:p, c, :],
                                       start=(c == 0 and x is XFh), stop=(c == 1 and x is XFl))
            mm.then_inc(logits_done, 1)

            def gate_up(e2, k):
                r, n = k // 3, k % 3
                cs, w = moe_columns(n), BLOCKS[n][2]
                if n == 0:
                    pe.wait_ge(w_hi, 6 * e2 + 3 * r + 3)
                    pe.wait_ge(w_lo, 6 * e2 + 3 * r + 3)
                for m in range(HC):
                    i = 6 * k + m
                    if not (isinstance(e2, int) and e2 == 0 and i < 3):
                        if due(36 * e2 + i - 2):
                            pe.wait_ge(hp_done, 36 * e2 + i - 2)
                    for side in range(2):
                        c0 = side * HID + 128 * m
                        ps = PS[:, 2 * (i % 3) + side, 0:w]
                        pe.matmul(ps, Wh[r][:, c0:c0 + 128], XFh[:, 0, cs], start=True, stop=False)
                        pe.matmul(ps, Wh[r][:, c0:c0 + 128], XFl[:, 0, cs], start=False, stop=False)
                        pe.matmul(ps, Wl[r][:, c0:c0 + 128], XFh[:, 0, cs], start=False, stop=False)
                        pe.matmul(ps, Wm[r][:, c0:c0 + 128], XFh[:, 1, cs], start=False, stop=False)
                        mm = pe.matmul(ps, Wm[r][0:64, c0:c0 + 128], XFl[0:64, 1, cs], start=False, stop=True)
                    mm.then_inc(gu_done, 1)

            def down(e2, k):
                r, n = k // 3, k % 3
                t0 = BLOCKS[n][0]
                pe.wait_ge(hh_done, 36 * e2 + 6 * k + 6)
                pe.wait_ge(hl_done, 36 * e2 + 6 * k + 6)
                for i in range(3):
                    t = t0 + i
                    d = 3 * k + i
                    if not (isinstance(e2, int) and e2 == 0 and d < 2):
                        if due(18 * e2 + d - 1):
                            pe.wait_ge(down_added, 18 * e2 + d - 1)
                    cs = slice(128 * i, 128 * i + ROWS[t])
                    ps = PS[0:ROWS[t], 6 + d % 2, 0:D]
                    for m in range(HC):
                        pe.matmul(ps, hH[k % 2][:, m, cs], Dh_[r][:, m, :], start=(m == 0), stop=False)
                        pe.matmul(ps, hH[k % 2][:, m, cs], Dl_[r][:, m, :], start=False, stop=False)
                        mm = pe.matmul(ps, hL[k % 2][:, m, cs], Dh_[r][:, m, :], start=False, stop=(m == HC - 1))
                    mm.then_inc(down_done, 1)

            def pe_pair(e2):
                gate_up(e2, 0)
                for k in range(1, 6):
                    gate_up(e2, k)
                    down(e2, k - 1)
                down(e2, 5)

            pe_pair(0)
            with pe.Fori(1, E // 2) as e2:
                pe_pair(e2)

        @block.vector
        def _(dve):
            count = [0]

            def link(ins):
                count[0] += 1
                ins.then_inc(dve_done, 1)
                dve.wait_ge(dve_done, count[0])

            link(dve.memset(ones[:], 1.0))
            dve.memset(asum[:], 1.0).then_inc(asum_set, 1)
            link(dve.memset(wabs[:], 0.0))
            dve.wait_ge(l_wqkv, 16)
            link(dve.tensor_reduce(wsum[0:HD, 0, :], wq_raw[:].rearrange("p c (a n) -> p (c a) n", n=48), AX.X, ALU.add,
                                   apply_absolute_value=True))
            dve.tensor_reduce(wabs[0:HD, 0:1], wsum[0:HD, 0, :], AX.X, ALU.add).then_inc(wsum_ready, 1)
            dve.wait_ge(l_wout, 16)
            link(dve.tensor_reduce(wsum[:, 1, 0:24], wo_raw[:].rearrange("p c (a n) -> p (c a) n", n=48), AX.X, ALU.add,
                                   apply_absolute_value=True))
            dve.tensor_reduce(wabs[:, 1:2], wsum[:, 1, 0:24], AX.X, ALU.add).then_inc(wsum_ready, 1)
            dve.wait_ge(tanh_done, 1)
            dve.tensor_scalar(gate[:, 1, :], gate[:, 0, :], 1.0, 0.5, ALU.add, ALU.mult).then_inc(gate_done, 1)
            dve.wait_ge(gate_done, 1)
            dve.tensor_scalar(gate[:, 2, :], gate[:, 1, :], -1.0, 1.0, ALU.mult, ALU.add).then_inc(gate_done, 1)
            dve.tensor_tensor(gate[:, 3, :], gate[:, 1, :], vecs[:, PG_B2, :], ALU.mult).then_inc(gate_done, 1)

            dve.wait_ge(wmean_ready, 1)
            dve.tensor_scalar(wscale[:, 0:1], PS[:, 7, 0:1], 1.0 / (3 * INNER * D), None, ALU.mult).then_inc(wmean_read, 1)
            dve.tensor_scalar(wscale[:, 1:2], PS[:, 7, 1:2], 1.0 / (INNER * D), None, ALU.mult).then_inc(wmean_read, 1)
            dve.wait_ge(wmean_read, 2)
            link(dve.tensor_scalar(wscale[:, 2:4], wscale[:, 0:2], 1e-8, 0.5, ALU.add, ALU.mult))
            link(dve.scalar_tensor_tensor(wscale[:, 4:5], wscale[:, 0:1], wscale[:, 0:1], wscale[:, 0:1],
                                          ALU.mult, ALU.bypass))
            link(dve.tensor_scalar(wscale[:, 4:5], wscale[:, 4:5], float(DH) ** -0.5, None, ALU.mult))
            link(dve.tensor_tensor(wscale[:, 5:6], wscale[:, 0:1], wscale[:, 1:2], ALU.mult))
            link(dve.tensor_scalar(wscale[:, 6:8], wscale[:, 2:4], -1.0, None, ALU.mult))
            for c in range(2):
                link(dve.tensor_scalar(neg1[0:HD, :], wq_raw[:, c, :], wscale[0:HD, 6:7], None, ALU.is_lt))
                link(dve.scalar_tensor_tensor(Tqkv[:, c, :], wq_raw[:, c, :], wscale[0:HD, 2:3], neg1[0:HD, :],
                                              ALU.is_gt, ALU.subtract))
            flat = wo_raw[:].rearrange("p c n -> p (c n)")
            link(dve.tensor_scalar(neg1[:, 0:HC * D], flat, wscale[:, 7:8], None, ALU.is_lt))
            link(dve.scalar_tensor_tensor(Tout[:].rearrange("p c n -> p (c n)"), flat, wscale[:, 3:4],
                                          neg1[:, 0:HC * D], ALU.is_gt, ALU.subtract))
            dve.wait_ge(l_dws, 16)

            def depthwise(n):
                f, h = DWS[n]
                pad, dst = dw_pad[f], dw_out[f]
                for tap in range(9):
                    dy, dx = tap // 3, tap % 3
                    for m in range(2):
                        if due(18 * n + 2 * tap + m - 1):
                            dve.wait_ge(tap_done, 18 * n + 2 * tap + m - 1)
                        src = window(pad, m, h, dy, dx)
                        w = dws[:, m, f, tap:tap + 1]
                        if tap == 0:
                            ins = dve.tensor_scalar(cols(dst, m, h), src, w, None, ALU.mult)
                        else:
                            ins = dve.scalar_tensor_tensor(cols(dst, m, h), src, w, cols(dst, m, h), ALU.mult, ALU.add)
                        ins.then_inc(tap_done, 1)

            for n in range(4):
                dve.wait_ge(job_copied, n + 1)
                depthwise(n)
            for h in range(2):
                dve.wait_ge(job_copied, 9 + h)
                for m in range(2):
                    c = slice(h * HALF, (h + 1) * HALF)
                    dve.scalar_tensor_tensor(inside(padA, m, h), cols(loc, m, h), gate[:, 2, m:m + 1], cols(t1, m, h),
                                             ALU.mult, ALU.add).then_inc(mix_done, 1)
                dve.wait_ge(mix_done, 2 * h + 2)
                dve.wait_ge(job_done, 5 + h)
                depthwise(4 + h)
            for h in range(2):
                dve.wait_ge(job_copied, 11 + h)
                dve.wait_ge(job_done, 7 + h)
                depthwise(6 + h)
            for h in range(2):
                dve.wait_ge(job_copied, 13 + h)
                for m in range(2):
                    dve.tensor_tensor(inside(padA, m, h), cols(loc, m, h), cols(t1, m, h), ALU.add).then_inc(mix_done, 1)
                dve.wait_ge(mix_done, 6 + 2 * h)
                dve.wait_ge(job_done, 11 + h)
                depthwise(8 + h)
            dve.wait_ge(l_rows, 16)

            def row(n, k):
                return rows[:, n, :].unsqueeze(1).to_broadcast([128, k, D])

            for h in range(2):
                dve.wait_ge(job_done, 15 + h)
                for k in range(2):
                    t = 4 * h + 2 * k
                    link(dve.tensor_tensor(H[:, t:t + 2, :], PS[:, 2 * (2 + h) + k, 0:2 * D].rearrange("p (t d) -> p t d", t=2),
                                           row(F3_PWB, 2), ALU.add))
            n_ln = [0]

            def norm(src, dst, nt):
                for t in range(nt):
                    ins = dve.bn_stats(bn[:, t, :], src[:, t, 0:D])
                link(ins)
                for t in range(nt):
                    ins = dve.bn_aggr(mv[:, t, :], bn[:, t, :])
                link(ins)
                n_ln[0] += 1
                dve.tensor_scalar(rstd[:, 0, 0:nt], mv[:, 0:nt, 1], EPS, None, ALU.add).then_inc(var_ready, 1)
                dve.wait_ge(std_ready, n_ln[0])
                link(dve.reciprocal(rstd[:, 2, 0:nt], rstd[:, 1, 0:nt]))
                link(dve.tensor_tensor(rstd[:, 3, 0:nt], rstd[:, 2, 0:nt], rstd[:, 2, 0:nt], ALU.mult))
                link(dve.tensor_tensor(rstd[:, 3, 0:nt], rstd[:, 3, 0:nt], rstd[:, 0, 0:nt], ALU.mult))
                link(dve.tensor_scalar(rstd[:, 3, 0:nt], rstd[:, 3, 0:nt], -0.5, 1.5, ALU.mult, ALU.add))
                link(dve.tensor_tensor(rstd[:, 2, 0:nt], rstd[:, 2, 0:nt], rstd[:, 3, 0:nt], ALU.mult))
                for t in range(nt):
                    ins = dve.tensor_scalar(dst[:, t, 0:D], src[:, t, 0:D], mv[:, t, 0:1], rstd[:, 2, t:t + 1],
                                            ALU.subtract, ALU.mult)
                link(ins)

            link(dve.memset(rstd[:], 1.0))
            link(dve.memset(cnt[:], 0.0))
            link(dve.memset(top8[:], 0.0))
            norm(H, H, 8)
            link(dve.tensor_tensor(H[:, 0:8, :], H[:, 0:8, :], row(LN_G, 8), ALU.mult))
            link(dve.tensor_tensor(H[:, 0:8, :], H[:, 0:8, :], row(LN_B, 8), ALU.add))
            dve.wait_ge(l_cls, 32)
            norm(H, Z, TT)
            norm(Z, Z, TT)
            link(dve.tensor_tensor(Z[:], Z[:], row(GAMMA, TT), ALU.mult))
            dve.tensor_tensor(Z[:], Z[:], row(BETA, TT), ALU.add).then_inc(abs_in, 1)
            dve.wait_ge(l_small, 64)
            for k, n in ((1, D), (2, INNER)):
                link(dve.tensor_scalar(qrank[:, k:k + 1], qrank[:, 0:1], float(n - 1), None, ALU.mult))
                link(dve.tensor_scalar(qrank[:, k:k + 1], qrank[:, k:k + 1], -1.0, float(n - 1), ALU.mult, ALU.add))
                link(dve.tensor_scalar(qrank[:, 2 + k:3 + k], qrank[:, k:k + 1], 4.0, None, ALU.subtract))

            def count_all(step, base, mag, n, level):
                for t in range(TT):
                    if t >= 2:
                        dve.wait_ge(step, base + t - 1)
                    dve.tensor_scalar(junk[0:ROWS[t], t % 2, 0:n], mag[0:ROWS[t], t, :], level[0:ROWS[t], t:t + 1],
                                      None, ALU.is_ge, ALU.add, accum_out=cnt[0:ROWS[t], t:t + 1]).then_inc(step, 1)
                dve.wait_ge(step, base + TT)

            def select_by_bits(step, mag, n, k):
                dve.memset(thr[:], 0).then_inc(step, 1)
                dve.memset(bitf[:], float(1 << 30)).then_inc(step, 1)
                dve.wait_ge(step, 2)
                with dve.Fori(0, 31) as i:
                    base = 14 * i + 2
                    dve.tensor_copy(biti[:], bitf[:]).then_inc(step, 1)
                    dve.wait_ge(step, base + 1)
                    dve.tensor_tensor(cand[:], thr[:], biti[:], ALU.bitwise_or).then_inc(step, 1)
                    dve.wait_ge(step, base + 2)
                    count_all(step, base + 2, mag, n, cand.bitcast(F32))
                    dve.scalar_tensor_tensor(hitb[:], cnt[:], qrank[:, k:k + 1], bitf[:], ALU.is_gt, ALU.mult).then_inc(step, 1)
                    dve.wait_ge(step, base + 12)
                    dve.tensor_tensor(thr[:], thr[:], hitb[:], ALU.bitwise_or).then_inc(step, 1)
                    dve.tensor_scalar(bitf[:], bitf[:], 0.5, None, ALU.mult).then_inc(step, 1)
                    dve.wait_ge(step, base + 14)

            def select(which, mag, n, k, start, slope):
                link(dve.tensor_scalar(lev[:], asum[:], qrank[:, 0:1], start / n, ALU.mult, ALU.mult))
                link(dve.tensor_scalar(inv[:], asum[:], 1.0 / (n * n * slope), None, ALU.mult))
                for p in range(PASSES):
                    if p:
                        link(dve.tensor_tensor(work[:, 1], err[:], inv[:], ALU.mult))
                        link(dve.tensor_tensor(work[:, 1], work[:, 1], work[:, 0], ALU.mult))
                        link(dve.tensor_tensor(lev[:], lev[:], work[:, 1], ALU.add))
                    step = count_done[which][p]
                    count_all(step, 0, mag, n, lev)
                    if p:
                        link(dve.tensor_copy(work[:, 2], err[:]))
                    link(dve.tensor_scalar(err[:], cnt[:], qrank[:, 2 + k:3 + k], None, ALU.subtract))
                    link(dve.tensor_tensor(work[:, 3], err[:], err[:], ALU.mult))
                    link(dve.tensor_scalar(work[:, 0], work[:, 3], 16.0, None, ALU.is_ge))
                    if p and p < PASSES - 1:
                        link(dve.tensor_tensor(work[:, 2], work[:, 2], err[:], ALU.subtract))
                        link(dve.tensor_tensor(work[:, 1], work[:, 1], work[:, 2], ALU.mult))
                        link(dve.scalar_tensor_tensor(work[:, 1], inv[:], 30.0, work[:, 1], ALU.mult, ALU.add))
                        link(dve.tensor_tensor(work[:, 2], work[:, 2], work[:, 2], ALU.mult))
                        link(dve.tensor_scalar(work[:, 2], work[:, 2], 30.0, None, ALU.add))
                        link(dve.reciprocal(work[:, 2], work[:, 2]))
                        link(dve.tensor_tensor(inv[:], work[:, 1], work[:, 2], ALU.mult))
                link(dve.memset(work[32:64, 0, 8:9], 0.0))
                link(dve.memset(work[64:128, 0, 8:9], 0.0))
                dve.tensor_reduce(far[:, 0:1], work[:, 0], AX.X, ALU.add).then_inc(far_ready, 1)
                for t in range(TT):
                    p = ROWS[t]
                    dve.scalar_tensor_tensor(below[0:p, t % 2, 0:n], mag[0:p, t, :], lev[0:p, t:t + 1], mag[0:p, t, :],
                                             ALU.is_lt, ALU.mult).then_inc(below_done, 1)
                    dve.wait_ge(below_done, 2 * TT * which + 2 * t + 1)
                    dve.max(top8[0:p, t, :], below[0:p, t % 2, 0:n]).then_inc(below_done, 1)
                    dve.wait_ge(below_done, 2 * TT * which + 2 * t + 2)
                link(dve.tensor_scalar(work[:, 1], cnt[:], qrank[:, k:k + 1], -1.0, ALU.subtract, ALU.mult))
                link(dve.tensor_tensor(pick[:], iota[:].unsqueeze(1).to_broadcast([128, TT, 8]),
                                       work[:, 1].unsqueeze(2).to_broadcast([128, TT, 8]), ALU.is_gt))
                link(dve.scalar_tensor_tensor(pick[:].rearrange("p t e -> p (t e)"), pick[:].rearrange("p t e -> p (t e)"),
                                              3e38, top8[:].rearrange("p t e -> p (t e)"), ALU.mult, ALU.add))
                link(dve.tensor_reduce(thr.bitcast(F32)[:], pick[:], AX.X, ALU.min))
                dve.wait_ge(far_summed, which + 1)
                link(dve.tensor_copy(far_i[0:1, :], PS[0:1, 0, 0:1]))
                left = dve.value_load(far_i[0:1, 0:1], min_val=0, max_val=NT)
                with dve.If(left > 0):
                    select_by_bits(bit_step[which], mag, n, k)

            dve.wait_ge(abs_done, TT)
            select(0, AB, D, 1, 1.43, 0.566)
            for t in range(TT):
                p = ROWS[t]
                dve.scalar_tensor_tensor(Z[0:p, t, :], AB[0:p, t, :], thr.bitcast(F32)[0:p, t:t + 1], Z[0:p, t, :],
                                         ALU.is_ge, ALU.mult).then_inc(masked1, 1)
            for n in range(6):
                g, c = n // 2, n % 2
                w = 512 if g < 2 else 32
                dve.wait_ge(xh_done, n + 1)
                dve.tensor_tensor(XL[:, c, 512 * g:512 * g + w], PS[0:HD, 3 * c + g, 0:w],
                                  XH.bitcast(F32)[:, c, 512 * g:512 * g + w], ALU.subtract).then_inc(xl_done, 1)
            link(dve.tensor_tensor(H[:], H[:], row(B_OUT, TT), ALU.add))
            for r in range(2):
                link(dve.memset(v_b[r][:, :, DH:DH + 1], 1.0))
            for q in range(1, 36, 2):
                dve.wait_ge(qk_done, q + 1)
                dve.tensor_copy(QKT[:, q // 3, 352 * (q % 3):352 * (q % 3) + 352], PS[:, (6 + q) % 8, 0:352])\
                   .then_inc(qk_copied_d, 1)
            dve.wait_ge(qk_copied_a, 18)
            dve.wait_ge(qk_copied_d, 18)

            def qk_copies(b, r):
                if due(b - 1):
                    dve.wait_ge(scores_done, b - 1)
                a, c = batch_cols(QKT, b)
                dve.tensor_copy(qk_b[r][:, :, 0:S], a)
                dve.tensor_copy(qk_b[r][:, :, S:KEYS].unsqueeze(3), c).then_inc(qkb_ready, 1)

            def shift(b):
                dve.wait_ge(scores_done, b + 1)
                sc = PS[0:KEYS, 0:2, 0:6 * KEYS].rearrange("p k (h n) -> p k h n", h=6)
                m = mx[:, 0, :].rearrange("p (k h) -> p k h", k=2)
                dve.tensor_reduce(m, sc, AX.X, ALU.max).then_inc(max_done, 1)
                dve.wait_ge(max_done, b + 1)
                if due(b):
                    dve.wait_ge(exp_done, b)
                dve.tensor_tensor(s_sb[:].rearrange("p (k h) n -> p k h n", k=2), sc,
                                  m.unsqueeze(3).to_broadcast([KEYS, 2, 6, KEYS]), ALU.subtract).then_inc(shifted, 1)

            def normalize(b, r):
                dve.wait_ge(pv_done, b + 1)
                pv = PS[0:KEYS, 6:8, 0:6 * (DH + 1)].rearrange("p k (h d) -> p k h d", h=6)
                rc = mx[:, 1, :].rearrange("p (k h) -> p k h", k=2)
                dve.reciprocal(rc.unsqueeze(3), pv[:, :, :, DH:DH + 1]).then_inc(recip_done, 1)
                dve.wait_ge(recip_done, b + 1)
                if not (isinstance(b, int) and b < 2):
                    if due(16 * b - 16 * r):
                        dve.wait_ge(o_stored[r], 16 * b - 16 * r)
                dve.tensor_tensor(o_b[r][:].rearrange("p (k h) d -> p k h d", k=2), pv[:, :, :, 0:DH],
                                  rc.unsqueeze(3).to_broadcast([KEYS, 2, 6, DH]), ALU.mult).then_inc(o_ready, 1)

            qk_copies(0, 0)
            qk_copies(1, 1)
            shift(0)
            qk_copies(2, 0)
            shift(1)
            normalize(0, 0)
            with dve.Fori(1, B // 2 - 1) as j:
                for k in range(2):
                    qk_copies(2 * j + k + 1, 1 - k)
                    shift(2 * j + k)
                    normalize(2 * j + (k - 1), 1 - k)
            qk_copies(B - 1, 1)
            shift(B - 2)
            normalize(B - 3, 1)
            shift(B - 1)
            normalize(B - 2, 0)
            normalize(B - 1, 1)

            dve.wait_ge(abs_done, 2 * TT)
            select(1, OA, INNER, 2, 1.74, 0.489)
            for t in range(TT):
                p = ROWS[t]
                dve.scalar_tensor_tensor(O[0:p, t, :], OA[0:p, t, :], thr.bitcast(F32)[0:p, t:t + 1], O[0:p, t, :],
                                         ALU.is_ge, ALU.mult).then_inc(masked2, 1)

            def rest_o(t):
                dve.wait_ge(oh_done, t + 1)
                cs = slice(t * 128, t * 128 + ROWS[t])
                dve.tensor_tensor(OL[:, :, cs].rearrange("p (k c) n -> p k c n", k=2),
                                  PS[:, 2 * (t % 3):2 * (t % 3) + 2, 0:384].rearrange("p k (c n) -> p k c n", c=3)[:, :, :, 0:ROWS[t]],
                                  OH.bitcast(F32)[:, :, cs].rearrange("p (k c) n -> p k c n", k=2),
                                  ALU.subtract).then_inc(ol_done, 1)

            def add_projection(t):
                p = ROWS[t]
                dve.wait_ge(proj_done, t + 1)
                dve.scalar_tensor_tensor(H[0:p, t, :], PS[0:p, 6 + t % 2, 0:D], wscale[0:p, 5:6], H[0:p, t, :],
                                         ALU.mult, ALU.add).then_inc(proj_added, 1)

            rest_o(0)
            for t in range(TT):
                if t + 1 < TT:
                    rest_o(t + 1)
                add_projection(t)
            dve.wait_ge(proj_added, TT)
            norm(H, X6, TT)
            dve.tensor_copy(X6[:, :, D:256], X6[:, :, 128:D]).then_inc(x6_ready, 1)
            for t in range(TT):
                dve.wait_ge(xfh_done, t + 1)
                cs = slice(t * 128, t * 128 + ROWS[t])
                dve.tensor_tensor(XFl[:, :, cs], PS[:, t % 4, 0:256].rearrange("p (c n) -> p c n", c=2)[:, :, 0:ROWS[t]],
                                  XFh.bitcast(F32)[:, :, cs], ALU.subtract).then_inc(xfl_done, 1)
            link(dve.memset(logit[:, 8, :], 0.0))
            dve.wait_ge(logits_done, 1)
            link(dve.tensor_copy(logit[:, 0:8, :], PS[:, 4, 0:8 * E].rearrange("p (t e) -> p t e", t=8)))
            link(dve.tensor_copy(logit[0:32, 8, :], PS[0:32, 4, 8 * E:9 * E]))
            for t in range(TT):
                ins = dve.max(top8[:, t, :], logit[:, t, :])
            link(ins)
            for t in range(TT):
                ins = dve.max_index(idx8[:, t, :], top8[:, t, :], logit[:, t, :])
            link(ins)
            dve.tensor_tensor(topw[:, 0, :], top8[:, :, 1], top8[:, :, 0], ALU.subtract).then_inc(diff_ready, 1)
            link(dve.tensor_copy(idxf[:], idx8[:, :, 0:2]))
            dve.wait_ge(exp2_done, 1)
            link(dve.tensor_scalar(topw[:, 2, :], topw[:, 1, :], 1.0, None, ALU.add))
            link(dve.reciprocal(topw[:, 2, :], topw[:, 2, :]))
            link(dve.tensor_tensor(topw[:, 3, :], topw[:, 1, :], topw[:, 2, :], ALU.mult))
            for t in range(TT):
                for k in range(2):
                    ins = dve.tensor_scalar(wsel[:, k, t, :], iota[:], idxf[:, t, k:k + 1], topw[:, 2 + k, t:t + 1],
                                            ALU.is_equal, ALU.mult)
            link(ins)
            link(dve.tensor_tensor(wE[:], wsel[:, 0], wsel[:, 1], ALU.add))

            def hidden(e2, k):
                w = BLOCKS[k % 3][2]
                for m in range(HC + 1):
                    if m < HC:
                        i = 6 * k + m
                        dve.wait_ge(silu_done, 36 * e2 + i + 1)
                        if not (isinstance(e2, int) and e2 == 0 and i < 2):
                            if due(36 * e2 + i - 1):
                                dve.wait_ge(hl_done, 36 * e2 + i - 1)
                        dve.tensor_tensor(hp[m % 2][:, 0:w], sg[m % 2][:, 0:w], PS[:, 2 * (i % 3) + 1, 0:w],
                                          ALU.mult).then_inc(hp_done, 1)
                    if m > 0:
                        i = 6 * k + m - 1
                        dve.wait_ge(hh_done, 36 * e2 + i + 1)
                        dve.tensor_tensor(hL[k % 2][:, m - 1, 0:w], hp[(m - 1) % 2][:, 0:w],
                                          hH[k % 2].bitcast(F32)[:, m - 1, 0:w], ALU.subtract).then_inc(hl_done, 1)

            def add_down(e2, k):
                n = k % 3
                for i in range(3):
                    t = BLOCKS[n][0] + i
                    d = 3 * k + i
                    p = ROWS[t]
                    dve.wait_ge(down_done, 18 * e2 + d + 1)
                    if due(18 * e2 + d - 8 if d >= 8 or not isinstance(e2, int) else 0):
                        dve.wait_ge(down_added, 18 * e2 + d - 8 if d >= 8 or not isinstance(e2, int) else 0)
                    w = wE[0:p, t, k // 3:k // 3 + 1] if isinstance(e2, int) else wE[0:p, t, bass.ts(e2 * 2 + k // 3, 1)]
                    if isinstance(e2, int):
                        w = wE[0:p, t, 2 * e2 + k // 3:2 * e2 + k // 3 + 1]
                    dve.scalar_tensor_tensor(H[0:p, t, :], PS[0:p, 6 + d % 2, 0:D], w, H[0:p, t, :], ALU.mult,
                                             ALU.add).then_inc(down_added, 1)

            def dve_pair(e2):
                hidden(e2, 0)
                for k in range(1, 6):
                    hidden(e2, k)
                    add_down(e2, k - 1)
                add_down(e2, 5)

            dve_pair(0)
            with dve.Fori(1, E // 2) as e2:
                dve_pair(e2)


def haar_matrix(np):
    one = np.array([[1.0, 1.0], [1.0, -1.0]])
    k = np.arange(256)
    m = np.ones((256, 256))
    for level in range(4):
        band = k >> 2 * (3 - level) & 3
        y, x = k // 16 >> level & 1, k % 16 >> level & 1
        m *= one[band >> 1][:, x] * one[band & 1][:, y]
    return m / 16


def kernel(**inputs):
    import numpy as np
    import concourse.bacc as bacc
    from concourse.bass_utils import run_bass_kernel_spmd

    a = {k: np.asarray(v) for k, v in inputs.items()}
    tok = {k[7:]: v for k, v in a.items() if k.startswith("L0_tok_")}
    c = np.ascontiguousarray
    dws = np.stack([tok[k].reshape(D, 9) for k in ("pl_dw", "pg_dw", "f1_dw", "f2_dw", "f3_dw")], 1)
    pws = np.stack([tok[k].reshape(D, D).T for k in ("pl_pw", "pg_pw", "pg_w2", "f1_pw", "f2_pw", "f3_pw")])
    vecs = np.stack([tok[k].reshape(D) for k in
                     ("pl_b", "pl_pwb", "pg_b1", "pg_pwb", "pg_b2", "alpha", "f1_pwb", "f2_pwb")])
    rows = np.stack([tok["f3_pwb"], tok["ln_g"], tok["ln_b"], a["L0_attn_gamma"], a["L0_attn_beta"],
                     a["L0_attn_b_out"], a["cls_tok"].reshape(D), tok["cls"].reshape(D)])
    wgu = np.concatenate([a["L0_ffn_Wg"].transpose(0, 2, 1), a["L0_ffn_Wu"].transpose(0, 2, 1)], 2)
    arrays = {
        "patches": c(a["x"].reshape(2, BH, C, G, PATCH, G, PATCH).transpose(2, 4, 6, 0, 3, 5, 1)
                     .reshape(KC, 128, NP_).transpose(1, 0, 2)),
        "plw": c(tok["pl_w"].reshape(D, KC, 128).transpose(2, 1, 0)),
        "w1t": c(tok["pg_w1"].reshape(D, 2, 128, C).transpose(2, 1, 3, 0).reshape(128, 2, C * D)),
        "haar": c(haar_matrix(np).astype(np.float32).reshape(2, 128, 256).transpose(1, 0, 2)),
        "ident": np.eye(128, dtype=np.float32),
        "vecs": c(vecs.reshape(8, 2, HD).transpose(2, 0, 1)),
        "dws": c(dws.reshape(2, HD, 5, 9).transpose(1, 0, 2, 3)),
        "pws": c(pws.reshape(6, 2, HD, D).transpose(2, 0, 1, 3)),
        "rows": c(rows),
        "sparsity": c(a["L0_attn_sparsity"].reshape(1)),
        "wqkv": c(a["L0_attn_w_qkv"].T.reshape(2, HD, 3 * INNER).transpose(1, 0, 2)),
        "wout": c(a["L0_attn_w_out"].T.reshape(HC, 128, D).transpose(1, 0, 2)),
        "router": c(a["L0_ffn_router_w"].T),
        "iota": c(np.tile(np.arange(E, dtype=np.float32), (128, 1))),
        "wgu": c(wgu),
        "wd": c(a["L0_ffn_Wd"].transpose(0, 2, 1).reshape(E, HC, 128, D).transpose(0, 2, 1, 3)),
    }
    nc = bacc.Bacc("TRN2", target_bir_lowering=False, num_devices=1)
    args = [nc.dram_tensor(k, v.shape, mybir.dt.from_np(v.dtype), kind="ExternalInput").ap() for k, v in arrays.items()]
    args.append(nc.dram_tensor("out", (B, KEYS, D), F32, kind="ExternalOutput").ap())
    build_tower(nc, *args)
    r = run_bass_kernel_spmd(nc, [arrays], core_ids=[0])
    return r.results[0]["out"]
```

```python
from contextlib import ExitStack

import concourse.bass as bass
from concourse import mybir

F32 = mybir.dt.float32
F32R = mybir.dt.float32r
BF16 = mybir.dt.bfloat16
I32 = mybir.dt.int32
U32 = mybir.dt.uint32
ALU = mybir.AluOpType
ACT = mybir.ActivationFunctionType
AX = mybir.AxisListType

B, C, IMG, PATCH = 16, 3, 128, 16
G = IMG // PATCH
S = G * G
D = 192
HD = D // 2
NP_ = B * S
NT = NP_ + 2 * B
BH = B // 2
HALF = NP_ // 2
KC = C * PATCH * PATCH // 128
HEADS, DH = 12, 64
INNER = HEADS * DH
KEYS = S + 2
TT = 9
E, HID = 8, 4 * D
HC = HID // 128
EPS = 1e-5
PASSES = 5
ROWS = [128] * 8 + [NT - NP_]
ACT_TILES = (7, 5)
EARLY = 6
DVE_ROWS = 6
FREE0, FREE1 = 16512, 229344

PL_B, PL_PWB, PG_B1, PG_PWB, PG_B2, ALPHA, F1_PWB, F2_PWB = range(8)
F3_PWB, LN_G, LN_B, GAMMA, BETA, B_OUT, CLS0, CLS1 = range(8)
DW_PL, DW_PG, DW_F1, DW_F2, DW_F3 = range(5)
PW_PL, PW_PG, PW_G2, PW_F1, PW_F2, PW_F3 = range(6)

BLOCKS = [(0, 3, 384), (3, 3, 384), (6, 3, NT - 768)]


def build_tower(nc, patches, plw, w1t, haar, ident_d, vecs_d, dws_d, pws_d, rows_d, sparsity, wqkv_d, wout_d,
                router_d, iota_d, wgu_d, wd_d, out):
    ctx = ExitStack()
    with ctx:
        o_scr = nc.dram_tensor("o_scratch", (NT, INNER), F32, kind="Internal").ap()

        plan = {}

        def place(zone, name, shape, dt):
            n = 1
            for k in shape[1:]:
                n *= k
            n *= 2 if dt == BF16 else 4
            at = (plan[zone] + 31) // 32 * 32
            plan[zone] = at + n
            assert plan[zone] <= FREE1, (name, plan[zone])
            return nc.alloc_sbuf_tensor_at(name, list(shape), dt, offset=at)

        def sem(name):
            return ctx.enter_context(nc.semaphore(name))

        def due(v):
            return not (isinstance(v, int) and v <= 0)

        plan["kept"] = FREE0
        ident = place("kept", "ident", [128, 128], F32)
        ones = place("kept", "ones", [128, 128], F32)
        rows = place("kept", "rows", [128, 6, D], F32)
        H = place("kept", "H", [128, TT, D], F32)
        vecs = place("kept", "vecs", [HD, 8, 2], F32)
        dws = place("kept", "dws", [HD, 2, 5, 9], F32)
        router = place("kept", "router", [128, 2, E], F32)
        router_h = place("kept", "router_h", [128, 2, E], F32R)
        router_l = place("kept", "router_l", [128, E], F32R)
        below = place("kept", "below", [128, 2, INNER], F32)
        iota = place("kept", "iota", [128, E], F32)
        gate = place("kept", "gate", [HD, 4, 2], F32)
        bn = place("kept", "bn", [128, TT, 6], F32)
        mv = place("kept", "mv", [128, TT, 2], F32)
        rstd = place("kept", "rstd", [128, 4, TT], F32)
        wsum = place("kept", "wsum", [128, 2, 96], F32)
        wabs = place("kept", "wabs", [128, 2], F32)
        wscale = place("kept", "wscale", [128, 8], F32)
        qrank = place("kept", "qrank", [128, 7], F32)
        thr = place("kept", "thr", [128, TT], I32)
        cand = place("kept", "cand", [128, TT], I32)
        biti = place("kept", "biti", [128, TT], I32)
        bitf = place("kept", "bitf", [128, TT], F32)
        hitb = place("kept", "hitb", [128, TT], I32)
        cnt = place("kept", "cnt", [128, TT], F32)
        asum = place("kept", "asum", [128, TT], F32)
        lev = place("kept", "lev", [128, TT], F32)
        inv = place("kept", "inv", [128, TT], F32)
        err = place("kept", "err", [128, 2, TT], F32)
        work = place("kept", "work", [128, 8, TT], F32)
        far = place("kept", "far", [128, 1], F32)
        far_i = place("kept", "far_i", [128, 1], I32)
        pick = place("kept", "pick", [128, TT, 8], F32)
        junk = place("kept", "junk", [128, 2, INNER], BF16)
        act_junk = place("kept", "act_junk", [128, 2, INNER], BF16)
        signs = place("kept", "signs", [128, TT], F32)
        logit = place("kept", "logit", [128, TT, E], F32)
        top8 = place("kept", "top8", [128, TT, 8], F32)
        idx8 = place("kept", "idx8", [128, TT, 8], U32)
        idxf = place("kept", "idxf", [128, TT, 2], F32)
        topw = place("kept", "topw", [128, 4, TT], F32)
        wsel = place("kept", "wsel", [128, 2, TT, E], F32)
        wE = place("kept", "wE", [128, TT, E], F32)
        Tqkv = place("kept", "Tqkv", [HD, 2, 3 * INNER], F32R)
        Tout = place("kept", "Tout", [128, HC, D], F32R)
        W0 = plan["kept"]

        plan["tok"] = W0
        patch = place("tok", "patch", [128, KC, NP_], F32)
        plw_sb = place("tok", "plw_sb", [128, KC, D], F32)
        wf_sb = place("tok", "wf_sb", [128, KC, D], F32)
        w1_sb = place("tok", "w1_sb", [128, 2, C * D], F32)
        haar_sb = place("tok", "haar_sb", [128, 2, 256], F32)
        padA = place("tok", "padA", [HD, 2, 2, G + 2, G + 2, BH], F32)
        padB = place("tok", "padB", [HD, 2, 2, G + 2, G + 2, BH], F32)
        dwA = place("tok", "dwA", [HD, 2, NP_], F32)
        dwB = place("tok", "dwB", [HD, 2, NP_], F32)
        loc = place("tok", "loc", [HD, 2, NP_], F32)
        g2 = place("tok", "g2", [HD, 2, NP_], F32)
        t1 = place("tok", "t1", [HD, 2, NP_], F32)
        pws = place("tok", "pws", [HD, 6, 2, D], F32)
        products = place("tok", "products", [HD, 8, 2, (G - DVE_ROWS) * G * BH], F32)
        wq_raw = place("tok", "wq_raw", [HD, 2, 3 * INNER], F32)
        wo_raw = place("tok", "wo_raw", [128, HC, D], F32)
        neg1 = place("tok", "neg1", [128, 3 * INNER], F32)

        plan["att"] = W0
        Z = place("att", "Z", [128, TT, D], F32)
        AB = place("att", "AB", [128, TT, D], F32)
        XH = place("att", "XH", [HD, 2, NT], F32R)
        XL = place("att", "XL", [HD, 2, NT], F32R)
        QKT = place("att", "QKT", [128, 12, NT], F32)
        qk_b = [place("att", f"qk_b{r}", [128, 12, KEYS], F32) for r in range(2)]
        xh_b = [place("att", f"xh_b{r}", [HD, 2, KEYS], F32R) for r in range(2)]
        xl_b = [place("att", f"xl_b{r}", [HD, 2, KEYS], F32R) for r in range(2)]
        v_b = [place("att", f"v_b{r}", [KEYS, HEADS, DH + 1], F32) for r in range(2)]
        s_sb = place("att", "s_sb", [KEYS, HEADS, KEYS], F32)
        p_sb = [place("att", f"p_sb{r}", [KEYS, HEADS, KEYS], F32) for r in range(2)]
        pT_sb = place("att", "pT_sb", [KEYS, HEADS, KEYS], F32)
        o_b = [place("att", f"o_b{r}", [KEYS, HEADS, DH], F32) for r in range(2)]
        mx = place("att", "mx", [KEYS, 2, HEADS], F32)
        O = place("att", "O", [128, TT, INNER], F32)
        plan["out"] = W0
        OA = place("out", "OA", [128, TT, INNER], F32)
        OH = place("out", "OH", [128, HC, NT], F32R)
        OL = place("out", "OL", [128, HC, NT], F32R)
        assert plan["out"] <= plan["att"] - TT * INNER * 4
        O_AT = plan["att"] - TT * INNER * 4
        plan["moe"] = W0
        X6 = place("moe", "X6", [128, TT, 256], F32)
        XFh = place("moe", "XFh", [128, 2, NT], F32R)
        XFl = place("moe", "XFl", [128, 2, NT], F32R)
        hH = [place("moe", f"hH{r}", [128, HC, 384], F32R) for r in range(2)]
        hL = [place("moe", f"hL{r}", [128, HC, 384], F32R) for r in range(2)]
        sg = [place("moe", f"sg{r}", [128, 384], F32) for r in range(2)]
        hp = [place("moe", f"hp{r}", [128, 384], F32) for r in range(2)]
        lgT = place("moe", "lgT", [E, NT], F32)
        assert plan["moe"] <= plan["out"]
        plan["raw"] = plan["att"]
        raw_a = place("raw", "raw_a", [128, 2 * HID], F32)
        raw_d = place("raw", "raw_d", [128, HC, D], F32)
        plan["w0"] = plan["out"]
        raw_b = place("w0", "raw_b", [128, 2 * HID], F32)
        plan["w1"] = O_AT
        Wh = [place(f"w{r}", f"Wh{r}", [128, 2 * HID], F32R) for r in range(2)]
        Wl = [place(f"w{r}", f"Wl{r}", [128, 2 * HID], F32R) for r in range(2)]
        Wm = [place(f"w{r}", f"Wm{r}", [128, 2 * HID], F32R) for r in range(2)]
        Dhl = [place(f"w{r}", f"Dhl{r}", [128, HC, 2 * D], F32R) for r in range(2)]
        assert plan["w0"] <= O_AT and plan["w1"] <= plan["att"]

        PS = ctx.enter_context(nc.psum_tensor("PS", [128, 8, 512], F32))

        l_fold, l_plw, l_vecs, l_dws, l_pws = (sem(n) for n in ("l_fold", "l_plw", "l_vecs", "l_dws", "l_pws"))
        l_patch = [[sem(f"l_patch{h}{k}") for k in range(KC // 2)] for h in range(2)]
        l_wqkv, l_wout, l_ident, l_rows, l_cls, l_small = (
            sem(n) for n in ("l_wqkv", "l_wout", "l_ident", "l_rows", "l_cls", "l_small"))
        l_o = [sem(f"l_o{t}") for t in range(TT)]
        l_exp = sem("l_exp")
        pads_zero, h8_zero = sem("pads_zero"), sem("h8_zero")
        fold_done, fold_copied = sem("fold_done"), sem("fold_copied")
        tanh_done, gate_done = sem("tanh_done"), sem("gate_done")
        job_done, job_copied = sem("job_done"), sem("job_copied")
        tap_done, product_done, sum_done, mix_done = (sem(n) for n in ("tap_done", "product_done", "sum_done", "mix_done"))
        wsum_ready, wmean_ready, wmean_read = sem("wsum_ready"), sem("wmean_ready"), sem("wmean_read")
        dve_done = sem("dve_done")
        var_ready, std_ready = sem("var_ready"), sem("std_ready")
        abs_in, abs_done = sem("abs_in"), sem("abs_done")
        asum_set, far_ready, far_summed, below_done = (sem(n) for n in ("asum_set", "far_ready", "far_summed", "below_done"))
        lev_ready, signs_done = [sem("lev_ready0"), sem("lev_ready1")], [sem("signs_done0"), sem("signs_done1")]
        count_done = [[sem(f"count_done{w}{p}") for p in range(PASSES)] for w in range(2)]
        bit_step = [sem("bit_step0"), sem("bit_step1")]
        masked1, xT_done, xh_done, xl_done = (sem(n) for n in ("masked1", "xT_done", "xh_done", "xl_done"))
        qk_done, qk_copied_a, qk_copied_d = sem("qk_done"), sem("qk_copied_a"), sem("qk_copied_d")
        qkb_ready, xb_ready = sem("qkb_ready"), sem("xb_ready")
        scores_done, v_done, pT_done, pv_done = (sem(n) for n in ("scores_done", "v_done", "pT_done", "pv_done"))
        max_done, shifted, exp_done = sem("max_done"), sem("shifted"), sem("exp_done")
        pT_copied, v_copied, recip_done, o_ready = (sem(n) for n in ("pT_copied", "v_copied", "recip_done", "o_ready"))
        o_stored = [sem("o_stored0"), sem("o_stored1")]
        masked2, oT_done, oh_done, ol_done = (sem(n) for n in ("masked2", "oT_done", "oh_done", "ol_done"))
        proj_done, proj_added = sem("proj_done"), sem("proj_added")
        x6_ready, xfT_done, xfh_done, xfl_done = (sem(n) for n in ("x6_ready", "xfT_done", "xfh_done", "xfl_done"))
        logits_done, diff_ready, exp2_done = sem("logits_done"), sem("diff_ready"), sem("exp2_done")
        router_split, lgT_done, lgT_copied, logits_read = (
            sem(n) for n in ("router_split", "lgT_done", "lgT_copied", "logits_read"))
        half_added = sem("half_added")
        w_hi, w_lo = sem("w_hi"), sem("w_lo")
        gu_done, silu_done, hp_done, hh_done, hl_done = (
            sem(n) for n in ("gu_done", "silu_done", "hp_done", "hh_done", "hl_done"))
        down_done, down_added = sem("down_done"), sem("down_added")
        stored = sem("stored")

        block = ctx.enter_context(nc.Block())

        JOBS = [("loc", 0), ("loc", 1), ("g", 0), (PW_PL, 0), ("g", 1), (PW_PG, 0), (PW_G2, 0), (PW_PL, 1), (PW_PG, 1),
                (PW_G2, 1), (PW_F1, 0), (PW_F1, 1), (PW_F2, 0), (PW_F2, 1), (PW_F3, 0), (PW_F3, 1)]
        DWS = [(DW_PL, 0), (DW_PL, 1), (DW_PG, 0), (DW_PG, 1), (DW_F1, 0), (DW_F1, 1), (DW_F2, 0), (DW_F2, 1), (DW_F3, 0),
               (DW_F3, 1)]
        dw_pad = {DW_PL: padA, DW_PG: padB, DW_F1: padA, DW_F2: padB, DW_F3: padA}
        dw_out = {DW_PL: dwA, DW_PG: dwB, DW_F1: dwA, DW_F2: dwB, DW_F3: dwA}
        pw_of = {PW_PL: DW_PL, PW_PG: DW_PG, PW_F1: DW_F1, PW_F2: DW_F2, PW_F3: DW_F3}
        source = {DW_PL: "loc", DW_PG: "g", DW_F1: PW_G2, DW_F2: PW_F1, DW_F3: PW_F2}
        last_use = {DW_F1: PW_PL, DW_F2: PW_PG, DW_F3: PW_F1}

        def window(pad, m, h, dy, dx, y0=0, y1=G):
            return pad[:, m, h, dy + y0:dy + y1, dx:dx + G, :].rearrange("p y x b -> p y (x b)")

        def inside(pad, m, h):
            return window(pad, m, h, 1, 1)

        def cols(t, m, h):
            return t[:, m, h * HALF:(h + 1) * HALF].rearrange("p (y n) -> p y n", y=G)

        def job(kind, h):
            return JOBS.index((kind, h)) + 1

        def tap_args(n, tap, m, y0, y1):
            f, h = DWS[n]
            return (cols(dw_out[f], m, h)[:, y0:y1, :], window(dw_pad[f], m, h, tap // 3, tap % 3, y0, y1),
                    dws[:, m, f, tap:tap + 1])

        def slot(h):
            return h % 2 * (HEADS // 2) + h // 2

        def patch_rows(b):
            return bass.DynSlice(b + (b // BH) * (HALF - BH), S, step=BH)

        def batch_cols(t, b):
            return t[:, :, patch_rows(b)], t[:, :, NP_:NT].rearrange("p c (k b) -> p c k b", k=2)[:, :, :, bass.ts(b, 1)]

        def moe_columns(n):
            t0, nt, w = BLOCKS[n]
            return slice(t0 * 128, t0 * 128 + w)

        @block.sync
        def _(sp):
            sp.dma_start(haar_sb[:], haar).then_inc(l_fold, 16)
            sp.dma_start(w1_sb[:], w1t).then_inc(l_fold, 16)
            sp.dma_start(plw_sb[:], plw).then_inc(l_plw, 16)
            for h in range(2):
                for k in range(0, KC, 2):
                    c = slice(h * HALF, (h + 1) * HALF)
                    sp.dma_start(patch[:, k:k + 2, c], patches[:, k:k + 2, c]).then_inc(l_patch[h][k // 2], 16)

            def store_o(b, r):
                sp.wait_ge(o_ready, b + 1)
                sp.dma_start(o_scr[patch_rows(b), :], o_b[r][0:S].rearrange("p h d -> p (h d)")).then_inc(o_stored[r], 16)
                sp.dma_start(o_scr[NP_:NT, :].rearrange("(k b) n -> k b n", k=2)[:, bass.ts(b, 1), :],
                             o_b[r][S:KEYS].rearrange("p h d -> p (h d)").unsqueeze(1)).then_inc(o_stored[r], 16)

            for half in range(2):
                with sp.Fori(half * (BH // 2), (half + 1) * (BH // 2)) as j:
                    store_o(2 * j, 0)
                    store_o(2 * j + 1, 1)
                sp.wait_ge(o_stored[0], 16 * BH * (half + 1))
                sp.wait_ge(o_stored[1], 16 * BH * (half + 1))
                for t in range(4 * half, 4 * half + 4 + half):
                    sp.dma_start(O[0:ROWS[t], t, :], o_scr[t * 128:t * 128 + ROWS[t], :]).then_inc(l_o[t], 16)

            def load_expert(e):
                if due(3 * e):
                    sp.wait_ge(w_lo, 3 * e)
                sp.dma_start(raw_a[:], wgu_d[bass.ts(e, 1), 0:128, :].rearrange("e p n -> (e p) n")).then_inc(l_exp, 16)
                for half in range(2):
                    sp.dma_start(raw_b[64 * half:64 * half + 64, :],
                                 wgu_d[bass.ts(e, 1), 128:D, :].rearrange("e p n -> (e p) n")).then_inc(l_exp, 16)
                sp.dma_start(raw_d[:], wd_d[bass.ts(e, 1)].rearrange("e p c n -> (e p) c n")).then_inc(l_exp, 16)

            load_expert(0)
            with sp.Fori(1, E) as e:
                load_expert(e)
            sp.wait_ge(down_added, E * TT)
            for b in range(B):
                h, i = b // BH, b % BH
                sp.dma_start(out[b, 2:KEYS, :].rearrange("(t s) d -> s t d", t=4), H[i::BH, 4 * h:4 * h + 4, :])\
                    .then_inc(stored, 16)
            for k in range(2):
                sp.dma_start(out[:, k, :], H[16 * k:16 * k + 16, 8, :]).then_inc(stored, 16)
            sp.wait_ge(stored, 18 * 16)

        @block.gpsimd
        def _(pool):
            pool.dma_start(ident[:], ident_d).then_inc(l_ident, 16)
            pool.memset(padA[:], 0.0).then_inc(pads_zero, 1)
            pool.memset(padB[:], 0.0).then_inc(pads_zero, 1)
            pool.memset(H[:, 8, :], 0.0).then_inc(h8_zero, 1)
            pool.dma_start(rows[:], rows_d[0:6, :].partition_broadcast(128)).then_inc(l_rows, 16)
            pool.dma_start(qrank[:, 0:1], sparsity.partition_broadcast(128)).then_inc(l_small, 16)
            pool.dma_start(iota[:], iota_d).then_inc(l_small, 16)
            pool.dma_start(router[:, 0, :], router_d[0:128, :]).then_inc(l_small, 16)
            for half in range(2):
                pool.dma_start(router[64 * half:64 * half + 64, 1, :], router_d[128:D, :]).then_inc(l_small, 16)
            pool.wait_ge(h8_zero, 1)
            for k in range(2):
                pool.dma_start(H[16 * k:16 * k + 16, 8, :], rows_d[CLS0 + k, :].partition_broadcast(16)).then_inc(l_cls, 16)

            for n in range(10):
                for tap in range(1, 9):
                    pool.wait_ge(product_done, 18 * n + 2 * tap + 2)
                    if due(8 * n + tap - 1):
                        pool.wait_ge(sum_done, 8 * n + tap - 1)
                    f, h = DWS[n]
                    dst = dw_out[f][:, :, h * HALF + DVE_ROWS * G * BH:(h + 1) * HALF]
                    pool.tensor_tensor(dst, dst, products[:, tap - 1], ALU.add).then_inc(sum_done, 1)

            def x_copies(b, r):
                if due(b - 1):
                    pool.wait_ge(v_done, b - 1)
                for src, dst in ((XH, xh_b[r]), (XL, xl_b[r])):
                    a, c = batch_cols(src.bitcast(F32), b)
                    pool.tensor_copy(dst[:, :, 0:S], a)
                    last = pool.tensor_copy(dst[:, :, S:KEYS].unsqueeze(3), c)
                last.then_inc(xb_ready, 1)

            pool.wait_ge(xh_done, 6)
            pool.wait_ge(xl_done, 6)
            x_copies(0, 0)
            x_copies(1, 1)
            with pool.Fori(1, B // 2) as j:
                x_copies(2 * j, 0)
                x_copies(2 * j + 1, 1)

            def rests(e, r):
                pool.wait_ge(w_hi, 3 * (e + 1))
                if not (isinstance(e, int) and e < 2):
                    if due(TT * (e - 1)):
                        pool.wait_ge(down_done, TT * (e - 1))
                pool.tensor_tensor(Wl[r][:], raw_a[:], Wh[r].bitcast(F32)[:], ALU.subtract).then_inc(w_lo, 1)
                pool.wait_ge(w_lo, 3 * e + 1)
                pool.tensor_tensor(Wm[r][64:128, :], raw_b[64:128, :], Wm[r].bitcast(F32)[64:128, :],
                                   ALU.subtract).then_inc(w_lo, 1)
                pool.wait_ge(w_lo, 3 * e + 2)
                pool.tensor_tensor(Dhl[r][:, :, D:2 * D], raw_d[:], Dhl[r].bitcast(F32)[:, :, 0:D], ALU.subtract).then_inc(w_lo, 1)

            rests(0, 0)
            rests(1, 1)
            with pool.Fori(1, E // 2) as j:
                rests(2 * j, 0)
                rests(2 * j + 1, 1)

        @block.scalar
        def _(act):
            act.dma_start(vecs[:], vecs_d).then_inc(l_vecs, 16)
            act.dma_start(dws[:], dws_d).then_inc(l_dws, 16)
            act.dma_start(wq_raw[:], wqkv_d).then_inc(l_wqkv, 16)
            act.dma_start(wo_raw[:], wout_d).then_inc(l_wout, 16)
            act.dma_start(pws[:], pws_d).then_inc(l_pws, 16)
            act.wait_ge(l_vecs, 16)
            act.activation(gate[:, 0, :], vecs[:, ALPHA, :], ACT.Tanh).then_inc(tanh_done, 1)
            act.wait_ge(fold_done, 1)
            for pc in range(2):
                act.activation(wf_sb[:, pc:pc + 3:2, :],
                               PS[:, 4 + 2 * pc, 0:2 * D].rearrange("p (c d) -> p c d", c=2), ACT.Copy).then_inc(fold_copied, 1)
                act.activation(wf_sb[:, 4 + pc, :], PS[:, 5 + 2 * pc, 0:D], ACT.Copy).then_inc(fold_copied, 1)
            act.wait_ge(pads_zero, 2)

            def copy_job(j):
                kind, h = JOBS[j]
                act.wait_ge(job_done, j + 1)
                if kind == PW_G2:
                    act.wait_ge(gate_done, 3)
                for m in range(2):
                    ps = PS[0:HD, 2 * (j % 4) + m, :]
                    psv = ps.rearrange("p (y n) -> p y n", y=G)
                    c = slice(h * HALF, (h + 1) * HALF)
                    bias = {"loc": PL_B, "g": PG_B1, PW_PL: PL_PWB, PW_PG: PG_PWB, PW_F1: F1_PWB, PW_F2: F2_PWB}.get(kind)
                    bias = gate[:, 3, m:m + 1] if bias is None else vecs[:, bias, m:m + 1]
                    if kind == "loc":
                        ins = act.activation(inside(padA, m, h), psv, ACT.Gelu, bias=bias)
                    elif kind == "g":
                        ins = act.activation(inside(padB, m, h), psv, ACT.Gelu, bias=bias)
                    elif kind == PW_PL:
                        ins = act.activation(loc[:, m, c], ps, ACT.Identity, bias=bias)
                    elif kind == PW_PG:
                        ins = act.activation(g2[:, m, c], ps, ACT.Gelu, bias=bias)
                    elif kind == PW_G2:
                        ins = act.activation(t1[:, m, c], ps, ACT.Identity, bias=bias, scale=gate[:, 1, m:m + 1])
                    elif kind == PW_F1:
                        ins = act.activation(inside(padB, m, h), psv, ACT.Relu, bias=bias)
                    else:
                        ins = act.activation(t1[:, m, c], ps, ACT.Relu, bias=bias)
                ins.then_inc(job_copied, 1)

            def products_of(n, first=0, last=9):
                f, h = DWS[n]
                act.wait_ge(job_copied, job(source[f], h))
                if f in (DW_F1, DW_F3):
                    act.wait_ge(mix_done, 2 * h + (2 if f == DW_F1 else 6))
                if f in last_use:
                    act.wait_ge(job_done, job(last_use[f], h))
                for tap in range(first, last):
                    if n and tap:
                        act.wait_ge(sum_done, 8 * (n - 1) + tap)
                    for m in range(2):
                        dst, src, w = tap_args(n, tap, m, DVE_ROWS, G)
                        if tap:
                            dst = products[:, tap - 1, m, :].rearrange("p (y n) -> p y n", y=G - DVE_ROWS)
                        act.activation(dst, src, ACT.Copy, scale=w).then_inc(product_done, 1)

            act.wait_ge(l_dws, 16)
            for step in ("c0", "p0", "c1", "p1", "c2", "p2", "c3", "c4", "a3", "c5", "b3", "c6", "c7",
                         "c8", "p4", "c9", "p5", "c10", "p6", "c11", "p7", "c12", "p8", "c13", "p9"):
                if step[0] == "c":
                    copy_job(int(step[1:]))
                elif step[0] == "p":
                    products_of(int(step[1:]))
                else:
                    products_of(int(step[1:]), *((0, 5) if step[0] == "a" else (5, 9)))

            def sqrt(n):
                if due(n):
                    act.wait_ge(var_ready, n)
                act.activation(rstd[:, 1, :], rstd[:, 0, :], ACT.Sqrt).then_inc(std_ready, 1)

            for n in range(3):
                sqrt(n + 1)
            act.wait_ge(abs_in, 1)
            act.wait_ge(asum_set, 1)
            for t in range(TT):
                act.activation(AB[0:ROWS[t], t, :], Z[0:ROWS[t], t, :], ACT.Abs,
                               accum_out=asum[0:ROWS[t], t:t + 1]).then_inc(abs_done, 1)

            def sign_counts(which, mag, n):
                for p in range(PASSES - 1):
                    act.wait_ge(lev_ready[which], p + 1)
                    for t in range(ACT_TILES[which], TT):
                        i = p * (TT - ACT_TILES[which]) + t - ACT_TILES[which]
                        if i >= 2:
                            act.wait_ge(signs_done[which], i - 1)
                        act.activation(act_junk[0:ROWS[t], i % 2, 0:n], mag[0:ROWS[t], t, :], ACT.Sign,
                                       bias=lev[0:ROWS[t], t:t + 1], scale=-1.0,
                                       accum_out=signs[0:ROWS[t], t:t + 1]).then_inc(signs_done[which], 1)

            sign_counts(0, AB, D)
            for n in range(6):
                g, c = n // 2, n % 2
                w = 512 if g < 2 else 32
                act.wait_ge(xT_done, n + 1)
                act.activation(XH[:, c, 512 * g:512 * g + w], PS[0:HD, 3 * c + g, 0:w], ACT.Copy).then_inc(xh_done, 1)
            for q in range(0, 36, 2):
                act.wait_ge(qk_done, q + 1)
                act.activation(QKT[:, q // 3, 352 * (q % 3):352 * (q % 3) + 352], PS[:, (6 + q) % 8, 0:352],
                               ACT.Copy).then_inc(qk_copied_a, 1)

            def copy_pT(b):
                act.wait_ge(pT_done, b + 1)
                if due(b):
                    act.wait_ge(pv_done, b)
                act.activation(pT_sb[:].rearrange("p (k h) n -> p k h n", k=2),
                               PS[0:KEYS, 4:6, 0:6 * KEYS].rearrange("p k (h n) -> p k h n", h=6),
                               ACT.Copy).then_inc(pT_copied, 1)

            def copy_v(b, r):
                act.wait_ge(v_done, b + 1)
                if due(b - 1):
                    act.wait_ge(pv_done, b - 1)
                act.activation(v_b[r][:, :, 0:DH].rearrange("p (k h) d -> p k h d", k=2),
                               PS[0:KEYS, 2:4, 0:384].rearrange("p k (h d) -> p k h d", h=6),
                               ACT.Copy).then_inc(v_copied, 1)

            def exp(b, r):
                act.wait_ge(shifted, b + 1)
                if due(b - 1):
                    act.wait_ge(pT_done, b - 1)
                act.activation(p_sb[r][:], s_sb[:], ACT.Exp, scale=wscale[0:KEYS, 4:5]).then_inc(exp_done, 1)

            copy_v(0, 0)
            copy_v(1, 1)
            exp(0, 0)
            copy_pT(0)
            exp(1, 1)
            def magnitudes(tiles):
                for t in tiles:
                    act.wait_ge(l_o[t], 16)
                    act.activation(OA[0:ROWS[t], t, :], O[0:ROWS[t], t, :], ACT.Abs,
                                   accum_out=asum[0:ROWS[t], t:t + 1]).then_inc(abs_done, 1)

            for first, end in ((1, EARLY), (EARLY, B // 2)):
                with act.Fori(first, end) as j:
                    for k in range(2):
                        copy_pT(2 * j + (k - 1))
                        copy_v(2 * j + k, k)
                        exp(2 * j + k, k)
                if end == EARLY:
                    magnitudes(range(4))
            copy_pT(B - 1)

            def highs(e, r):
                act.wait_ge(l_exp, 64 * (e + 1))
                if not (isinstance(e, int) and e < 2):
                    if due(TT * (e - 1)):
                        act.wait_ge(down_done, TT * (e - 1))
                act.activation(Wh[r][:], raw_a[:], ACT.Copy).then_inc(w_hi, 1)
                act.activation(Wm[r][:], raw_b[:], ACT.Copy).then_inc(w_hi, 1)
                act.activation(Dhl[r][:, :, 0:D], raw_d[:], ACT.Copy).then_inc(w_hi, 1)

            magnitudes(range(4, TT))
            sign_counts(1, OA, INNER)
            highs(0, 0)
            for t in range(TT):
                act.wait_ge(oT_done, t + 1)
                act.activation(OH[:, :, t * 128:t * 128 + ROWS[t]].rearrange("p (k c) n -> p k c n", k=2),
                               PS[:, 2 * (t % 3):2 * (t % 3) + 2, 0:384].rearrange("p k (c n) -> p k c n", c=3)[:, :, :, 0:ROWS[t]],
                               ACT.Copy).then_inc(oh_done, 1)
            sqrt(4)
            for t in range(TT):
                act.wait_ge(xfT_done, t + 1)
                act.activation(XFh[:, :, t * 128:t * 128 + ROWS[t]],
                               PS[:, t % 4, 0:256].rearrange("p (c n) -> p c n", c=2)[:, :, 0:ROWS[t]],
                               ACT.Copy).then_inc(xfh_done, 1)
            for n in range(3):
                act.wait_ge(lgT_done, n + 1)
                act.activation(lgT[:, 352 * n:352 * n + 352], PS[0:E, 5 + n, 0:352], ACT.Copy).then_inc(lgT_copied, 1)

            def act_block(e2, k):
                n, w = k % 3, BLOCKS[k % 3][2]
                for m in range(HC + 1):
                    if m < HC:
                        i = 6 * k + m
                        act.wait_ge(gu_done, 36 * e2 + i + 1)
                        if due(36 * e2 + i - 1):
                            act.wait_ge(hp_done, 36 * e2 + i - 1)
                        act.activation(sg[m % 2][:, 0:w], PS[:, 2 * (i % 3), 0:w], ACT.Silu).then_inc(silu_done, 1)
                    if m > 0:
                        i = 6 * k + m - 1
                        act.wait_ge(hp_done, 36 * e2 + i + 1)
                        if k >= 2 or not isinstance(e2, int):
                            if due(18 * e2 + 3 * (k - 1)):
                                act.wait_ge(down_done, 18 * e2 + 3 * (k - 1))
                        act.activation(hH[k % 2][:, m - 1, 0:w], hp[(m - 1) % 2][:, 0:w], ACT.Copy).then_inc(hh_done, 1)

            for k in range(6):
                act_block(0, k)
                if k == 0:
                    act.wait_ge(diff_ready, 1)
                    act.activation(topw[:, 1, :], topw[:, 0, :], ACT.Exp).then_inc(exp2_done, 1)
                    highs(1, 1)
                if k == 4:
                    highs(2, 0)
            with act.Fori(1, E // 2 - 1) as e2:
                for k in range(6):
                    act_block(e2, k)
                    if k == 0:
                        highs(2 * e2 + 1, 1)
                    if k == 4:
                        highs(2 * e2 + 2, 0)
            for k in range(6):
                act_block(E // 2 - 1, k)
                if k == 0:
                    highs(E - 1, 1)

        @block.tensor
        def _(pe):
            pe.wait_ge(l_fold, 32)
            for pc in range(2):
                for bank, c0, n in ((4 + 2 * pc, 0, 2 * D), (5 + 2 * pc, 2 * D, D)):
                    for k in range(2):
                        mm = pe.matmul(PS[:, bank, 0:n], haar_sb[:, k, 128 * pc:128 * pc + 128],
                                       w1_sb[:, k, c0:c0 + n], start=(k == 0), stop=(k == 1))
            mm.then_inc(fold_done, 1)
            pe.wait_ge(l_plw, 16)
            for j, (kind, h) in enumerate(JOBS):
                b0 = 2 * (j % 4)
                c = slice(h * HALF, (h + 1) * HALF)
                if j == 2:
                    pe.wait_ge(fold_copied, 4)
                if j == 3:
                    pe.wait_ge(wmean_read, 2)
                if j >= 4:
                    if due(j - 3):
                        pe.wait_ge(job_copied, j - 3)
                if kind not in ("loc", "g"):
                    pe.wait_ge(l_pws, 16)
                if kind in pw_of:
                    pe.wait_ge(tap_done, 18 * (DWS.index((pw_of[kind], h)) + 1))
                    pe.wait_ge(sum_done, 8 * (DWS.index((pw_of[kind], h)) + 1))
                if kind == PW_G2:
                    pe.wait_ge(job_copied, job(PW_PG, h))
                if kind == PW_F3:
                    src = dw_out[DW_F3]
                    for i in range(4):
                        t = 4 * h + i
                        for k in range(2):
                            mm = pe.matmul(PS[:, b0 + i // 2, (i % 2) * D:(i % 2) * D + D],
                                           src[:, k, t * 128:t * 128 + 128], pws[:, PW_F3, k, :],
                                           start=(k == 0), stop=(k == 1))
                elif kind in ("loc", "g"):
                    w = plw_sb if kind == "loc" else wf_sb
                    for k in range(KC):
                        if kind == "loc" and k % 2 == 0:
                            pe.wait_ge(l_patch[h][k // 2], 16)
                        for m in range(2):
                            mm = pe.matmul(PS[0:HD, b0 + m, :], w[:, k, m * HD:m * HD + HD], patch[:, k, c],
                                           start=(k == 0), stop=(k == KC - 1))
                else:
                    src = g2 if kind == PW_G2 else dw_out[pw_of[kind]]
                    for m in range(2):
                        for k in range(2):
                            mm = pe.matmul(PS[0:HD, b0 + m, :], pws[:, kind, k, m * HD:m * HD + HD], src[:, k, c],
                                           start=(k == 0), stop=(k == 1))
                mm.then_inc(job_done, 1)
                if j == 0:
                    pe.wait_ge(wsum_ready, 2)
                    pe.wait_ge(fold_copied, 4)
                    pe.matmul(PS[:, 7, 0:1], ones[0:HD, :], wabs[0:HD, 0:1], start=True, stop=True)
                    pe.matmul(PS[:, 7, 1:2], ones[:, :], wabs[:, 1:2], start=True, stop=True).then_inc(wmean_ready, 1)
            def sum_far(which):
                pe.wait_ge(far_ready, which + 1)
                pe.matmul(PS[:, 0, 0:1], ones[:], far[:], start=True, stop=True).then_inc(far_summed, 1)

            sum_far(0)
            pe.wait_ge(l_ident, 16)
            for g in range(3):
                for c in range(2):
                    for t in range(4 * g, min(4 * g + 4, TT)):
                        pe.wait_ge(masked1, t + 1)
                        tr = pe.transpose(PS[0:HD, 3 * c + g, (t % 4) * 128:(t % 4) * 128 + ROWS[t]],
                                          Z[0:ROWS[t], t, c * HD:c * HD + HD], ident[0:ROWS[t], 0:ROWS[t]])
                    tr.then_inc(xT_done, 1)
            pe.wait_ge(xh_done, 6)
            pe.wait_ge(xl_done, 6)
            for q in range(36):
                m, n = q // 3, q % 3
                if due((q - 8) // 2 + 1):
                    pe.wait_ge(qk_copied_a if q % 2 == 0 else qk_copied_d, (q - 8) // 2 + 1)
                for c in range(2):
                    for x in (XH, XL):
                        mm = pe.matmul(PS[:, (6 + q) % 8, 0:352], Tqkv[:, c, 128 * m:128 * m + 128],
                                       x[:, c, 352 * n:352 * n + 352], start=(c == 0 and x is XH), stop=(c == 1 and x is XL))
                mm.then_inc(qk_done, 1)

            def scores(b, r):
                pe.wait_ge(qkb_ready, b + 1)
                if due(b):
                    pe.wait_ge(shifted, b)
                for h in range(HEADS):
                    p = 64 * (h % 2)
                    mm = pe.matmul(PS[0:KEYS, h % 2, (h // 2) * KEYS:(h // 2 + 1) * KEYS],
                                   qk_b[r][p:p + 64, h // 2, :], qk_b[r][p:p + 64, 6 + h // 2, :],
                                   start=True, stop=True)
                mm.then_inc(scores_done, 1)

            def values(b, r):
                pe.wait_ge(xb_ready, b + 1)
                if due(b):
                    pe.wait_ge(v_copied, b)
                for k in range(2):
                    for c in range(2):
                        for x in (xh_b, xl_b):
                            mm = pe.matmul(PS[0:KEYS, 2 + k, 0:384], x[r][:, c, :],
                                           Tqkv[:, c, 2 * INNER + 384 * k:2 * INNER + 384 * k + 384],
                                           start=(c == 0 and x is xh_b), stop=(c == 1 and x is xl_b))
                mm.then_inc(v_done, 1)

            def transposed(b, r):
                pe.wait_ge(exp_done, b + 1)
                if due(b):
                    pe.wait_ge(pT_copied, b)
                for h in range(HEADS):
                    tr = pe.transpose(PS[0:KEYS, 4 + h // 6, (h % 6) * KEYS:(h % 6 + 1) * KEYS], p_sb[r][:, h, :],
                                      ident[0:KEYS, 0:KEYS])
                tr.then_inc(pT_done, 1)

            def weighted(b, r):
                pe.wait_ge(pT_copied, b + 1)
                pe.wait_ge(v_copied, b + 1)
                if due(b):
                    pe.wait_ge(o_ready, b)
                for h in range(HEADS):
                    mm = pe.matmul(PS[0:KEYS, 6 + h // 6, (h % 6) * (DH + 1):(h % 6 + 1) * (DH + 1)], pT_sb[:, slot(h), :],
                                   v_b[r][:, h, :], start=True, stop=True)
                mm.then_inc(pv_done, 1)

            pe.wait_ge(qk_copied_a, 17)
            pe.wait_ge(qk_copied_d, 17)
            values(0, 0)
            pe.wait_ge(qk_copied_a, 18)
            pe.wait_ge(qk_copied_d, 18)
            scores(0, 0)
            values(1, 1)
            scores(1, 1)
            transposed(0, 0)
            weighted(0, 0)
            with pe.Fori(1, B // 2) as j:
                for k in range(2):
                    scores(2 * j + k, k)
                    transposed(2 * j + (k - 1), 1 - k)
                    values(2 * j + k, k)
                    weighted(2 * j + (k - 1), 1 - k)
            transposed(B - 1, 1)
            weighted(B - 1, 1)
            pe.wait_ge(o_ready, B)

            def turn_o(t):
                pe.wait_ge(masked2, t + 1)
                if due(t - 2):
                    pe.wait_ge(ol_done, t - 2)
                for c in range(HC):
                    tr = pe.transpose(PS[:, 2 * (t % 3) + c // 3, (c % 3) * 128:(c % 3) * 128 + ROWS[t]],
                                      O[0:ROWS[t], t, 128 * c:128 * c + 128], ident[0:ROWS[t], 0:ROWS[t]])
                tr.then_inc(oT_done, 1)

            def project(t):
                pe.wait_ge(oh_done, t + 1)
                pe.wait_ge(ol_done, t + 1)
                if due(t - 1):
                    pe.wait_ge(proj_added, t - 1)
                for c in range(HC):
                    for x in (OH, OL):
                        mm = pe.matmul(PS[0:ROWS[t], 6 + t % 2, 0:D], x[:, c, t * 128:t * 128 + ROWS[t]], Tout[:, c, :],
                                       start=(c == 0 and x is OH), stop=(c == HC - 1 and x is OL))
                mm.then_inc(proj_done, 1)

            sum_far(1)
            turn_o(0)
            turn_o(1)
            for t in range(TT):
                if t + 2 < TT:
                    turn_o(t + 2)
                project(t)
            pe.wait_ge(x6_ready, 1)
            for t in range(TT):
                if due(t - 3):
                    pe.wait_ge(xfl_done, t - 3)
                for c in range(2):
                    tr = pe.transpose(PS[:, t % 4, 128 * c:128 * c + ROWS[t]], X6[0:ROWS[t], t, 128 * c:128 * c + 128],
                                      ident[0:ROWS[t], 0:ROWS[t]])
                tr.then_inc(xfT_done, 1)
            pe.wait_ge(xfl_done, TT)
            pe.wait_ge(xfh_done, TT)
            pe.wait_ge(router_split, 3)
            for n in range(3):
                cs = slice(352 * n, 352 * n + 352)
                ps = PS[0:E, 5 + n, 0:352]
                pe.matmul(ps, router_h[:, 0, :], XFh[:, 0, cs], start=True, stop=False)
                pe.matmul(ps, router_h[:, 0, :], XFl[:, 0, cs], start=False, stop=False)
                pe.matmul(ps, router_l[:], XFh[:, 0, cs], start=False, stop=False)
                pe.matmul(ps, router_h[:, 1, :], XFh[:, 1, cs], start=False, stop=False)
                pe.matmul(ps, router_h[0:64, 1, :], XFl[0:64, 1, cs], start=False, stop=True).then_inc(lgT_done, 1)

            def turn_logits():
                pe.wait_ge(lgT_copied, 3)
                for t in range(TT):
                    tr = pe.transpose(PS[0:ROWS[t], 6, E * t:E * t + E], lgT[:, t * 128:t * 128 + ROWS[t]], ident[0:E, 0:E])
                tr.then_inc(logits_done, 1)

            def gate_up(e2, k):
                r, n = k // 3, k % 3
                cs, w = moe_columns(n), BLOCKS[n][2]
                if n == 0:
                    pe.wait_ge(w_hi, 6 * e2 + 3 * r + 3)
                    pe.wait_ge(w_lo, 6 * e2 + 3 * r + 3)
                for m in range(HC):
                    i = 6 * k + m
                    if isinstance(e2, int) and i == 2:
                        pe.wait_ge(lgT_copied, 1)
                    if not (isinstance(e2, int) and e2 == 0 and i < 3):
                        if due(36 * e2 + i - 2):
                            pe.wait_ge(hp_done, 36 * e2 + i - 2)
                    for side in range(2):
                        c0 = side * HID + 128 * m
                        ps = PS[:, 2 * (i % 3) + side, 0:w]
                        pe.matmul(ps, Wh[r][:, c0:c0 + 128], XFh[:, 0, cs], start=True, stop=False)
                        pe.matmul(ps, Wh[r][:, c0:c0 + 128], XFl[:, 0, cs], start=False, stop=False)
                        pe.matmul(ps, Wl[r][:, c0:c0 + 128], XFh[:, 0, cs], start=False, stop=False)
                        pe.matmul(ps, Wm[r][:, c0:c0 + 128], XFh[:, 1, cs], start=False, stop=False)
                        mm = pe.matmul(ps, Wm[r][0:64, c0:c0 + 128], XFl[0:64, 1, cs], start=False, stop=True)
                    mm.then_inc(gu_done, 1)

            def down(e2, k):
                r, n = k // 3, k % 3
                t0 = BLOCKS[n][0]
                if isinstance(e2, int) and k == 0:
                    pe.wait_ge(logits_read, 2)
                pe.wait_ge(hh_done, 36 * e2 + 6 * k + 6)
                pe.wait_ge(hl_done, 36 * e2 + 6 * k + 6)
                for i in range(3):
                    t = t0 + i
                    d = 3 * k + i
                    if not (isinstance(e2, int) and e2 == 0 and d < 2):
                        if due(18 * e2 + d - 1):
                            pe.wait_ge(down_added, 18 * e2 + d - 1)
                    cs = slice(128 * i, 128 * i + ROWS[t])
                    ps = PS[0:ROWS[t], 6 + d % 2, 0:2 * D]
                    for m in range(HC):
                        both = (ps, hH[k % 2][:, m, cs], Dhl[r][:, m, :])
                        rest = (ps[:, 0:D], hL[k % 2][:, m, cs], Dhl[r][:, m, 0:D])
                        for n_, mm_ in enumerate((both, rest) if m < HC - 1 else (rest, both)):
                            mm = pe.matmul(*mm_, start=(m == 0 and n_ == 0), stop=(m == HC - 1 and n_ == 1))
                    mm.then_inc(down_done, 1)

            def pe_pair(e2):
                gate_up(e2, 0)
                if isinstance(e2, int):
                    turn_logits()
                for k in range(1, 6):
                    gate_up(e2, k)
                    down(e2, k - 1)
                down(e2, 5)

            pe_pair(0)
            with pe.Fori(1, E // 2) as e2:
                pe_pair(e2)

        @block.vector
        def _(dve):
            count = [0]

            def link(*steps):
                for ins in steps:
                    count[0] += 1
                    ins.then_inc(dve_done, 1)
                dve.wait_ge(dve_done, count[0])

            link(dve.memset(ones[:], 1.0))
            dve.memset(asum[:], 1.0).then_inc(asum_set, 1)
            link(dve.memset(wabs[:], 0.0))
            dve.wait_ge(l_wqkv, 16)
            link(dve.tensor_reduce(wsum[0:HD, 0, :], wq_raw[:].rearrange("p c (a n) -> p (c a) n", n=48), AX.X, ALU.add,
                                   apply_absolute_value=True))
            dve.tensor_reduce(wabs[0:HD, 0:1], wsum[0:HD, 0, :], AX.X, ALU.add).then_inc(wsum_ready, 1)
            dve.wait_ge(l_wout, 16)
            link(dve.tensor_reduce(wsum[:, 1, 0:24], wo_raw[:].rearrange("p c (a n) -> p (c a) n", n=48), AX.X, ALU.add,
                                   apply_absolute_value=True))
            dve.tensor_reduce(wabs[:, 1:2], wsum[:, 1, 0:24], AX.X, ALU.add).then_inc(wsum_ready, 1)
            dve.wait_ge(tanh_done, 1)
            dve.tensor_scalar(gate[:, 1, :], gate[:, 0, :], 1.0, 0.5, ALU.add, ALU.mult).then_inc(gate_done, 1)
            dve.wait_ge(gate_done, 1)
            dve.tensor_scalar(gate[:, 2, :], gate[:, 1, :], -1.0, 1.0, ALU.mult, ALU.add).then_inc(gate_done, 1)
            dve.tensor_tensor(gate[:, 3, :], gate[:, 1, :], vecs[:, PG_B2, :], ALU.mult).then_inc(gate_done, 1)

            dve.wait_ge(wmean_ready, 1)
            dve.tensor_scalar(wscale[:, 0:1], PS[:, 7, 0:1], 1.0 / (3 * INNER * D), None, ALU.mult).then_inc(wmean_read, 1)
            dve.tensor_scalar(wscale[:, 1:2], PS[:, 7, 1:2], 1.0 / (INNER * D), None, ALU.mult).then_inc(wmean_read, 1)
            dve.wait_ge(wmean_read, 2)
            link(dve.tensor_scalar(wscale[:, 2:4], wscale[:, 0:2], 1e-8, 0.5, ALU.add, ALU.mult))
            link(dve.scalar_tensor_tensor(wscale[:, 4:5], wscale[:, 0:1], wscale[:, 0:1], wscale[:, 0:1],
                                          ALU.mult, ALU.bypass))
            link(dve.tensor_scalar(wscale[:, 4:5], wscale[:, 4:5], float(DH) ** -0.5, None, ALU.mult))
            link(dve.tensor_tensor(wscale[:, 5:6], wscale[:, 0:1], wscale[:, 1:2], ALU.mult))
            link(dve.tensor_scalar(wscale[:, 6:8], wscale[:, 2:4], -1.0, None, ALU.mult))
            for c in range(2):
                link(dve.tensor_scalar(neg1[0:HD, :], wq_raw[:, c, :], wscale[0:HD, 6:7], None, ALU.is_lt))
                link(dve.scalar_tensor_tensor(Tqkv[:, c, :], wq_raw[:, c, :], wscale[0:HD, 2:3], neg1[0:HD, :],
                                              ALU.is_gt, ALU.subtract))
            flat = wo_raw[:].rearrange("p c n -> p (c n)")
            link(dve.tensor_scalar(neg1[:, 0:HC * D], flat, wscale[:, 7:8], None, ALU.is_lt))
            link(dve.scalar_tensor_tensor(Tout[:].rearrange("p c n -> p (c n)"), flat, wscale[:, 3:4],
                                          neg1[:, 0:HC * D], ALU.is_gt, ALU.subtract))
            dve.wait_ge(l_dws, 16)

            def depthwise(n):
                for tap in range(9):
                    for m in range(2):
                        if due(18 * n + 2 * tap + m - 1):
                            dve.wait_ge(tap_done, 18 * n + 2 * tap + m - 1)
                        dst, src, w = tap_args(n, tap, m, 0, DVE_ROWS)
                        if tap == 0:
                            dve.tensor_scalar(dst, src, w, None, ALU.mult).then_inc(tap_done, 1)
                        else:
                            dve.scalar_tensor_tensor(dst, src, w, dst, ALU.mult, ALU.add).then_inc(tap_done, 1)

            for n, (f, h) in enumerate(DWS):
                dve.wait_ge(job_copied, job(source[f], h))
                for m in range(2):
                    if f == DW_F1:
                        dve.scalar_tensor_tensor(inside(padA, m, h), cols(loc, m, h), gate[:, 2, m:m + 1], cols(t1, m, h),
                                                 ALU.mult, ALU.add).then_inc(mix_done, 1)
                    if f == DW_F3:
                        dve.tensor_tensor(inside(padA, m, h), cols(loc, m, h), cols(t1, m, h), ALU.add)\
                           .then_inc(mix_done, 1)
                if f in (DW_F1, DW_F3):
                    dve.wait_ge(mix_done, 2 * h + (2 if f == DW_F1 else 6))
                if f in last_use:
                    dve.wait_ge(job_done, job(last_use[f], h))
                depthwise(n)
            dve.wait_ge(l_rows, 16)

            def row(n, k):
                return rows[:, n, :].unsqueeze(1).to_broadcast([128, k, D])

            for h in range(2):
                dve.wait_ge(job_done, 15 + h)
                for k in range(2):
                    t = 4 * h + 2 * k
                    link(dve.tensor_tensor(H[:, t:t + 2, :], PS[:, 2 * (2 + h) + k, 0:2 * D].rearrange("p (t d) -> p t d", t=2),
                                           row(F3_PWB, 2), ALU.add))
            n_ln = [0]

            def norm(src, dst, nt):
                for t in range(nt):
                    ins = dve.bn_stats(bn[:, t, :], src[:, t, 0:D])
                link(ins)
                for t in range(nt):
                    ins = dve.bn_aggr(mv[:, t, :], bn[:, t, :])
                link(ins)
                n_ln[0] += 1
                dve.tensor_scalar(rstd[:, 0, 0:nt], mv[:, 0:nt, 1], EPS, None, ALU.add).then_inc(var_ready, 1)
                dve.wait_ge(std_ready, n_ln[0])
                link(dve.reciprocal(rstd[:, 2, 0:nt], rstd[:, 1, 0:nt]))
                link(dve.tensor_tensor(rstd[:, 3, 0:nt], rstd[:, 2, 0:nt], rstd[:, 2, 0:nt], ALU.mult))
                link(dve.tensor_tensor(rstd[:, 3, 0:nt], rstd[:, 3, 0:nt], rstd[:, 0, 0:nt], ALU.mult))
                link(dve.tensor_scalar(rstd[:, 3, 0:nt], rstd[:, 3, 0:nt], -0.5, 1.5, ALU.mult, ALU.add))
                link(dve.tensor_tensor(rstd[:, 2, 0:nt], rstd[:, 2, 0:nt], rstd[:, 3, 0:nt], ALU.mult))
                for t in range(nt):
                    ins = dve.tensor_scalar(dst[:, t, 0:D], src[:, t, 0:D], mv[:, t, 0:1], rstd[:, 2, t:t + 1],
                                            ALU.subtract, ALU.mult)
                link(ins)

            link(dve.memset(rstd[:], 1.0))
            link(dve.memset(cnt[:], 0.0))
            link(dve.memset(signs[:], 0.0))
            link(dve.memset(top8[:], 0.0))
            norm(H, H, 8)
            link(dve.tensor_tensor(H[:, 0:8, :], H[:, 0:8, :], row(LN_G, 8), ALU.mult))
            link(dve.tensor_tensor(H[:, 0:8, :], H[:, 0:8, :], row(LN_B, 8), ALU.add))
            dve.wait_ge(l_cls, 32)
            norm(H, Z, TT)
            norm(Z, Z, TT)
            link(dve.tensor_tensor(Z[:], Z[:], row(GAMMA, TT), ALU.mult))
            dve.tensor_tensor(Z[:], Z[:], row(BETA, TT), ALU.add).then_inc(abs_in, 1)
            dve.wait_ge(l_small, 80)
            dve.tensor_copy(router_h[:], router[:]).then_inc(router_split, 1)
            dve.wait_ge(router_split, 1)
            dve.tensor_tensor(router_l[:], router[:, 0, :], router_h.bitcast(F32)[:, 0, :], ALU.subtract).then_inc(router_split, 1)
            dve.tensor_tensor(router_h[64:128, 1, :], router[64:128, 1, :], router_h.bitcast(F32)[64:128, 1, :],
                              ALU.subtract).then_inc(router_split, 1)
            for k, n in ((1, D), (2, INNER)):
                link(dve.tensor_scalar(qrank[:, k:k + 1], qrank[:, 0:1], float(n - 1), None, ALU.mult))
                link(dve.tensor_scalar(qrank[:, k:k + 1], qrank[:, k:k + 1], -1.0, float(n - 1), ALU.mult, ALU.add))
                link(dve.tensor_scalar(qrank[:, 2 + k:3 + k], qrank[:, k:k + 1], 4.0, None, ALU.subtract))
                link(dve.tensor_scalar(qrank[:, 4 + k:5 + k], qrank[:, 2 + k:3 + k], -1.0, n / 2, ALU.mult, ALU.add))

            def count_all(step, base, mag, n, level, tiles=TT):
                for t in range(tiles):
                    if t >= 2:
                        dve.wait_ge(step, base + t - 1)
                    dve.tensor_scalar(junk[0:ROWS[t], t % 2, 0:n], mag[0:ROWS[t], t, :], level[0:ROWS[t], t:t + 1],
                                      None, ALU.is_ge, ALU.add, accum_out=cnt[0:ROWS[t], t:t + 1]).then_inc(step, 1)
                dve.wait_ge(step, base + tiles)

            def select_by_bits(step, mag, n, k):
                dve.memset(thr[:], 0).then_inc(step, 1)
                dve.memset(bitf[:], float(1 << 30)).then_inc(step, 1)
                dve.wait_ge(step, 2)
                with dve.Fori(0, 31) as i:
                    base = 14 * i + 2
                    dve.tensor_copy(biti[:], bitf[:]).then_inc(step, 1)
                    dve.wait_ge(step, base + 1)
                    dve.tensor_tensor(cand[:], thr[:], biti[:], ALU.bitwise_or).then_inc(step, 1)
                    dve.wait_ge(step, base + 2)
                    count_all(step, base + 2, mag, n, cand.bitcast(F32))
                    dve.scalar_tensor_tensor(hitb[:], cnt[:], qrank[:, k:k + 1], bitf[:], ALU.is_gt, ALU.mult).then_inc(step, 1)
                    dve.wait_ge(step, base + 12)
                    dve.tensor_tensor(thr[:], thr[:], hitb[:], ALU.bitwise_or).then_inc(step, 1)
                    dve.tensor_scalar(bitf[:], bitf[:], 0.5, None, ALU.mult).then_inc(step, 1)
                    dve.wait_ge(step, base + 14)

            def select(which, mag, n, k, start, slope):
                link(dve.tensor_scalar(inv[:], asum[:], 1.0 / (n * n * slope), None, ALU.mult))
                dve.tensor_scalar(lev[:], asum[:], qrank[:, 0:1], start / n, ALU.mult, ALU.mult)\
                   .then_inc(lev_ready[which], 1)
                dve.wait_ge(lev_ready[which], 1)
                far_, step, moved, square, fit, weight, near, top = (work[:, i] for i in range(8))
                a = ACT_TILES[which]
                for p in range(PASSES):
                    e, before = err[:, p % 2], err[:, (p + 1) % 2]
                    if p < PASSES - 1:
                        count_all(count_done[which][p], 0, mag, n, lev, a)
                        dve.wait_ge(signs_done[which], (p + 1) * (TT - a))
                        link(dve.tensor_scalar(e[:, 0:a], cnt[:, 0:a], qrank[:, 2 + k:3 + k], None, ALU.subtract),
                             dve.tensor_scalar(e[:, a:TT], signs[:, a:TT], -0.5, qrank[:, 4 + k:5 + k], ALU.mult, ALU.add))
                    else:
                        count_all(count_done[which][p], 0, mag, n, lev)
                        link(dve.tensor_scalar(e, cnt[:], qrank[:, 2 + k:3 + k], None, ALU.subtract))
                        link(dve.tensor_tensor(square, e, e, ALU.mult))
                        link(dve.tensor_scalar(far_, square, 16.0, None, ALU.is_ge))
                        break
                    if p == 0:
                        link(dve.tensor_tensor(square, e, e, ALU.mult),
                             dve.tensor_tensor(near, e, inv[:], ALU.mult))
                        link(dve.scalar_tensor_tensor(step, square, 16.0, near, ALU.is_ge, ALU.mult))
                    else:
                        link(dve.tensor_tensor(square, e, e, ALU.mult),
                             dve.tensor_tensor(moved, before, e, ALU.subtract))
                        link(dve.scalar_tensor_tensor(near, square, 16.0, e, ALU.is_ge, ALU.mult),
                             dve.tensor_tensor(fit, step, moved, ALU.mult),
                             dve.tensor_tensor(weight, moved, moved, ALU.mult))
                        link(dve.scalar_tensor_tensor(fit, inv[:], 30.0, fit, ALU.mult, ALU.add),
                             dve.tensor_scalar(weight, weight, 30.0, None, ALU.add))
                        link(dve.reciprocal(weight, weight),
                             dve.tensor_tensor(top, fit, near, ALU.mult))
                        link(dve.tensor_tensor(inv[:], fit, weight, ALU.mult),
                             dve.tensor_tensor(step, top, weight, ALU.mult))
                    dve.tensor_tensor(lev[:], lev[:], step, ALU.add).then_inc(lev_ready[which], 1)
                    dve.wait_ge(lev_ready[which], p + 2)
                link(dve.memset(work[32:64, 0, 8:9], 0.0))
                link(dve.memset(work[64:128, 0, 8:9], 0.0))
                dve.tensor_reduce(far[:, 0:1], work[:, 0], AX.X, ALU.add).then_inc(far_ready, 1)
                for t in range(TT):
                    p = ROWS[t]
                    dve.scalar_tensor_tensor(below[0:p, t % 2, 0:n], mag[0:p, t, :], lev[0:p, t:t + 1], mag[0:p, t, :],
                                             ALU.is_lt, ALU.mult).then_inc(below_done, 1)
                    dve.wait_ge(below_done, 2 * TT * which + 2 * t + 1)
                    dve.max(top8[0:p, t, :], below[0:p, t % 2, 0:n]).then_inc(below_done, 1)
                    dve.wait_ge(below_done, 2 * TT * which + 2 * t + 2)
                link(dve.tensor_scalar(work[:, 1], cnt[:], qrank[:, k:k + 1], -1.0, ALU.subtract, ALU.mult))
                link(dve.tensor_tensor(pick[:], iota[:].unsqueeze(1).to_broadcast([128, TT, 8]),
                                       work[:, 1].unsqueeze(2).to_broadcast([128, TT, 8]), ALU.is_gt))
                link(dve.scalar_tensor_tensor(pick[:].rearrange("p t e -> p (t e)"), pick[:].rearrange("p t e -> p (t e)"),
                                              3e38, top8[:].rearrange("p t e -> p (t e)"), ALU.mult, ALU.add))
                link(dve.tensor_reduce(thr.bitcast(F32)[:], pick[:], AX.X, ALU.min))
                dve.wait_ge(far_summed, which + 1)
                link(dve.tensor_copy(far_i[0:1, :], PS[0:1, 0, 0:1]))
                left = dve.value_load(far_i[0:1, 0:1], min_val=0, max_val=NT)
                with dve.If(left > 0):
                    select_by_bits(bit_step[which], mag, n, k)

            dve.wait_ge(abs_done, TT)
            select(0, AB, D, 1, 1.43, 0.566)
            for t in range(TT):
                p = ROWS[t]
                dve.scalar_tensor_tensor(Z[0:p, t, :], AB[0:p, t, :], thr.bitcast(F32)[0:p, t:t + 1], Z[0:p, t, :],
                                         ALU.is_ge, ALU.mult).then_inc(masked1, 1)
            for n in range(6):
                g, c = n // 2, n % 2
                w = 512 if g < 2 else 32
                dve.wait_ge(xh_done, n + 1)
                dve.tensor_tensor(XL[:, c, 512 * g:512 * g + w], PS[0:HD, 3 * c + g, 0:w],
                                  XH.bitcast(F32)[:, c, 512 * g:512 * g + w], ALU.subtract).then_inc(xl_done, 1)
            link(dve.tensor_tensor(H[:], H[:], row(B_OUT, TT), ALU.add))
            for r in range(2):
                link(dve.memset(v_b[r][:, :, DH:DH + 1], 1.0))
            for q in range(1, 36, 2):
                dve.wait_ge(qk_done, q + 1)
                dve.tensor_copy(QKT[:, q // 3, 352 * (q % 3):352 * (q % 3) + 352], PS[:, (6 + q) % 8, 0:352])\
                   .then_inc(qk_copied_d, 1)
            dve.wait_ge(qk_copied_a, 18)
            dve.wait_ge(qk_copied_d, 18)

            def qk_copies(b, r):
                if due(b - 1):
                    dve.wait_ge(scores_done, b - 1)
                a, c = batch_cols(QKT, b)
                dve.tensor_copy(qk_b[r][:, :, 0:S], a)
                dve.tensor_copy(qk_b[r][:, :, S:KEYS].unsqueeze(3), c).then_inc(qkb_ready, 1)

            def shift(b):
                dve.wait_ge(scores_done, b + 1)
                sc = PS[0:KEYS, 0:2, 0:6 * KEYS].rearrange("p k (h n) -> p k h n", h=6)
                m = mx[:, 0, :].rearrange("p (k h) -> p k h", k=2)
                dve.tensor_reduce(m, sc, AX.X, ALU.max).then_inc(max_done, 1)
                dve.wait_ge(max_done, b + 1)
                if due(b):
                    dve.wait_ge(exp_done, b)
                dve.tensor_tensor(s_sb[:].rearrange("p (k h) n -> p k h n", k=2), sc,
                                  m.unsqueeze(3).to_broadcast([KEYS, 2, 6, KEYS]), ALU.subtract).then_inc(shifted, 1)

            def normalize(b, r):
                dve.wait_ge(pv_done, b + 1)
                pv = PS[0:KEYS, 6:8, 0:6 * (DH + 1)].rearrange("p k (h d) -> p k h d", h=6)
                rc = mx[:, 1, :].rearrange("p (k h) -> p k h", k=2)
                dve.reciprocal(rc.unsqueeze(3), pv[:, :, :, DH:DH + 1]).then_inc(recip_done, 1)
                dve.wait_ge(recip_done, b + 1)
                if not (isinstance(b, int) and b < 2):
                    if due(16 * b - 16 * r):
                        dve.wait_ge(o_stored[r], 16 * b - 16 * r)
                dve.tensor_tensor(o_b[r][:].rearrange("p (k h) d -> p k h d", k=2), pv[:, :, :, 0:DH],
                                  rc.unsqueeze(3).to_broadcast([KEYS, 2, 6, DH]), ALU.mult).then_inc(o_ready, 1)

            qk_copies(0, 0)
            qk_copies(1, 1)
            shift(0)
            qk_copies(2, 0)
            shift(1)
            normalize(0, 0)
            with dve.Fori(1, B // 2 - 1) as j:
                for k in range(2):
                    qk_copies(2 * j + k + 1, 1 - k)
                    shift(2 * j + k)
                    normalize(2 * j + (k - 1), 1 - k)
            qk_copies(B - 1, 1)
            shift(B - 2)
            normalize(B - 3, 1)
            shift(B - 1)
            normalize(B - 2, 0)
            normalize(B - 1, 1)

            dve.wait_ge(abs_done, 2 * TT)
            select(1, OA, INNER, 2, 1.74, 0.489)
            for t in range(TT):
                p = ROWS[t]
                dve.scalar_tensor_tensor(O[0:p, t, :], OA[0:p, t, :], thr.bitcast(F32)[0:p, t:t + 1], O[0:p, t, :],
                                         ALU.is_ge, ALU.mult).then_inc(masked2, 1)

            def rest_o(t):
                dve.wait_ge(oh_done, t + 1)
                cs = slice(t * 128, t * 128 + ROWS[t])
                dve.tensor_tensor(OL[:, :, cs].rearrange("p (k c) n -> p k c n", k=2),
                                  PS[:, 2 * (t % 3):2 * (t % 3) + 2, 0:384].rearrange("p k (c n) -> p k c n", c=3)[:, :, :, 0:ROWS[t]],
                                  OH.bitcast(F32)[:, :, cs].rearrange("p (k c) n -> p k c n", k=2),
                                  ALU.subtract).then_inc(ol_done, 1)

            def add_projection(t):
                p = ROWS[t]
                dve.wait_ge(proj_done, t + 1)
                dve.scalar_tensor_tensor(H[0:p, t, :], PS[0:p, 6 + t % 2, 0:D], wscale[0:p, 5:6], H[0:p, t, :],
                                         ALU.mult, ALU.add).then_inc(proj_added, 1)

            rest_o(0)
            for t in range(TT):
                if t + 1 < TT:
                    rest_o(t + 1)
                add_projection(t)
            dve.wait_ge(proj_added, TT)
            norm(H, X6, TT)
            dve.tensor_copy(X6[:, :, D:256], X6[:, :, 128:D]).then_inc(x6_ready, 1)
            for t in range(TT):
                dve.wait_ge(xfh_done, t + 1)
                cs = slice(t * 128, t * 128 + ROWS[t])
                dve.tensor_tensor(XFl[:, :, cs], PS[:, t % 4, 0:256].rearrange("p (c n) -> p c n", c=2)[:, :, 0:ROWS[t]],
                                  XFh.bitcast(F32)[:, :, cs], ALU.subtract).then_inc(xfl_done, 1)
            def hidden(e2, k):
                w = BLOCKS[k % 3][2]
                for m in range(HC + 1):
                    if m < HC:
                        i = 6 * k + m
                        dve.wait_ge(silu_done, 36 * e2 + i + 1)
                        if not (isinstance(e2, int) and e2 == 0 and i < 2):
                            if due(36 * e2 + i - 1):
                                dve.wait_ge(hl_done, 36 * e2 + i - 1)
                        dve.tensor_tensor(hp[m % 2][:, 0:w], sg[m % 2][:, 0:w], PS[:, 2 * (i % 3) + 1, 0:w],
                                          ALU.mult).then_inc(hp_done, 1)
                    if m > 0:
                        i = 6 * k + m - 1
                        dve.wait_ge(hh_done, 36 * e2 + i + 1)
                        dve.tensor_tensor(hL[k % 2][:, m - 1, 0:w], hp[(m - 1) % 2][:, 0:w],
                                          hH[k % 2].bitcast(F32)[:, m - 1, 0:w], ALU.subtract).then_inc(hl_done, 1)

            def add_down(e2, k):
                n = k % 3
                for i in range(3):
                    t = BLOCKS[n][0] + i
                    d = 3 * k + i
                    p = ROWS[t]
                    dve.wait_ge(down_done, 18 * e2 + d + 1)
                    if due(18 * e2 + d - 8 if d >= 8 or not isinstance(e2, int) else 0):
                        dve.wait_ge(down_added, 18 * e2 + d - 8 if d >= 8 or not isinstance(e2, int) else 0)
                    w = wE[0:p, t, k // 3:k // 3 + 1] if isinstance(e2, int) else wE[0:p, t, bass.ts(e2 * 2 + k // 3, 1)]
                    if isinstance(e2, int):
                        w = wE[0:p, t, 2 * e2 + k // 3:2 * e2 + k // 3 + 1]
                    dve.scalar_tensor_tensor(H[0:p, t, :], PS[0:p, 6 + d % 2, 0:D], w, H[0:p, t, :], ALU.mult,
                                             ALU.add).then_inc(half_added, 1)
                    dve.wait_ge(half_added, 18 * e2 + d + 1)
                    dve.scalar_tensor_tensor(H[0:p, t, :], PS[0:p, 6 + d % 2, D:2 * D], w, H[0:p, t, :], ALU.mult,
                                             ALU.add).then_inc(down_added, 1)

            def route():
                link(dve.memset(logit[:, 8, :], 0.0))
                dve.wait_ge(logits_done, 1)
                dve.tensor_copy(logit[:, 0:8, :], PS[:, 6, 0:8 * E].rearrange("p (t e) -> p t e", t=8)).then_inc(logits_read, 1)
                dve.tensor_copy(logit[0:32, 8, :], PS[0:32, 6, 8 * E:9 * E]).then_inc(logits_read, 1)
                dve.wait_ge(logits_read, 2)
                for t in range(TT):
                    ins = dve.max(top8[:, t, :], logit[:, t, :])
                link(ins)
                for t in range(TT):
                    ins = dve.max_index(idx8[:, t, :], top8[:, t, :], logit[:, t, :])
                link(ins)
                dve.tensor_tensor(topw[:, 0, :], top8[:, :, 1], top8[:, :, 0], ALU.subtract).then_inc(diff_ready, 1)
                link(dve.tensor_copy(idxf[:], idx8[:, :, 0:2]))
                dve.wait_ge(exp2_done, 1)
                link(dve.tensor_scalar(topw[:, 2, :], topw[:, 1, :], 1.0, None, ALU.add))
                link(dve.reciprocal(topw[:, 2, :], topw[:, 2, :]))
                link(dve.tensor_tensor(topw[:, 3, :], topw[:, 1, :], topw[:, 2, :], ALU.mult))
                for t in range(TT):
                    for k in range(2):
                        ins = dve.tensor_scalar(wsel[:, k, t, :], iota[:], idxf[:, t, k:k + 1], topw[:, 2 + k, t:t + 1],
                                                ALU.is_equal, ALU.mult)
                link(ins)
                link(dve.tensor_tensor(wE[:], wsel[:, 0], wsel[:, 1], ALU.add))

            def dve_pair(e2):
                hidden(e2, 0)
                if isinstance(e2, int):
                    route()
                for k in range(1, 6):
                    hidden(e2, k)
                    add_down(e2, k - 1)
                add_down(e2, 5)

            dve_pair(0)
            with dve.Fori(1, E // 2) as e2:
                dve_pair(e2)


def haar_matrix(np):
    one = np.array([[1.0, 1.0], [1.0, -1.0]])
    k = np.arange(256)
    m = np.ones((256, 256))
    for level in range(4):
        band = k >> 2 * (3 - level) & 3
        y, x = k // 16 >> level & 1, k % 16 >> level & 1
        m *= one[band >> 1][:, x] * one[band & 1][:, y]
    return m / 16


def kernel(**inputs):
    import numpy as np
    import concourse.bacc as bacc
    from concourse.bass_utils import run_bass_kernel_spmd

    a = {k: np.asarray(v) for k, v in inputs.items()}
    tok = {k[7:]: v for k, v in a.items() if k.startswith("L0_tok_")}
    c = np.ascontiguousarray
    dws = np.stack([tok[k].reshape(D, 9) for k in ("pl_dw", "pg_dw", "f1_dw", "f2_dw", "f3_dw")], 1)
    pws = np.stack([tok[k].reshape(D, D).T for k in ("pl_pw", "pg_pw", "pg_w2", "f1_pw", "f2_pw", "f3_pw")])
    vecs = np.stack([tok[k].reshape(D) for k in
                     ("pl_b", "pl_pwb", "pg_b1", "pg_pwb", "pg_b2", "alpha", "f1_pwb", "f2_pwb")])
    rows = np.stack([tok["f3_pwb"], tok["ln_g"], tok["ln_b"], a["L0_attn_gamma"], a["L0_attn_beta"],
                     a["L0_attn_b_out"], a["cls_tok"].reshape(D), tok["cls"].reshape(D)])
    wgu = np.concatenate([a["L0_ffn_Wg"].transpose(0, 2, 1), a["L0_ffn_Wu"].transpose(0, 2, 1)], 2)
    arrays = {
        "patches": c(a["x"].reshape(2, BH, C, G, PATCH, G, PATCH).transpose(2, 4, 6, 0, 3, 5, 1)
                     .reshape(KC, 128, NP_).transpose(1, 0, 2)),
        "plw": c(tok["pl_w"].reshape(D, KC, 128).transpose(2, 1, 0)),
        "w1t": c(tok["pg_w1"].reshape(D, 2, 128, C).transpose(2, 1, 3, 0).reshape(128, 2, C * D)),
        "haar": c(haar_matrix(np).astype(np.float32).reshape(2, 128, 256).transpose(1, 0, 2)),
        "ident": np.eye(128, dtype=np.float32),
        "vecs": c(vecs.reshape(8, 2, HD).transpose(2, 0, 1)),
        "dws": c(dws.reshape(2, HD, 5, 9).transpose(1, 0, 2, 3)),
        "pws": c(pws.reshape(6, 2, HD, D).transpose(2, 0, 1, 3)),
        "rows": c(rows),
        "sparsity": c(a["L0_attn_sparsity"].reshape(1)),
        "wqkv": c(a["L0_attn_w_qkv"].T.reshape(2, HD, 3 * INNER).transpose(1, 0, 2)),
        "wout": c(a["L0_attn_w_out"].T.reshape(HC, 128, D).transpose(1, 0, 2)),
        "router": c(a["L0_ffn_router_w"].T),
        "iota": c(np.tile(np.arange(E, dtype=np.float32), (128, 1))),
        "wgu": c(wgu),
        "wd": c(a["L0_ffn_Wd"].transpose(0, 2, 1).reshape(E, HC, 128, D).transpose(0, 2, 1, 3)),
    }
    nc = bacc.Bacc("TRN2", target_bir_lowering=False, num_devices=1)
    args = [nc.dram_tensor(k, v.shape, mybir.dt.from_np(v.dtype), kind="ExternalInput").ap() for k, v in arrays.items()]
    args.append(nc.dram_tensor("out", (B, KEYS, D), F32, kind="ExternalOutput").ap())
    build_tower(nc, *args)
    r = run_bass_kernel_spmd(nc, [arrays], core_ids=[0])
    return r.results[0]["out"]
```

```python
from contextlib import ExitStack

import concourse.bass as bass
from concourse import mybir

F32 = mybir.dt.float32
F32R = mybir.dt.float32r
BF16 = mybir.dt.bfloat16
I32 = mybir.dt.int32
U32 = mybir.dt.uint32
ALU = mybir.AluOpType
ACT = mybir.ActivationFunctionType
AX = mybir.AxisListType

B, C, IMG, PATCH = 16, 3, 128, 16
G = IMG // PATCH
S = G * G
D = 192
HD = D // 2
NP_ = B * S
NT = NP_ + 2 * B
BH = B // 2
HALF = NP_ // 2
KC = C * PATCH * PATCH // 128
HEADS, DH = 12, 64
INNER = HEADS * DH
KEYS = S + 2
TT = 9
E, HID = 8, 4 * D
HC = HID // 128
EPS = 1e-5
PASSES = 5
ROWS = [128] * 8 + [NT - NP_]
SEARCHES = [(0, TT, 7), (0, 4, 1), (4, TT, 7)]
EARLY = 11
DVE_ROWS = [6] * 6 + [5] * 4
FREE0, FREE1 = 16512, 229344

PL_B, PL_PWB, PG_B1, PG_PWB, PG_B2, ALPHA, F1_PWB, F2_PWB = range(8)
F3_PWB, LN_G, LN_B, GAMMA, BETA, B_OUT, CLS0, CLS1 = range(8)
DW_PL, DW_PG, DW_F1, DW_F2, DW_F3 = range(5)
PW_PL, PW_PG, PW_G2, PW_F1, PW_F2, PW_F3 = range(6)

V_TILES = [0, 1, 2, 3, 8, 4, 5, 6, 7]
V_FIRST = 5

assert EARLY + PASSES == B

BLOCKS = [(0, 3, 384), (3, 3, 384), (6, 3, NT - 768)]


def build_tower(nc, patches, plw, w1t, haar, ident_d, vecs_d, dws_d, pws_d, rows_d, sparsity, wqkv_d, wout_d,
                router_d, iota_d, wgu_d, wd_d, out):
    ctx = ExitStack()
    with ctx:
        o_scr = nc.dram_tensor("o_scratch", (NT, INNER), F32, kind="Internal").ap()
        v_scr = nc.dram_tensor("v_scratch", (NT, HEADS * (DH + 1)), F32, kind="Internal").ap()

        plan = {}

        def place(zone, name, shape, dt):
            n = 1
            for k in shape[1:]:
                n *= k
            n *= 2 if dt == BF16 else 4
            at = (plan[zone] + 31) // 32 * 32
            plan[zone] = at + n
            assert plan[zone] <= FREE1, (name, plan[zone])
            return nc.alloc_sbuf_tensor_at(name, list(shape), dt, offset=at)

        def sem(name):
            return ctx.enter_context(nc.semaphore(name))

        def due(v):
            return not (isinstance(v, int) and v <= 0)

        plan["kept"] = FREE0
        ident = place("kept", "ident", [128, 128], F32)
        ones = place("kept", "ones", [128, 128], F32)
        rows = place("kept", "rows", [128, 6, D], F32)
        H = place("kept", "H", [128, TT, D], F32)
        vecs = place("kept", "vecs", [HD, 8, 2], F32)
        dws = place("kept", "dws", [HD, 2, 5, 9], F32)
        router = place("kept", "router", [128, 2, E], F32)
        router_h = place("kept", "router_h", [128, 2, E], F32R)
        router_l = place("kept", "router_l", [128, E], F32R)
        below = place("kept", "below", [128, 2, INNER], F32)
        iota = place("kept", "iota", [128, E], F32)
        gate = place("kept", "gate", [HD, 4, 2], F32)
        bn = place("kept", "bn", [128, TT, 6], F32)
        mv = place("kept", "mv", [128, TT, 2], F32)
        rstd = place("kept", "rstd", [128, 5, TT], F32)
        wsum = place("kept", "wsum", [128, 2, 96], F32)
        wabs = place("kept", "wabs", [128, 2], F32)
        wscale = place("kept", "wscale", [128, 8], F32)
        qrank = place("kept", "qrank", [128, 7], F32)
        thr = place("kept", "thr", [128, TT], I32)
        cand = place("kept", "cand", [128, TT], I32)
        biti = place("kept", "biti", [128, TT], I32)
        bitf = place("kept", "bitf", [128, TT], F32)
        hitb = place("kept", "hitb", [128, TT], I32)
        cnt = place("kept", "cnt", [128, TT], F32)
        asum = place("kept", "asum", [128, TT], F32)
        lev = place("kept", "lev", [128, TT], F32)
        inv = place("kept", "inv", [128, TT], F32)
        err = place("kept", "err", [128, 2, TT], F32)
        work = place("kept", "work", [128, 8, TT], F32)
        far = place("kept", "far", [128, 1], F32)
        far_i = place("kept", "far_i", [128, 1], I32)
        pick = place("kept", "pick", [128, TT, 8], F32)
        junk = place("kept", "junk", [128, 2, INNER], BF16)
        act_junk = place("kept", "act_junk", [128, 2, INNER], BF16)
        signs = place("kept", "signs", [128, TT], F32)
        logit = place("kept", "logit", [128, TT, E], F32)
        top8 = place("kept", "top8", [128, TT, 8], F32)
        idx8 = place("kept", "idx8", [128, TT, 8], U32)
        idxf = place("kept", "idxf", [128, TT, 2], F32)
        topw = place("kept", "topw", [128, 4, TT], F32)
        wsel = place("kept", "wsel", [128, 2, TT, E], F32)
        wE = place("kept", "wE", [128, TT, E], F32)
        Tqkv = place("kept", "Tqkv", [128, 2, 3 * INNER], F32R)
        Tout = place("kept", "Tout", [128, HC, D], F32R)
        W0 = plan["kept"]

        plan["tok"] = W0
        patch = place("tok", "patch", [128, KC, NP_], F32)
        plw_sb = place("tok", "plw_sb", [128, KC, D], F32)
        wf_sb = place("tok", "wf_sb", [128, KC, D], F32)
        w1_sb = place("tok", "w1_sb", [128, 2, C * D], F32)
        haar_sb = place("tok", "haar_sb", [128, 2, 256], F32)
        padA = place("tok", "padA", [HD, 2, 2, G + 2, G + 2, BH], F32)
        padB = place("tok", "padB", [HD, 2, 2, G + 2, G + 2, BH], F32)
        dwA = place("tok", "dwA", [HD, 2, NP_], F32)
        dwB = place("tok", "dwB", [HD, 2, NP_], F32)
        loc = place("tok", "loc", [HD, 2, NP_], F32)
        g2 = place("tok", "g2", [HD, 2, NP_], F32)
        t1 = place("tok", "t1", [HD, 2, NP_], F32)
        pws = place("tok", "pws", [HD, 6, 2, D], F32)
        products = place("tok", "products", [HD, 8, 2, (G - min(DVE_ROWS)) * G * BH], F32)
        wq_raw = place("tok", "wq_raw", [128, 2, 3 * INNER], F32)
        wo_raw = place("tok", "wo_raw", [128, HC, D], F32)
        neg1 = place("tok", "neg1", [128, 3 * INNER], BF16)

        plan["att"] = W0
        Z = place("att", "Z", [128, TT, 256], F32)
        AB = place("att", "AB", [128, TT, D], F32)
        XH = place("att", "XH", [128, 2, NT], F32R)
        XL = place("att", "XL", [128, NT], F32R)
        QKT = place("att", "QKT", [128, 12, NT], F32)
        qk_b = [place("att", f"qk_b{r}", [128, 12, KEYS], F32) for r in range(2)]
        v_b = [place("att", f"v_b{r}", [KEYS, HEADS, DH + 1], F32) for r in range(2)]
        s_sb = place("att", "s_sb", [KEYS, HEADS, KEYS], F32)
        p_sb = [place("att", f"p_sb{r}", [KEYS, HEADS, KEYS], F32) for r in range(2)]
        pT_sb = [place("att", f"pT_sb{r}", [KEYS, HEADS, KEYS], F32) for r in range(2)]
        o_b = [place("att", f"o_b{r}", [KEYS, HEADS, DH], F32) for r in range(2)]
        mx = place("att", "mx", [KEYS, 4, HEADS], F32)
        plan["values"] = plan["att"]
        vt = place("values", "vt", [128, TT, HEADS, DH + 1], F32)
        O = place("att", "O", [128, TT, INNER], F32)
        plan["out"] = W0
        OA = place("out", "OA", [128, TT, INNER], F32)
        OH = place("out", "OH", [128, HC, NT], F32R)
        OL = place("out", "OL", [128, HC, NT], F32R)
        assert plan["out"] <= plan["att"] - TT * INNER * 4
        O_AT = plan["att"] - TT * INNER * 4
        plan["moe"] = W0
        X6 = place("moe", "X6", [128, TT, 256], F32)
        XFh = place("moe", "XFh", [128, 2, NT], F32R)
        XFl = place("moe", "XFl", [128, 2, NT], F32R)
        hH = [place("moe", f"hH{r}", [128, HC, 384], F32R) for r in range(2)]
        hL = [place("moe", f"hL{r}", [128, HC, 384], F32R) for r in range(2)]
        sg = [place("moe", f"sg{r}", [128, 384], F32) for r in range(2)]
        hp = [place("moe", f"hp{r}", [128, 384], F32) for r in range(2)]
        lgT = place("moe", "lgT", [E, NT], F32)
        assert plan["moe"] <= plan["out"]
        plan["raw"] = plan["att"]
        raw_a = place("raw", "raw_a", [128, 2 * HID], F32)
        raw_d = place("raw", "raw_d", [128, HC, D], F32)
        plan["w0"] = plan["out"]
        raw_b = place("w0", "raw_b", [128, 2 * HID], F32)
        plan["w1"] = O_AT
        Wh = [place(f"w{r}", f"Wh{r}", [128, 2 * HID], F32R) for r in range(2)]
        Wl = [place(f"w{r}", f"Wl{r}", [128, 2 * HID], F32R) for r in range(2)]
        Wm = [place(f"w{r}", f"Wm{r}", [128, 2 * HID], F32R) for r in range(2)]
        Dhl = [place(f"w{r}", f"Dhl{r}", [128, HC, 2 * D], F32R) for r in range(2)]
        assert plan["w0"] <= O_AT and plan["w1"] <= plan["att"]

        PS = ctx.enter_context(nc.psum_tensor("PS", [128, 8, 512], F32))

        l_fold, l_plw, l_vecs, l_dws, l_pws = (sem(n) for n in ("l_fold", "l_plw", "l_vecs", "l_dws", "l_pws"))
        l_patch = [[sem(f"l_patch{h}{k}") for k in range(KC // 2)] for h in range(2)]
        l_wqkv, l_wout, l_ident, l_rows, l_cls, l_small = (
            sem(n) for n in ("l_wqkv", "l_wout", "l_ident", "l_rows", "l_cls", "l_small"))
        l_o = [sem(f"l_o{t}") for t in range(TT)]
        l_exp = sem("l_exp")
        pads_zero, h8_zero = sem("pads_zero"), sem("h8_zero")
        fold_done, fold_copied = sem("fold_done"), sem("fold_copied")
        tanh_done, gate_done = sem("tanh_done"), sem("gate_done")
        job_done, job_copied = sem("job_done"), sem("job_copied")
        tap_done, product_done, sum_done, mix_done = (sem(n) for n in ("tap_done", "product_done", "sum_done", "mix_done"))
        wsum_ready, wmean_ready, wmean_read = sem("wsum_ready"), sem("wmean_ready"), sem("wmean_read")
        dve_done = sem("dve_done")
        var_ready, std_ready = sem("var_ready"), sem("std_ready")
        abs_in, abs_done = sem("abs_in"), sem("abs_done")
        asum_set, far_ready, far_summed, below_done = (sem(n) for n in ("asum_set", "far_ready", "far_summed", "below_done"))
        lev_ready = [sem(f"lev_ready{g}") for g in range(3)]
        signs_done = [sem(f"signs_done{g}") for g in range(3)]
        count_done = [[sem(f"count_done{g}{p}") for p in range(PASSES)] for g in range(3)]
        bit_step = [sem("bit_step0"), sem("bit_step1")]
        masked1, xT_done, xh_done, xl_done = (sem(n) for n in ("masked1", "xT_done", "xh_done", "xl_done"))
        ones_set = sem("ones_set")
        qkv_done, qkv_copied_a, qkv_copied_d = sem("qkv_done"), sem("qkv_copied_a"), sem("qkv_copied_d")
        v_stored = [sem("v_stored0"), sem("v_stored1")]
        qkb_ready = sem("qkb_ready")
        v_loaded = [sem("v_loaded0"), sem("v_loaded1")]
        scores_done, pT_done, pv_done = (sem(n) for n in ("scores_done", "pT_done", "pv_done"))
        max_done, shifted, exp_done = sem("max_done"), sem("shifted"), sem("exp_done")
        pT_copied, recip_done, o_ready = (sem(n) for n in ("pT_copied", "recip_done", "o_ready"))
        o_stored = [sem("o_stored0"), sem("o_stored1")]
        masked2, oT_done, oh_done, ol_done = (sem(n) for n in ("masked2", "oT_done", "oh_done", "ol_done"))
        proj_done, proj_added = sem("proj_done"), sem("proj_added")
        x6_ready, xfT_done, xfh_done, xfl_done = (sem(n) for n in ("x6_ready", "xfT_done", "xfh_done", "xfl_done"))
        logits_done, diff_ready, exp2_done = sem("logits_done"), sem("diff_ready"), sem("exp2_done")
        router_split, lgT_done, lgT_copied, logits_read = (
            sem(n) for n in ("router_split", "lgT_done", "lgT_copied", "logits_read"))
        half_added = sem("half_added")
        w_hi, w_lo = sem("w_hi"), sem("w_lo")
        gu_done, silu_done, hp_done, hh_done, hl_done = (
            sem(n) for n in ("gu_done", "silu_done", "hp_done", "hh_done", "hl_done"))
        down_done, down_added = sem("down_done"), sem("down_added")
        stored = sem("stored")

        block = ctx.enter_context(nc.Block())

        JOBS = [("loc", 0), ("loc", 1), ("g", 0), (PW_PL, 0), ("g", 1), (PW_PG, 0), (PW_G2, 0), (PW_PL, 1), (PW_PG, 1),
                (PW_G2, 1), (PW_F1, 0), (PW_F1, 1), (PW_F2, 0), (PW_F2, 1), (PW_F3, 0), (PW_F3, 1)]
        DWS = [(DW_PL, 0), (DW_PL, 1), (DW_PG, 0), (DW_PG, 1), (DW_F1, 0), (DW_F1, 1), (DW_F2, 0), (DW_F2, 1), (DW_F3, 0),
               (DW_F3, 1)]
        dw_pad = {DW_PL: padA, DW_PG: padB, DW_F1: padA, DW_F2: padB, DW_F3: padA}
        dw_out = {DW_PL: dwA, DW_PG: dwB, DW_F1: dwA, DW_F2: dwB, DW_F3: dwA}
        pw_of = {PW_PL: DW_PL, PW_PG: DW_PG, PW_F1: DW_F1, PW_F2: DW_F2, PW_F3: DW_F3}
        source = {DW_PL: "loc", DW_PG: "g", DW_F1: PW_G2, DW_F2: PW_F1, DW_F3: PW_F2}
        last_use = {DW_F1: PW_PL, DW_F2: PW_PG, DW_F3: PW_F1}

        def window(pad, m, h, dy, dx, y0=0, y1=G):
            return pad[:, m, h, dy + y0:dy + y1, dx:dx + G, :].rearrange("p y x b -> p y (x b)")

        def inside(pad, m, h):
            return window(pad, m, h, 1, 1)

        def cols(t, m, h):
            return t[:, m, h * HALF:(h + 1) * HALF].rearrange("p (y n) -> p y n", y=G)

        def job(kind, h):
            return JOBS.index((kind, h)) + 1

        def tap_args(n, tap, m, y0, y1):
            f, h = DWS[n]
            return (cols(dw_out[f], m, h)[:, y0:y1, :], window(dw_pad[f], m, h, tap // 3, tap % 3, y0, y1),
                    dws[:, m, f, tap:tap + 1])

        def slot(h):
            return h % 2 * (HEADS // 2) + h // 2

        def patch_rows(b):
            return bass.DynSlice(b + (b // BH) * (HALF - BH), S, step=BH)

        def batch_cols(t, b):
            return t[:, :, patch_rows(b)], t[:, :, NP_:NT].rearrange("p c (k b) -> p c k b", k=2)[:, :, :, bass.ts(b, 1)]

        def qkv_bank(i):
            return (6 + i) % 8

        def moe_columns(n):
            t0, nt, w = BLOCKS[n]
            return slice(t0 * 128, t0 * 128 + w)

        @block.sync
        def _(sp):
            sp.dma_start(plw_sb[:], plw).then_inc(l_plw, 16)
            for h in range(2):
                if h == 1:
                    sp.dma_start(haar_sb[:], haar).then_inc(l_fold, 16)
                    sp.dma_start(w1_sb[:], w1t).then_inc(l_fold, 16)
                for k in range(0, KC, 2):
                    c = slice(h * HALF, (h + 1) * HALF)
                    sp.dma_start(patch[:, k:k + 2, c], patches[:, k:k + 2, c]).then_inc(l_patch[h][k // 2], 16)

            def store_o(b, r):
                sp.wait_ge(o_ready, b + 1)
                sp.dma_start(o_scr[patch_rows(b), :], o_b[r][0:S].rearrange("p h d -> p (h d)")).then_inc(o_stored[r], 16)
                sp.dma_start(o_scr[NP_:NT, :].rearrange("(k b) n -> k b n", k=2)[:, bass.ts(b, 1), :],
                             o_b[r][S:KEYS].rearrange("p h d -> p (h d)").unsqueeze(1)).then_inc(o_stored[r], 16)

            def load_v(b, r):
                if due(b - 1):
                    sp.wait_ge(pv_done, b - 1)
                sp.dma_start(v_b[r][0:S].rearrange("p h d -> p (h d)"), v_scr[patch_rows(b), :]).then_inc(v_loaded[r], 16)
                sp.dma_start(v_b[r][S:KEYS].rearrange("p h d -> p (h d)").unsqueeze(1),
                             v_scr[NP_:NT, :].rearrange("(k b) n -> k b n", k=2)[:, bass.ts(b, 1), :]).then_inc(v_loaded[r], 16)

            for i, t in enumerate(V_TILES):
                sp.wait_ge(qkv_copied_a, i + 1)
                sp.wait_ge(qkv_copied_d, i + 1)
                sp.dma_start(v_scr[t * 128:t * 128 + ROWS[t], :], vt[0:ROWS[t], t].rearrange("p h d -> p (h d)"))\
                  .then_inc(v_stored[i // V_FIRST], 16)
            sp.wait_ge(v_stored[0], 16 * V_FIRST)
            load_v(0, 0)
            load_v(1, 1)
            sp.wait_ge(v_stored[1], 16 * (TT - V_FIRST))
            for half in range(2):
                with sp.Fori(half * (BH // 2), (half + 1) * (BH // 2) - half) as j:
                    for r in range(2):
                        store_o(2 * j + r, r)
                        load_v(2 * j + 2 + r, r)
                if half:
                    store_o(B - 2, 0)
                    store_o(B - 1, 1)
                sp.wait_ge(o_stored[0], 16 * BH * (half + 1))
                sp.wait_ge(o_stored[1], 16 * BH * (half + 1))
                for t in range(4 * half, 4 * half + 4 + half):
                    sp.dma_start(O[0:ROWS[t], t, :], o_scr[t * 128:t * 128 + ROWS[t], :]).then_inc(l_o[t], 16)

            def load_expert(e):
                if due(3 * e):
                    sp.wait_ge(w_lo, 3 * e)
                sp.dma_start(raw_a[:], wgu_d[bass.ts(e, 1), 0:128, :].rearrange("e p n -> (e p) n")).then_inc(l_exp, 16)
                for half in range(2):
                    sp.dma_start(raw_b[64 * half:64 * half + 64, :],
                                 wgu_d[bass.ts(e, 1), 128:D, :].rearrange("e p n -> (e p) n")).then_inc(l_exp, 16)
                sp.dma_start(raw_d[:], wd_d[bass.ts(e, 1)].rearrange("e p c n -> (e p) c n")).then_inc(l_exp, 16)

            load_expert(0)
            with sp.Fori(1, E) as e:
                load_expert(e)
            for t in range(TT - 1):
                sp.wait_ge(down_added, (E - 1) * TT + t + 1)
                first = 2 + t % 4 * (128 // BH)
                sp.dma_start(out[t // 4 * BH:(t // 4 + 1) * BH, first:first + 128 // BH, :].rearrange("b s d -> s b d"),
                             H[:, t, :]).then_inc(stored, 16)
            sp.wait_ge(down_added, E * TT)
            sp.dma_start(out[:, 0:2, :].rearrange("b k d -> k b d"), H[0:2 * B, 8, :]).then_inc(stored, 16)
            sp.wait_ge(stored, TT * 16)

        @block.gpsimd
        def _(pool):
            pool.dma_start(ident[:], ident_d).then_inc(l_ident, 16)
            pool.memset(padA[:], 0.0).then_inc(pads_zero, 1)
            pool.memset(padB[:], 0.0).then_inc(pads_zero, 1)
            pool.memset(H[:, 8, :], 0.0).then_inc(h8_zero, 1)
            pool.dma_start(rows[:], rows_d[0:6, :].partition_broadcast(128)).then_inc(l_rows, 16)
            pool.dma_start(qrank[:, 0:1], sparsity.partition_broadcast(128)).then_inc(l_small, 16)
            pool.dma_start(iota[:], iota_d).then_inc(l_small, 16)
            pool.dma_start(router[:, 0, :], router_d[0:128, :]).then_inc(l_small, 16)
            for half in range(2):
                pool.dma_start(router[64 * half:64 * half + 64, 1, :], router_d[128:D, :]).then_inc(l_small, 16)
            pool.wait_ge(h8_zero, 1)
            for k in range(2):
                pool.dma_start(H[16 * k:16 * k + 16, 8, :], rows_d[CLS0 + k, :].partition_broadcast(16)).then_inc(l_cls, 16)

            for n in range(10):
                for tap in range(1, 9):
                    pool.wait_ge(product_done, 18 * n + 2 * tap + 2)
                    if due(8 * n + tap - 1):
                        pool.wait_ge(sum_done, 8 * n + tap - 1)
                    f, h = DWS[n]
                    n_cols = (G - DVE_ROWS[n]) * G * BH
                    dst = dw_out[f][:, :, (h + 1) * HALF - n_cols:(h + 1) * HALF]
                    pool.tensor_tensor(dst, dst, products[:, tap - 1, :, 0:n_cols], ALU.add).then_inc(sum_done, 1)

            def split(e, r):
                if not isinstance(e, int) or e >= 2:
                    pool.wait_ge(down_done, TT * (e - 1))
                if isinstance(e, int) and e == 1:
                    pool.wait_ge(oT_done, TT)
                if not isinstance(e, int) or e >= 1:
                    pool.wait_ge(l_exp, 64 * (e + 1))
                    pool.tensor_tensor(Wh[r][:], raw_a[:], ones[:, 0:1].to_broadcast([128, 2 * HID]), ALU.mult).then_inc(w_hi, 1)
                    pool.tensor_tensor(Wm[r][:], raw_b[:], ones[:, 0:1].to_broadcast([128, 2 * HID]), ALU.mult).then_inc(w_hi, 1)
                    pool.tensor_tensor(Dhl[r][:, :, 0:D], raw_d[:], ones[:, 0:1].unsqueeze(2).to_broadcast([128, HC, D]), ALU.mult).then_inc(w_hi, 1)
                pool.wait_ge(w_hi, 3 * (e + 1))
                pool.tensor_tensor(Wl[r][:], raw_a[:], Wh[r].bitcast(F32)[:], ALU.subtract).then_inc(w_lo, 1)
                pool.wait_ge(w_lo, 3 * e + 1)
                pool.tensor_tensor(Wm[r][64:128, :], raw_b[64:128, :], Wm[r].bitcast(F32)[64:128, :],
                                   ALU.subtract).then_inc(w_lo, 1)
                pool.wait_ge(w_lo, 3 * e + 2)
                pool.tensor_tensor(Dhl[r][:, :, D:2 * D], raw_d[:], Dhl[r].bitcast(F32)[:, :, 0:D], ALU.subtract).then_inc(w_lo, 1)

            split(0, 0)
            split(1, 1)
            with pool.Fori(1, E // 2) as j:
                split(2 * j, 0)
                split(2 * j + 1, 1)

        @block.scalar
        def _(act):
            act.dma_start(vecs[:], vecs_d).then_inc(l_vecs, 16)
            act.dma_start(dws[:], dws_d).then_inc(l_dws, 16)
            act.dma_start(wq_raw[:, 0, :], wqkv_d[0:128, :]).then_inc(l_wqkv, 16)
            for half in range(2):
                act.dma_start(wq_raw[64 * half:64 * half + 64, 1, :], wqkv_d[128:D, :]).then_inc(l_wqkv, 16)
            act.dma_start(wo_raw[:], wout_d).then_inc(l_wout, 16)
            act.dma_start(pws[:], pws_d).then_inc(l_pws, 16)
            act.wait_ge(l_vecs, 16)
            act.activation(gate[:, 0, :], vecs[:, ALPHA, :], ACT.Tanh).then_inc(tanh_done, 1)
            act.wait_ge(pads_zero, 2)

            def copy_job(j):
                kind, h = JOBS[j]
                act.wait_ge(job_done, j + 1)
                if kind == PW_G2:
                    act.wait_ge(gate_done, 3)
                for m in range(2):
                    ps = PS[0:HD, 2 * (j % 4) + m, :]
                    psv = ps.rearrange("p (y n) -> p y n", y=G)
                    c = slice(h * HALF, (h + 1) * HALF)
                    bias = {"loc": PL_B, "g": PG_B1, PW_PL: PL_PWB, PW_PG: PG_PWB, PW_F1: F1_PWB, PW_F2: F2_PWB}.get(kind)
                    bias = gate[:, 3, m:m + 1] if bias is None else vecs[:, bias, m:m + 1]
                    if kind == "loc":
                        ins = act.activation(inside(padA, m, h), psv, ACT.Gelu, bias=bias)
                    elif kind == "g":
                        ins = act.activation(inside(padB, m, h), psv, ACT.Gelu, bias=bias)
                    elif kind == PW_PL:
                        ins = act.activation(loc[:, m, c], ps, ACT.Identity, bias=bias)
                    elif kind == PW_PG:
                        ins = act.activation(g2[:, m, c], ps, ACT.Gelu, bias=bias)
                    elif kind == PW_G2:
                        ins = act.activation(t1[:, m, c], ps, ACT.Identity, bias=bias, scale=gate[:, 1, m:m + 1])
                    elif kind == PW_F1:
                        ins = act.activation(inside(padB, m, h), psv, ACT.Relu, bias=bias)
                    else:
                        ins = act.activation(t1[:, m, c], ps, ACT.Relu, bias=bias)
                ins.then_inc(job_copied, 1)

            def products_of(n, first=0, last=9):
                f, h = DWS[n]
                act.wait_ge(job_copied, job(source[f], h))
                if f in (DW_F1, DW_F3):
                    act.wait_ge(mix_done, 2 * h + (2 if f == DW_F1 else 6))
                if f in last_use:
                    act.wait_ge(job_done, job(last_use[f], h))
                for tap in range(first, last):
                    if n and tap:
                        act.wait_ge(sum_done, 8 * (n - 1) + tap)
                    for m in range(2):
                        dst, src, w = tap_args(n, tap, m, DVE_ROWS[n], G)
                        if tap:
                            dst = products[:, tap - 1, m, 0:(G - DVE_ROWS[n]) * G * BH]\
                                .rearrange("p (y n) -> p y n", n=G * BH)
                        act.activation(dst, src, ACT.Copy, scale=w).then_inc(product_done, 1)

            act.wait_ge(l_dws, 16)
            def copy_fold():
                act.wait_ge(fold_done, 1)
                for pc in range(2):
                    act.activation(wf_sb[:, pc:pc + 3:2, :],
                                   PS[:, 4 + 2 * pc, 0:2 * D].rearrange("p (c d) -> p c d", c=2), ACT.Copy).then_inc(fold_copied, 1)
                    act.activation(wf_sb[:, 4 + pc, :], PS[:, 5 + 2 * pc, 0:D], ACT.Copy).then_inc(fold_copied, 1)

            for step in ("c0", "p0", "c1", "p1", "c2", "p2", "c3", "c4", "a3", "c5", "b3", "c6", "c7",
                         "c8", "p4", "c9", "p5", "c10", "p6", "c11", "p7", "c12", "p8", "c13", "p9"):
                if step[0] == "c":
                    copy_job(int(step[1:]))
                    if step == "c0":
                        copy_fold()
                elif step[0] == "p":
                    products_of(int(step[1:]))
                else:
                    products_of(int(step[1:]), *((0, 5) if step[0] == "a" else (5, 9)))

            def sqrt(n):
                if due(n):
                    act.wait_ge(var_ready, n)
                act.activation(rstd[:, 1, :], rstd[:, 0, :], ACT.Sqrt).then_inc(std_ready, 1)

            for n in range(4):
                sqrt(n + 1)
            act.wait_ge(asum_set, 1)
            for t in range(TT):
                act.wait_ge(abs_in, t + 1)
                act.activation(AB[0:ROWS[t], t, :], Z[0:ROWS[t], t, 0:D], ACT.Abs,
                               accum_out=asum[0:ROWS[t], t:t + 1]).then_inc(abs_done, 1)

            def sign_counts(g, p, mag, n):
                _, end, first = SEARCHES[g]
                act.wait_ge(lev_ready[g], p + 1)
                for t in range(first, end):
                    i = p * (end - first) + t - first
                    if i >= 2:
                        act.wait_ge(signs_done[g], i - 1)
                    act.activation(act_junk[0:ROWS[t], i % 2, 0:n], mag[0:ROWS[t], t, :], ACT.Sign,
                                   bias=lev[0:ROWS[t], t:t + 1], scale=-1.0,
                                   accum_out=signs[0:ROWS[t], t:t + 1]).then_inc(signs_done[g], 1)

            for p in range(PASSES - 1):
                sign_counts(0, p, AB, D)
            for n in range(6):
                g, c = n // 2, n % 2
                w = 512 if g < 2 else 32
                act.wait_ge(xT_done, n + 1)
                act.activation(XH[:, c, 512 * g:512 * g + w], PS[:, 3 * c + g, 0:w], ACT.Copy).then_inc(xh_done, 1)
            act.wait_ge(ones_set, 1)
            for i, t in enumerate(V_TILES):
                act.wait_ge(qkv_done, 2 * i + 1)
                act.activation(vt[0:ROWS[t], t, 0:6, 0:DH],
                               PS[0:ROWS[t], qkv_bank(2 * i), 0:6 * DH].rearrange("p (h d) -> p h d", h=6),
                               ACT.Copy).then_inc(qkv_copied_a, 1)
            for q in range(0, 36, 2):
                act.wait_ge(qkv_done, 2 * TT + q + 1)
                act.activation(QKT[:, q // 3, 352 * (q % 3):352 * (q % 3) + 352], PS[:, qkv_bank(2 * TT + q), 0:352],
                               ACT.Copy).then_inc(qkv_copied_a, 1)

            def copy_pT(b, r):
                act.wait_ge(pT_done, b + 1)
                if due(b - 1):
                    act.wait_ge(pv_done, b - 1)
                act.activation(pT_sb[r][:].rearrange("p (k h) n -> p k h n", k=2),
                               PS[0:KEYS, 4:6, 0:6 * KEYS].rearrange("p k (h n) -> p k h n", h=6),
                               ACT.Copy).then_inc(pT_copied, 1)

            def exp(b, r):
                act.wait_ge(shifted, b + 1)
                if due(b - 1):
                    act.wait_ge(pT_done, b - 1)
                act.activation(p_sb[r][:], s_sb[:], ACT.Exp, scale=wscale[0:KEYS, 4:5]).then_inc(exp_done, 1)

            exp(0, 0)
            copy_pT(0, 0)
            exp(1, 1)
            def magnitudes(tiles):
                for t in tiles:
                    act.wait_ge(l_o[t], 16)
                    act.activation(OA[0:ROWS[t], t, :], O[0:ROWS[t], t, :], ACT.Abs,
                                   accum_out=asum[0:ROWS[t], t:t + 1]).then_inc(abs_done, 1)

            def act_images(j):
                for k in range(2):
                    copy_pT(2 * j + (k - 1), 1 - k)
                    exp(2 * j + k, k)

            act_images(1)
            with act.Fori(2, EARLY // 2) as j:
                act_images(j)
            for b in range(EARLY - 1, B):
                copy_pT(b - 1, (b - 1) % 2)
                exp(b, b % 2)
                if b == EARLY - 1:
                    magnitudes(range(4))
                if 0 <= b - EARLY < PASSES - 1:
                    sign_counts(1, b - EARLY, OA, INNER)
            copy_pT(B - 1, 1)

            magnitudes(range(4, TT))
            for p in range(PASSES - 1):
                sign_counts(2, p, OA, INNER)
            act.wait_ge(l_exp, 64)
            act.activation(Wh[0][:], raw_a[:], ACT.Copy).then_inc(w_hi, 1)
            act.activation(Wm[0][:], raw_b[:], ACT.Copy).then_inc(w_hi, 1)
            act.activation(Dhl[0][:, :, 0:D], raw_d[:], ACT.Copy).then_inc(w_hi, 1)
            for t in range(TT):
                act.wait_ge(oT_done, t + 1)
                act.activation(OH[:, :, t * 128:t * 128 + ROWS[t]].rearrange("p (k c) n -> p k c n", k=2),
                               PS[:, 2 * (t % 3):2 * (t % 3) + 2, 0:384].rearrange("p k (c n) -> p k c n", c=3)[:, :, :, 0:ROWS[t]],
                               ACT.Copy).then_inc(oh_done, 1)
            sqrt(5)
            for t in range(TT):
                act.wait_ge(xfT_done, t + 1)
                act.activation(XFh[:, :, t * 128:t * 128 + ROWS[t]],
                               PS[:, t % 4, 0:256].rearrange("p (c n) -> p c n", c=2)[:, :, 0:ROWS[t]],
                               ACT.Copy).then_inc(xfh_done, 1)
            for n in range(3):
                act.wait_ge(lgT_done, n + 1)
                act.activation(lgT[:, 352 * n:352 * n + 352], PS[0:E, 5 + n, 0:352], ACT.Copy).then_inc(lgT_copied, 1)

            def act_block(e2, k):
                n, w = k % 3, BLOCKS[k % 3][2]
                for m in range(HC + 1):
                    if m < HC:
                        i = 6 * k + m
                        act.wait_ge(gu_done, 36 * e2 + i + 1)
                        if due(36 * e2 + i - 1):
                            act.wait_ge(hp_done, 36 * e2 + i - 1)
                        act.activation(sg[m % 2][:, 0:w], PS[:, 2 * (i % 3), 0:w], ACT.Silu).then_inc(silu_done, 1)
                    if m > 0:
                        i = 6 * k + m - 1
                        act.wait_ge(hp_done, 36 * e2 + i + 1)
                        if k >= 2 or not isinstance(e2, int):
                            if due(18 * e2 + 3 * (k - 1)):
                                act.wait_ge(down_done, 18 * e2 + 3 * (k - 1))
                        act.activation(hH[k % 2][:, m - 1, 0:w], hp[(m - 1) % 2][:, 0:w], ACT.Copy).then_inc(hh_done, 1)

            for k in range(6):
                act_block(0, k)
                if k == 0:
                    act.wait_ge(diff_ready, 1)
                    act.activation(topw[:, 1, :], topw[:, 0, :], ACT.Exp).then_inc(exp2_done, 1)
            with act.Fori(1, E // 2) as e2:
                for k in range(6):
                    act_block(e2, k)

        @block.tensor
        def _(pe):
            pe.wait_ge(l_plw, 16)
            for j, (kind, h) in enumerate(JOBS):
                b0 = 2 * (j % 4)
                c = slice(h * HALF, (h + 1) * HALF)
                if j == 2:
                    pe.wait_ge(fold_copied, 4)
                if j == 3:
                    pe.wait_ge(wmean_read, 2)
                if j >= 4:
                    if due(j - 3):
                        pe.wait_ge(job_copied, j - 3)
                if kind not in ("loc", "g"):
                    pe.wait_ge(l_pws, 16)
                if kind in pw_of:
                    pe.wait_ge(tap_done, 18 * (DWS.index((pw_of[kind], h)) + 1))
                    pe.wait_ge(sum_done, 8 * (DWS.index((pw_of[kind], h)) + 1))
                if kind == PW_G2:
                    pe.wait_ge(job_copied, job(PW_PG, h))
                if kind == PW_F3:
                    src = dw_out[DW_F3]
                    for i in range(4):
                        t = 4 * h + i
                        for k in range(2):
                            mm = pe.matmul(PS[:, b0 + i // 2, (i % 2) * D:(i % 2) * D + D],
                                           src[:, k, t * 128:t * 128 + 128], pws[:, PW_F3, k, :],
                                           start=(k == 0), stop=(k == 1))
                elif kind in ("loc", "g"):
                    w = plw_sb if kind == "loc" else wf_sb
                    for k in range(KC):
                        if kind == "loc" and k % 2 == 0:
                            pe.wait_ge(l_patch[h][k // 2], 16)
                        for m in range(2):
                            mm = pe.matmul(PS[0:HD, b0 + m, :], w[:, k, m * HD:m * HD + HD], patch[:, k, c],
                                           start=(k == 0), stop=(k == KC - 1))
                else:
                    src = g2 if kind == PW_G2 else dw_out[pw_of[kind]]
                    for m in range(2):
                        for k in range(2):
                            mm = pe.matmul(PS[0:HD, b0 + m, :], pws[:, kind, k, m * HD:m * HD + HD], src[:, k, c],
                                           start=(k == 0), stop=(k == 1))
                mm.then_inc(job_done, 1)
                if j == 0:
                    pe.wait_ge(l_fold, 32)
                    for pc in range(2):
                        for bank, c0, n in ((4 + 2 * pc, 0, 2 * D), (5 + 2 * pc, 2 * D, D)):
                            for k in range(2):
                                mm = pe.matmul(PS[:, bank, 0:n], haar_sb[:, k, 128 * pc:128 * pc + 128],
                                               w1_sb[:, k, c0:c0 + n], start=(k == 0), stop=(k == 1))
                    mm.then_inc(fold_done, 1)
                    pe.wait_ge(wsum_ready, 2)
                    pe.wait_ge(fold_copied, 4)
                    pe.matmul(PS[:, 7, 0:1], ones[:, :], wabs[:, 0:1], start=True, stop=True)
                    pe.matmul(PS[:, 7, 1:2], ones[:, :], wabs[:, 1:2], start=True, stop=True).then_inc(wmean_ready, 1)
            def sum_far(which):
                pe.wait_ge(far_ready, which + 1)
                pe.matmul(PS[:, 0, 0:1], ones[:], far[:], start=True, stop=True).then_inc(far_summed, 1)

            sum_far(0)
            pe.wait_ge(l_ident, 16)
            for g in range(3):
                for c in range(2):
                    for t in range(4 * g, min(4 * g + 4, TT)):
                        pe.wait_ge(masked1, TT + t + 1)
                        tr = pe.transpose(PS[:, 3 * c + g, (t % 4) * 128:(t % 4) * 128 + ROWS[t]],
                                          Z[0:ROWS[t], t, c * 128:c * 128 + 128], ident[0:ROWS[t], 0:ROWS[t]])
                    tr.then_inc(xT_done, 1)
            pe.wait_ge(xh_done, 6)
            pe.wait_ge(xl_done, 6)
            for i in range(2 * TT + 36):
                if due((i - 8) // 2 + 1):
                    pe.wait_ge(qkv_copied_a if i % 2 == 0 else qkv_copied_d, (i - 8) // 2 + 1)
                if i < 2 * TT:
                    t, k = V_TILES[i // 2], i % 2
                    ts = slice(t * 128, t * 128 + ROWS[t])
                    ps = PS[0:ROWS[t], qkv_bank(i), 0:6 * DH]
                    cs = slice(2 * INNER + 384 * k, 2 * INNER + 384 * k + 384)
                    pe.matmul(ps, XH[:, 0, ts], Tqkv[:, 0, cs], start=True, stop=False)
                    pe.matmul(ps, XL[:, ts], Tqkv[:, 0, cs], start=False, stop=False)
                    mm = pe.matmul(ps, XH[:, 1, ts], Tqkv[:, 1, cs], start=False, stop=True)
                else:
                    m, n = (i - 2 * TT) // 3, (i - 2 * TT) % 3
                    ts = slice(352 * n, 352 * n + 352)
                    ps = PS[:, qkv_bank(i), 0:352]
                    cs = slice(128 * m, 128 * m + 128)
                    pe.matmul(ps, Tqkv[:, 0, cs], XH[:, 0, ts], start=True, stop=False)
                    pe.matmul(ps, Tqkv[:, 0, cs], XL[:, ts], start=False, stop=False)
                    mm = pe.matmul(ps, Tqkv[:, 1, cs], XH[:, 1, ts], start=False, stop=True)
                mm.then_inc(qkv_done, 1)

            def scores(b, r):
                pe.wait_ge(qkb_ready, b + 1)
                if due(b - 1):
                    pe.wait_ge(shifted, b - 1)
                for h in range(HEADS):
                    p = 64 * (h % 2)
                    mm = pe.matmul(PS[0:KEYS, 2 * r + h % 2, (h // 2) * KEYS:(h // 2 + 1) * KEYS],
                                   qk_b[r][p:p + 64, h // 2, :], qk_b[r][p:p + 64, 6 + h // 2, :],
                                   start=True, stop=True)
                mm.then_inc(scores_done, 1)

            def transposed(b, r):
                pe.wait_ge(exp_done, b + 1)
                if due(b):
                    pe.wait_ge(pT_copied, b)
                for h in range(HEADS):
                    tr = pe.transpose(PS[0:KEYS, 4 + h // 6, (h % 6) * KEYS:(h % 6 + 1) * KEYS], p_sb[r][:, h, :],
                                      ident[0:KEYS, 0:KEYS])
                tr.then_inc(pT_done, 1)

            def weighted(b, r):
                pe.wait_ge(pT_copied, b + 1)
                pe.wait_ge(v_loaded[r], 16 * (b - r) + 32)
                if due(b):
                    pe.wait_ge(o_ready, b)
                for h in range(HEADS):
                    mm = pe.matmul(PS[0:KEYS, 6 + h // 6, (h % 6) * (DH + 1):(h % 6 + 1) * (DH + 1)], pT_sb[r][:, slot(h), :],
                                   v_b[r][:, h, :], start=True, stop=True)
                mm.then_inc(pv_done, 1)

            pe.wait_ge(qkv_copied_a, TT + 18)
            pe.wait_ge(qkv_copied_d, TT + 18)
            scores(0, 0)
            scores(1, 1)
            transposed(0, 0)

            def pe_images(j):
                for k in range(2):
                    scores(2 * j + k, k)
                    transposed(2 * j + (k - 1), 1 - k)
                    weighted(2 * j + (k - 2), k)

            pe_images(1)
            with pe.Fori(2, B // 2) as j:
                pe_images(j)
            transposed(B - 1, 1)
            weighted(B - 2, 0)
            weighted(B - 1, 1)
            pe.wait_ge(o_ready, B)

            def turn_o(t):
                pe.wait_ge(masked2, t + 1)
                if due(t - 2):
                    pe.wait_ge(ol_done, t - 2)
                for c in range(HC):
                    tr = pe.transpose(PS[:, 2 * (t % 3) + c // 3, (c % 3) * 128:(c % 3) * 128 + ROWS[t]],
                                      O[0:ROWS[t], t, 128 * c:128 * c + 128], ident[0:ROWS[t], 0:ROWS[t]])
                tr.then_inc(oT_done, 1)

            def project(t):
                pe.wait_ge(oh_done, t + 1)
                pe.wait_ge(ol_done, t + 1)
                if due(t - 1):
                    pe.wait_ge(proj_added, t - 1)
                for c in range(HC):
                    for x in (OH, OL):
                        mm = pe.matmul(PS[0:ROWS[t], 6 + t % 2, 0:D], x[:, c, t * 128:t * 128 + ROWS[t]], Tout[:, c, :],
                                       start=(c == 0 and x is OH), stop=(c == HC - 1 and x is OL))
                mm.then_inc(proj_done, 1)

            sum_far(1)
            turn_o(0)
            turn_o(1)
            for t in range(TT):
                if t + 2 < TT:
                    turn_o(t + 2)
                project(t)
            pe.wait_ge(x6_ready, 1)
            for t in range(TT):
                if due(t - 3):
                    pe.wait_ge(xfl_done, t - 3)
                for c in range(2):
                    tr = pe.transpose(PS[:, t % 4, 128 * c:128 * c + ROWS[t]], X6[0:ROWS[t], t, 128 * c:128 * c + 128],
                                      ident[0:ROWS[t], 0:ROWS[t]])
                tr.then_inc(xfT_done, 1)
            pe.wait_ge(xfl_done, TT)
            pe.wait_ge(xfh_done, TT)
            pe.wait_ge(router_split, 3)
            for n in range(3):
                cs = slice(352 * n, 352 * n + 352)
                ps = PS[0:E, 5 + n, 0:352]
                pe.matmul(ps, router_h[:, 0, :], XFh[:, 0, cs], start=True, stop=False)
                pe.matmul(ps, router_h[:, 0, :], XFl[:, 0, cs], start=False, stop=False)
                pe.matmul(ps, router_l[:], XFh[:, 0, cs], start=False, stop=False)
                pe.matmul(ps, router_h[:, 1, :], XFh[:, 1, cs], start=False, stop=False)
                pe.matmul(ps, router_h[0:64, 1, :], XFl[0:64, 1, cs], start=False, stop=True).then_inc(lgT_done, 1)

            def turn_logits():
                pe.wait_ge(lgT_copied, 3)
                for t in range(TT):
                    tr = pe.transpose(PS[0:ROWS[t], 6, E * t:E * t + E], lgT[:, t * 128:t * 128 + ROWS[t]], ident[0:E, 0:E])
                tr.then_inc(logits_done, 1)

            def gate_up(e2, k):
                r, n = k // 3, k % 3
                cs, w = moe_columns(n), BLOCKS[n][2]
                if n == 0:
                    pe.wait_ge(w_hi, 6 * e2 + 3 * r + 3)
                    pe.wait_ge(w_lo, 6 * e2 + 3 * r + 3)
                for m in range(HC):
                    i = 6 * k + m
                    if isinstance(e2, int) and i == 2:
                        pe.wait_ge(lgT_copied, 1)
                    if not (isinstance(e2, int) and e2 == 0 and i < 3):
                        if due(36 * e2 + i - 2):
                            pe.wait_ge(hp_done, 36 * e2 + i - 2)
                    for side in range(2):
                        c0 = side * HID + 128 * m
                        ps = PS[:, 2 * (i % 3) + side, 0:w]
                        pe.matmul(ps, Wh[r][:, c0:c0 + 128], XFh[:, 0, cs], start=True, stop=False)
                        pe.matmul(ps, Wh[r][:, c0:c0 + 128], XFl[:, 0, cs], start=False, stop=False)
                        pe.matmul(ps, Wl[r][:, c0:c0 + 128], XFh[:, 0, cs], start=False, stop=False)
                        pe.matmul(ps, Wm[r][:, c0:c0 + 128], XFh[:, 1, cs], start=False, stop=False)
                        mm = pe.matmul(ps, Wm[r][0:64, c0:c0 + 128], XFl[0:64, 1, cs], start=False, stop=True)
                    mm.then_inc(gu_done, 1)

            def down(e2, k):
                r, n = k // 3, k % 3
                t0 = BLOCKS[n][0]
                if isinstance(e2, int) and k == 0:
                    pe.wait_ge(logits_read, 2)
                pe.wait_ge(hh_done, 36 * e2 + 6 * k + 6)
                pe.wait_ge(hl_done, 36 * e2 + 6 * k + 6)
                for i in range(3):
                    t = t0 + i
                    d = 3 * k + i
                    if not (isinstance(e2, int) and e2 == 0 and d < 2):
                        if due(18 * e2 + d - 1):
                            pe.wait_ge(down_added, 18 * e2 + d - 1)
                    cs = slice(128 * i, 128 * i + ROWS[t])
                    ps = PS[0:ROWS[t], 6 + d % 2, 0:2 * D]
                    for m in range(HC):
                        both = (ps, hH[k % 2][:, m, cs], Dhl[r][:, m, :])
                        rest = (ps[:, 0:D], hL[k % 2][:, m, cs], Dhl[r][:, m, 0:D])
                        for n_, mm_ in enumerate((both, rest) if m < HC - 1 else (rest, both)):
                            mm = pe.matmul(*mm_, start=(m == 0 and n_ == 0), stop=(m == HC - 1 and n_ == 1))
                    mm.then_inc(down_done, 1)

            def pe_pair(e2):
                gate_up(e2, 0)
                if isinstance(e2, int):
                    turn_logits()
                for k in range(1, 6):
                    gate_up(e2, k)
                    down(e2, k - 1)
                down(e2, 5)

            pe_pair(0)
            with pe.Fori(1, E // 2) as e2:
                pe_pair(e2)

        @block.vector
        def _(dve):
            count = [0]

            def link(*steps):
                for ins in steps:
                    count[0] += 1
                    ins.then_inc(dve_done, 1)
                dve.wait_ge(dve_done, count[0])

            link(dve.memset(ones[:], 1.0))
            dve.memset(asum[:], 1.0).then_inc(asum_set, 1)
            link(dve.memset(wabs[:], 0.0))
            dve.wait_ge(tanh_done, 1)
            dve.tensor_scalar(gate[:, 1, :], gate[:, 0, :], 1.0, 0.5, ALU.add, ALU.mult).then_inc(gate_done, 1)
            dve.wait_ge(gate_done, 1)
            dve.tensor_scalar(gate[:, 2, :], gate[:, 1, :], -1.0, 1.0, ALU.mult, ALU.add).then_inc(gate_done, 1)
            dve.tensor_tensor(gate[:, 3, :], gate[:, 1, :], vecs[:, PG_B2, :], ALU.mult).then_inc(gate_done, 1)

            dve.wait_ge(l_dws, 16)

            def depthwise(n):
                for tap in range(9):
                    for m in range(2):
                        if due(18 * n + 2 * tap + m - 1):
                            dve.wait_ge(tap_done, 18 * n + 2 * tap + m - 1)
                        dst, src, w = tap_args(n, tap, m, 0, DVE_ROWS[n])
                        if tap == 0:
                            dve.tensor_scalar(dst, src, w, None, ALU.mult).then_inc(tap_done, 1)
                        else:
                            dve.scalar_tensor_tensor(dst, src, w, dst, ALU.mult, ALU.add).then_inc(tap_done, 1)

            def weight_sums():
                dve.wait_ge(l_wqkv, 48)
                link(dve.memset(wsum[64:128, 0, 48:96], 0.0),
                     dve.tensor_reduce(wsum[:, 0, 0:48], wq_raw[:, 0, :].rearrange("p (a n) -> p a n", n=48), AX.X, ALU.add,
                                       apply_absolute_value=True),
                     dve.tensor_reduce(wsum[0:64, 0, 48:96], wq_raw[0:64, 1, :].rearrange("p (a n) -> p a n", n=48), AX.X,
                                       ALU.add, apply_absolute_value=True))
                dve.tensor_reduce(wabs[:, 0:1], wsum[:, 0, :], AX.X, ALU.add).then_inc(wsum_ready, 1)
                dve.wait_ge(l_wout, 16)
                link(dve.tensor_reduce(wsum[:, 1, 0:24], wo_raw[:].rearrange("p c (a n) -> p (c a) n", n=48), AX.X, ALU.add,
                                       apply_absolute_value=True))
                dve.tensor_reduce(wabs[:, 1:2], wsum[:, 1, 0:24], AX.X, ALU.add).then_inc(wsum_ready, 1)

            def weight_scales():
                dve.wait_ge(wmean_ready, 1)
                dve.tensor_scalar(wscale[:, 0:1], PS[:, 7, 0:1], 1.0 / (3 * INNER * D), None, ALU.mult).then_inc(wmean_read, 1)
                dve.tensor_scalar(wscale[:, 1:2], PS[:, 7, 1:2], 1.0 / (INNER * D), None, ALU.mult).then_inc(wmean_read, 1)
                dve.wait_ge(wmean_read, 2)
                link(dve.tensor_scalar(wscale[:, 2:4], wscale[:, 0:2], 1e-8, 0.5, ALU.add, ALU.mult))
                link(dve.scalar_tensor_tensor(wscale[:, 4:5], wscale[:, 0:1], wscale[:, 0:1], wscale[:, 0:1],
                                              ALU.mult, ALU.bypass))
                link(dve.tensor_scalar(wscale[:, 4:5], wscale[:, 4:5], float(DH) ** -0.5, None, ALU.mult))
                link(dve.tensor_tensor(wscale[:, 5:6], wscale[:, 0:1], wscale[:, 1:2], ALU.mult))
                link(dve.tensor_scalar(wscale[:, 6:8], wscale[:, 2:4], -1.0, None, ALU.mult))

            def ternary_qkv(c):
                link(dve.tensor_scalar(neg1[:], wq_raw[:, c, :], wscale[:, 6:7], None, ALU.is_lt))
                link(dve.scalar_tensor_tensor(Tqkv[:, c, :], wq_raw[:, c, :], wscale[:, 2:3], neg1[:],
                                              ALU.is_gt, ALU.subtract))

            def ternary_out():
                flat = wo_raw[:].rearrange("p c n -> p (c n)")
                link(dve.tensor_scalar(neg1[:, 0:HC * D], flat, wscale[:, 7:8], None, ALU.is_lt))
                link(dve.scalar_tensor_tensor(Tout[:].rearrange("p c n -> p (c n)"), flat, wscale[:, 3:4],
                                              neg1[:, 0:HC * D], ALU.is_gt, ALU.subtract))

            for n, (f, h) in enumerate(DWS):
                if n == 0:
                    weight_sums()
                if n == 1:
                    weight_scales()
                    ternary_qkv(0)
                if n == 2:
                    ternary_out()
                if n == 3:
                    ternary_qkv(1)
                dve.wait_ge(job_copied, job(source[f], h))
                for m in range(2):
                    if f == DW_F1:
                        dve.scalar_tensor_tensor(inside(padA, m, h), cols(loc, m, h), gate[:, 2, m:m + 1], cols(t1, m, h),
                                                 ALU.mult, ALU.add).then_inc(mix_done, 1)
                    if f == DW_F3:
                        dve.tensor_tensor(inside(padA, m, h), cols(loc, m, h), cols(t1, m, h), ALU.add)\
                           .then_inc(mix_done, 1)
                if f in (DW_F1, DW_F3):
                    dve.wait_ge(mix_done, 2 * h + (2 if f == DW_F1 else 6))
                if f in last_use:
                    dve.wait_ge(job_done, job(last_use[f], h))
                depthwise(n)
            dve.wait_ge(l_rows, 16)

            def row(n, k):
                return rows[:, n, :].unsqueeze(1).to_broadcast([128, k, D])

            n_ln = [0]

            def inverse_root(src, dst, tiles):
                n_ln[0] += 1
                dve.tensor_scalar(rstd[:, 0, tiles], src, EPS, None, ALU.add).then_inc(var_ready, 1)
                dve.wait_ge(std_ready, n_ln[0])
                link(dve.reciprocal(rstd[:, dst, tiles], rstd[:, 1, tiles]))
                link(dve.tensor_tensor(rstd[:, 3, tiles], rstd[:, dst, tiles], rstd[:, dst, tiles], ALU.mult))
                link(dve.tensor_tensor(rstd[:, 3, tiles], rstd[:, 3, tiles], rstd[:, 0, tiles], ALU.mult))
                link(dve.tensor_scalar(rstd[:, 3, tiles], rstd[:, 3, tiles], -0.5, 1.5, ALU.mult, ALU.add))
                link(dve.tensor_tensor(rstd[:, dst, tiles], rstd[:, dst, tiles], rstd[:, 3, tiles], ALU.mult))

            def norm(src, dst, t0, t1, twice=False, affine=None, signal=None):
                tiles = slice(t0, t1)
                link(*[dve.bn_stats(bn[:, t, :], src[:, t, 0:D]) for t in range(t0, t1)])
                link(*[dve.bn_aggr(mv[:, t, :], bn[:, t, :]) for t in range(t0, t1)])
                inverse_root(mv[:, tiles, 1], 2, tiles)
                if twice:
                    link(dve.tensor_tensor(rstd[:, 3, tiles], rstd[:, 2, tiles], rstd[:, 2, tiles], ALU.mult))
                    link(dve.tensor_tensor(rstd[:, 3, tiles], rstd[:, 3, tiles], mv[:, tiles, 1], ALU.mult))
                    inverse_root(rstd[:, 3, tiles], 4, tiles)
                    link(dve.tensor_tensor(rstd[:, 2, tiles], rstd[:, 2, tiles], rstd[:, 4, tiles], ALU.mult))
                if affine is None:
                    link(*[dve.tensor_scalar(dst[:, t, 0:D], src[:, t, 0:D], mv[:, t, 0:1], rstd[:, 2, t:t + 1],
                                             ALU.subtract, ALU.mult) for t in range(t0, t1)])
                    return
                factors, shifts = (rows[:, n, :] for n in affine)
                link(*[dve.scalar_tensor_tensor(dst[:, t, 0:D], src[:, t, 0:D], mv[:, t, 0:1], factors,
                                                ALU.subtract, ALU.mult) for t in range(t0, t1)])
                last = [dve.scalar_tensor_tensor(dst[:, t, 0:D], dst[:, t, 0:D], rstd[:, 2, t:t + 1], shifts,
                                                 ALU.mult, ALU.add) for t in range(t0, t1)]
                if signal is None:
                    link(*last)
                else:
                    for ins in last:
                        ins.then_inc(signal, 1)

            link(dve.memset(rstd[:], 1.0))
            link(dve.memset(cnt[:], 0.0))
            link(dve.memset(signs[:], 0.0))
            link(dve.memset(top8[:], 0.0))
            for h in range(2):
                dve.wait_ge(job_done, 15 + h)
                link(*[dve.tensor_tensor(H[:, t:t + 2, :],
                                         PS[:, 2 * (2 + h) + (t % 4) // 2, 0:2 * D].rearrange("p (t d) -> p t d", t=2),
                                         row(F3_PWB, 2), ALU.add) for t in (4 * h, 4 * h + 2)])
                norm(H, H, 4 * h, 4 * h + 4, affine=(LN_G, LN_B))
            dve.wait_ge(l_cls, 32)
            norm(H, Z, 0, TT, twice=True, affine=(GAMMA, BETA), signal=abs_in)
            dve.wait_ge(l_small, 80)
            dve.tensor_copy(router_h[:], router[:]).then_inc(router_split, 1)
            dve.wait_ge(router_split, 1)
            dve.tensor_tensor(router_l[:], router[:, 0, :], router_h.bitcast(F32)[:, 0, :], ALU.subtract).then_inc(router_split, 1)
            dve.tensor_tensor(router_h[64:128, 1, :], router[64:128, 1, :], router_h.bitcast(F32)[64:128, 1, :],
                              ALU.subtract).then_inc(router_split, 1)
            for k, n in ((1, D), (2, INNER)):
                link(dve.tensor_scalar(qrank[:, k:k + 1], qrank[:, 0:1], float(n - 1), None, ALU.mult))
                link(dve.tensor_scalar(qrank[:, k:k + 1], qrank[:, k:k + 1], -1.0, float(n - 1), ALU.mult, ALU.add))
                link(dve.tensor_scalar(qrank[:, 2 + k:3 + k], qrank[:, k:k + 1], 4.0, None, ALU.subtract))
                link(dve.tensor_scalar(qrank[:, 4 + k:5 + k], qrank[:, 2 + k:3 + k], -1.0, n / 2, ALU.mult, ALU.add))

            def count_all(step, base, mag, n, level, t0=0, t1=TT):
                for i, t in enumerate(range(t0, t1)):
                    if i >= 2:
                        dve.wait_ge(step, base + i - 1)
                    dve.tensor_scalar(junk[0:ROWS[t], i % 2, 0:n], mag[0:ROWS[t], t, :], level[0:ROWS[t], t:t + 1],
                                      None, ALU.is_ge, ALU.add, accum_out=cnt[0:ROWS[t], t:t + 1]).then_inc(step, 1)
                dve.wait_ge(step, base + t1 - t0)

            def select_by_bits(step, mag, n, k):
                dve.memset(thr[:], 0).then_inc(step, 1)
                dve.memset(bitf[:], float(1 << 30)).then_inc(step, 1)
                dve.wait_ge(step, 2)
                with dve.Fori(0, 31) as i:
                    base = 14 * i + 2
                    dve.tensor_copy(biti[:], bitf[:]).then_inc(step, 1)
                    dve.wait_ge(step, base + 1)
                    dve.tensor_tensor(cand[:], thr[:], biti[:], ALU.bitwise_or).then_inc(step, 1)
                    dve.wait_ge(step, base + 2)
                    count_all(step, base + 2, mag, n, cand.bitcast(F32))
                    dve.scalar_tensor_tensor(hitb[:], cnt[:], qrank[:, k:k + 1], bitf[:], ALU.is_gt, ALU.mult).then_inc(step, 1)
                    dve.wait_ge(step, base + 12)
                    dve.tensor_tensor(thr[:], thr[:], hitb[:], ALU.bitwise_or).then_inc(step, 1)
                    dve.tensor_scalar(bitf[:], bitf[:], 0.5, None, ALU.mult).then_inc(step, 1)
                    dve.wait_ge(step, base + 14)

            def first_levels(g, n, start, slope):
                ts = slice(*SEARCHES[g][:2])
                link(dve.tensor_scalar(inv[:, ts], asum[:, ts], 1.0 / (n * n * slope), None, ALU.mult))
                dve.tensor_scalar(lev[:, ts], asum[:, ts], qrank[:, 0:1], start / n, ALU.mult, ALU.mult)\
                   .then_inc(lev_ready[g], 1)
                dve.wait_ge(lev_ready[g], 1)

            def counts(g, p, mag, n):
                t0, t1, a = SEARCHES[g]
                count_all(count_done[g][p], 0, mag, n, lev, t0, a if p < PASSES - 1 else t1)

            def next_levels(g, p, k):
                t0, t1, a = SEARCHES[g]
                ts, own, acts = slice(t0, t1), slice(t0, a), slice(a, t1)
                step, moved, square, fit, weight, near, top = (work[:, i, ts] for i in range(1, 8))
                e, before = err[:, p % 2, ts], err[:, (p + 1) % 2, ts]
                dve.wait_ge(signs_done[g], (p + 1) * (t1 - a))
                link(dve.tensor_scalar(err[:, p % 2, own], cnt[:, own], qrank[:, 2 + k:3 + k], None, ALU.subtract),
                     dve.tensor_scalar(err[:, p % 2, acts], signs[:, acts], -0.5, qrank[:, 4 + k:5 + k], ALU.mult, ALU.add))
                if p == 0:
                    link(dve.tensor_tensor(square, e, e, ALU.mult),
                         dve.tensor_tensor(near, e, inv[:, ts], ALU.mult))
                    link(dve.scalar_tensor_tensor(step, square, 16.0, near, ALU.is_ge, ALU.mult))
                else:
                    link(dve.tensor_tensor(square, e, e, ALU.mult),
                         dve.tensor_tensor(moved, before, e, ALU.subtract))
                    link(dve.scalar_tensor_tensor(near, square, 16.0, e, ALU.is_ge, ALU.mult),
                         dve.tensor_tensor(fit, step, moved, ALU.mult),
                         dve.tensor_tensor(weight, moved, moved, ALU.mult))
                    link(dve.scalar_tensor_tensor(fit, inv[:, ts], 30.0, fit, ALU.mult, ALU.add),
                         dve.tensor_scalar(weight, weight, 30.0, None, ALU.add))
                    link(dve.reciprocal(weight, weight),
                         dve.tensor_tensor(top, fit, near, ALU.mult))
                    link(dve.tensor_tensor(inv[:, ts], fit, weight, ALU.mult),
                         dve.tensor_tensor(step, top, weight, ALU.mult))
                dve.tensor_tensor(lev[:, ts], lev[:, ts], step, ALU.add).then_inc(lev_ready[g], 1)
                dve.wait_ge(lev_ready[g], p + 2)

            def judge(g, k):
                ts = slice(*SEARCHES[g][:2])
                e, square = err[:, (PASSES - 1) % 2, ts], work[:, 3, ts]
                link(dve.tensor_scalar(e, cnt[:, ts], qrank[:, 2 + k:3 + k], None, ALU.subtract))
                link(dve.tensor_tensor(square, e, e, ALU.mult))
                link(dve.tensor_scalar(work[:, 0, ts], square, 16.0, None, ALU.is_ge))

            def largest(g, mag, n):
                t0, t1, _ = SEARCHES[g]
                b0 = 2 * sum(end - first for first, end, _ in SEARCHES[:g])
                nt = t1 - t0
                for i in range(nt + 1):
                    if i < nt:
                        t, p = t0 + i, ROWS[t0 + i]
                        if i >= 2:
                            dve.wait_ge(below_done, b0 + 2 * i - 1)
                        dve.scalar_tensor_tensor(below[0:p, i % 2, 0:n], mag[0:p, t, :], lev[0:p, t:t + 1], mag[0:p, t, :],
                                                 ALU.is_lt, ALU.mult).then_inc(below_done, 1)
                    if i > 0:
                        t, p = t0 + i - 1, ROWS[t0 + i - 1]
                        dve.wait_ge(below_done, b0 + (max(2 * i - 2, 1) if i < nt else 2 * nt - 1))
                        dve.max(top8[0:p, t, :], below[0:p, (i - 1) % 2, 0:n]).then_inc(below_done, 1)
                dve.wait_ge(below_done, b0 + 2 * nt)

            def thresholds(which, mag, n, k):
                dve.wait_ge(far_summed, which + 1)
                link(dve.tensor_scalar(work[:, 1], cnt[:], qrank[:, k:k + 1], -1.0, ALU.subtract, ALU.mult),
                     dve.tensor_copy(far_i[0:1, :], PS[0:1, 0, 0:1]))
                link(dve.tensor_tensor(pick[:], iota[:].unsqueeze(1).to_broadcast([128, TT, 8]),
                                       work[:, 1].unsqueeze(2).to_broadcast([128, TT, 8]), ALU.is_gt))
                link(dve.scalar_tensor_tensor(pick[:].rearrange("p t e -> p (t e)"), pick[:].rearrange("p t e -> p (t e)"),
                                              3e38, top8[:].rearrange("p t e -> p (t e)"), ALU.mult, ALU.add))
                link(dve.tensor_reduce(thr.bitcast(F32)[:], pick[:], AX.X, ALU.min))
                left = dve.value_load(far_i[0:1, 0:1], min_val=0, max_val=NT)
                with dve.If(left > 0):
                    select_by_bits(bit_step[which], mag, n, k)

            def sum_far_rows():
                link(dve.memset(work[32:64, 0, 8:9], 0.0),
                     dve.memset(work[64:128, 0, 8:9], 0.0))
                dve.tensor_reduce(far[:, 0:1], work[:, 0], AX.X, ALU.add).then_inc(far_ready, 1)

            dve.wait_ge(abs_done, TT)
            first_levels(0, D, 1.43, 0.566)
            for p in range(PASSES - 1):
                counts(0, p, AB, D)
                next_levels(0, p, 1)
            counts(0, PASSES - 1, AB, D)
            judge(0, 1)
            sum_far_rows()
            largest(0, AB, D)
            thresholds(0, AB, D, 1)
            for dst, src in ((slice(D, 256), slice(128, D)), (slice(0, D), slice(0, D))):
                if dst.start == 0:
                    dve.wait_ge(masked1, TT)
                for t in range(TT):
                    p = ROWS[t]
                    dve.scalar_tensor_tensor(Z[0:p, t, dst], AB[0:p, t, src], thr.bitcast(F32)[0:p, t:t + 1],
                                             Z[0:p, t, src], ALU.is_ge, ALU.mult).then_inc(masked1, 1)
            for n in range(6):
                g, c = n // 2, n % 2
                w = 512 if g < 2 else 32
                cs = slice(512 * g, 512 * g + w)
                dve.wait_ge(xh_done, n + 1)
                if c == 0:
                    dve.tensor_tensor(XL[:, cs], PS[:, g, 0:w], XH.bitcast(F32)[:, 0, cs], ALU.subtract).then_inc(xl_done, 1)
                else:
                    dve.tensor_tensor(XH[64:128, 1, cs], PS[64:128, 3 + g, 0:w], XH.bitcast(F32)[64:128, 1, cs],
                                      ALU.subtract).then_inc(xl_done, 1)
            dve.memset(vt[:, :, :, DH:DH + 1], 1.0).then_inc(ones_set, 1)
            dve.wait_ge(ones_set, 1)
            for i, t in enumerate(V_TILES):
                dve.wait_ge(qkv_done, 2 * i + 2)
                dve.tensor_copy(vt[0:ROWS[t], t, 6:12, 0:DH],
                                PS[0:ROWS[t], qkv_bank(2 * i + 1), 0:6 * DH].rearrange("p (h d) -> p h d", h=6))\
                   .then_inc(qkv_copied_d, 1)
            for q in range(1, 36, 2):
                dve.wait_ge(qkv_done, 2 * TT + q + 1)
                dve.tensor_copy(QKT[:, q // 3, 352 * (q % 3):352 * (q % 3) + 352], PS[:, qkv_bank(2 * TT + q), 0:352])\
                   .then_inc(qkv_copied_d, 1)
            link(dve.tensor_tensor(H[:], H[:], row(B_OUT, TT), ALU.add))
            dve.wait_ge(qkv_copied_a, TT + 18)
            dve.wait_ge(qkv_copied_d, TT + 18)

            def qk_copies(b, r):
                if due(b - 1):
                    dve.wait_ge(scores_done, b - 1)
                a, c = batch_cols(QKT, b)
                dve.tensor_copy(qk_b[r][:, :, 0:S], a)
                dve.tensor_copy(qk_b[r][:, :, S:KEYS].unsqueeze(3), c).then_inc(qkb_ready, 1)

            def shift(b, r):
                dve.wait_ge(scores_done, b + 1)
                sc = PS[0:KEYS, 2 * r:2 * r + 2, 0:6 * KEYS].rearrange("p k (h n) -> p k h n", h=6)
                m = mx[:, r, :].rearrange("p (k h) -> p k h", k=2)
                if due(b - 1):
                    dve.wait_ge(shifted, b - 1)
                dve.tensor_reduce(m, sc, AX.X, ALU.max).then_inc(max_done, 1)
                dve.wait_ge(max_done, b + 1)
                if due(b):
                    dve.wait_ge(exp_done, b)
                dve.tensor_tensor(s_sb[:].rearrange("p (k h) n -> p k h n", k=2), sc,
                                  m.unsqueeze(3).to_broadcast([KEYS, 2, 6, KEYS]), ALU.subtract).then_inc(shifted, 1)

            def normalize(b, r):
                dve.wait_ge(pv_done, b + 1)
                pv = PS[0:KEYS, 6:8, 0:6 * (DH + 1)].rearrange("p k (h d) -> p k h d", h=6)
                rc = mx[:, 2 + r, :].rearrange("p (k h) -> p k h", k=2)
                if due(b - 1):
                    dve.wait_ge(o_ready, b - 1)
                dve.reciprocal(rc.unsqueeze(3), pv[:, :, :, DH:DH + 1]).then_inc(recip_done, 1)
                dve.wait_ge(recip_done, b + 1)
                if not (isinstance(b, int) and b < 2):
                    if due(16 * b - 16 * r):
                        dve.wait_ge(o_stored[r], 16 * b - 16 * r)
                dve.tensor_tensor(o_b[r][:].rearrange("p (k h) d -> p k h d", k=2), pv[:, :, :, 0:DH],
                                  rc.unsqueeze(3).to_broadcast([KEYS, 2, 6, DH]), ALU.mult).then_inc(o_ready, 1)

            qk_copies(0, 0)
            qk_copies(1, 1)
            shift(0, 0)
            qk_copies(2, 0)
            shift(1, 1)

            def dve_images(j):
                for k in range(2):
                    if k:
                        qk_copies(2 * j + 2, 0)
                    else:
                        qk_copies(2 * j + 1, 1)
                    shift(2 * j + k, k)
                    normalize(2 * j + (k - 2), k)

            dve_images(1)
            with dve.Fori(2, EARLY // 2) as j:
                dve_images(j)
            for b in range(EARLY - 1, B):
                if b + 1 < B:
                    qk_copies(b + 1, (b + 1) % 2)
                shift(b, b % 2)
                p = b - EARLY
                if p == 0:
                    dve.wait_ge(abs_done, TT + 4)
                    first_levels(1, INNER, 1.74, 0.489)
                if p > 0:
                    next_levels(1, p - 1, 2)
                normalize(b - 2, b % 2)
                if 0 <= p < PASSES - 1:
                    counts(1, p, OA, INNER)
            normalize(B - 2, 0)
            normalize(B - 1, 1)
            counts(1, PASSES - 1, OA, INNER)
            judge(1, 2)
            largest(1, OA, INNER)

            dve.wait_ge(abs_done, 2 * TT)
            first_levels(2, INNER, 1.74, 0.489)
            for p in range(PASSES - 1):
                counts(2, p, OA, INNER)
                next_levels(2, p, 2)
            counts(2, PASSES - 1, OA, INNER)
            judge(2, 2)
            sum_far_rows()
            largest(2, OA, INNER)
            thresholds(1, OA, INNER, 2)

            def mask_o(t):
                p = ROWS[t]
                dve.scalar_tensor_tensor(O[0:p, t, :], OA[0:p, t, :], thr.bitcast(F32)[0:p, t:t + 1], O[0:p, t, :],
                                         ALU.is_ge, ALU.mult).then_inc(masked2, 1)

            def rest_o(t):
                dve.wait_ge(oh_done, t + 1)
                cs = slice(t * 128, t * 128 + ROWS[t])
                dve.tensor_tensor(OL[:, :, cs].rearrange("p (k c) n -> p k c n", k=2),
                                  PS[:, 2 * (t % 3):2 * (t % 3) + 2, 0:384].rearrange("p k (c n) -> p k c n", c=3)[:, :, :, 0:ROWS[t]],
                                  OH.bitcast(F32)[:, :, cs].rearrange("p (k c) n -> p k c n", k=2),
                                  ALU.subtract).then_inc(ol_done, 1)

            def add_projection(t):
                p = ROWS[t]
                dve.wait_ge(proj_done, t + 1)
                dve.scalar_tensor_tensor(H[0:p, t, :], PS[0:p, 6 + t % 2, 0:D], wscale[0:p, 5:6], H[0:p, t, :],
                                         ALU.mult, ALU.add).then_inc(proj_added, 1)

            mask_o(0)
            mask_o(1)
            for t in range(TT + 1):
                if t + 2 < TT:
                    mask_o(t + 2)
                if t < TT:
                    rest_o(t)
                if t > 0:
                    add_projection(t - 1)
            dve.wait_ge(proj_added, TT)
            norm(H, X6, 0, TT)
            dve.tensor_copy(X6[:, :, D:256], X6[:, :, 128:D]).then_inc(x6_ready, 1)
            for t in range(TT):
                dve.wait_ge(xfh_done, t + 1)
                cs = slice(t * 128, t * 128 + ROWS[t])
                dve.tensor_tensor(XFl[:, :, cs], PS[:, t % 4, 0:256].rearrange("p (c n) -> p c n", c=2)[:, :, 0:ROWS[t]],
                                  XFh.bitcast(F32)[:, :, cs], ALU.subtract).then_inc(xfl_done, 1)
            def hidden(e2, k):
                w = BLOCKS[k % 3][2]
                for m in range(HC + 1):
                    if m < HC:
                        i = 6 * k + m
                        dve.wait_ge(silu_done, 36 * e2 + i + 1)
                        if not (isinstance(e2, int) and e2 == 0 and i < 2):
                            if due(36 * e2 + i - 1):
                                dve.wait_ge(hl_done, 36 * e2 + i - 1)
                        dve.tensor_tensor(hp[m % 2][:, 0:w], sg[m % 2][:, 0:w], PS[:, 2 * (i % 3) + 1, 0:w],
                                          ALU.mult).then_inc(hp_done, 1)
                    if m > 0:
                        i = 6 * k + m - 1
                        dve.wait_ge(hh_done, 36 * e2 + i + 1)
                        dve.tensor_tensor(hL[k % 2][:, m - 1, 0:w], hp[(m - 1) % 2][:, 0:w],
                                          hH[k % 2].bitcast(F32)[:, m - 1, 0:w], ALU.subtract).then_inc(hl_done, 1)

            def add_down(e2, k):
                n = k % 3
                for i in range(3):
                    t = BLOCKS[n][0] + i
                    d = 3 * k + i
                    p = ROWS[t]
                    dve.wait_ge(down_done, 18 * e2 + d + 1)
                    if due(18 * e2 + d - 8 if d >= 8 or not isinstance(e2, int) else 0):
                        dve.wait_ge(down_added, 18 * e2 + d - 8 if d >= 8 or not isinstance(e2, int) else 0)
                    w = wE[0:p, t, k // 3:k // 3 + 1] if isinstance(e2, int) else wE[0:p, t, bass.ts(e2 * 2 + k // 3, 1)]
                    if isinstance(e2, int):
                        w = wE[0:p, t, 2 * e2 + k // 3:2 * e2 + k // 3 + 1]
                    dve.scalar_tensor_tensor(H[0:p, t, :], PS[0:p, 6 + d % 2, 0:D], w, H[0:p, t, :], ALU.mult,
                                             ALU.add).then_inc(half_added, 1)
                    dve.wait_ge(half_added, 18 * e2 + d + 1)
                    dve.scalar_tensor_tensor(H[0:p, t, :], PS[0:p, 6 + d % 2, D:2 * D], w, H[0:p, t, :], ALU.mult,
                                             ALU.add).then_inc(down_added, 1)

            def route():
                link(dve.memset(logit[:, 8, :], 0.0))
                dve.wait_ge(logits_done, 1)
                dve.tensor_copy(logit[:, 0:8, :], PS[:, 6, 0:8 * E].rearrange("p (t e) -> p t e", t=8)).then_inc(logits_read, 1)
                dve.tensor_copy(logit[0:32, 8, :], PS[0:32, 6, 8 * E:9 * E]).then_inc(logits_read, 1)
                dve.wait_ge(logits_read, 2)
                for t in range(TT):
                    ins = dve.max(top8[:, t, :], logit[:, t, :])
                link(ins)
                for t in range(TT):
                    ins = dve.max_index(idx8[:, t, :], top8[:, t, :], logit[:, t, :])
                link(ins)
                dve.tensor_tensor(topw[:, 0, :], top8[:, :, 1], top8[:, :, 0], ALU.subtract).then_inc(diff_ready, 1)
                link(dve.tensor_copy(idxf[:], idx8[:, :, 0:2]))
                dve.wait_ge(exp2_done, 1)
                link(dve.tensor_scalar(topw[:, 2, :], topw[:, 1, :], 1.0, None, ALU.add))
                link(dve.reciprocal(topw[:, 2, :], topw[:, 2, :]))
                link(dve.tensor_tensor(topw[:, 3, :], topw[:, 1, :], topw[:, 2, :], ALU.mult))
                every = iota[:].unsqueeze(1).to_broadcast([128, TT, E])
                link(*[dve.tensor_tensor(wsel[:, k], every, idxf[:, :, k].unsqueeze(2).to_broadcast([128, TT, E]), ALU.is_equal)
                       for k in range(2)])
                link(*[dve.tensor_tensor(wsel[:, k], wsel[:, k], topw[:, 2 + k, :].unsqueeze(2).to_broadcast([128, TT, E]),
                                         ALU.mult) for k in range(2)])
                link(dve.tensor_tensor(wE[:], wsel[:, 0], wsel[:, 1], ALU.add))

            def dve_pair(e2):
                hidden(e2, 0)
                if isinstance(e2, int):
                    route()
                for k in range(1, 6):
                    hidden(e2, k)
                    add_down(e2, k - 1)
                add_down(e2, 5)

            dve_pair(0)
            with dve.Fori(1, E // 2) as e2:
                dve_pair(e2)


def haar_matrix(np):
    one = np.array([[1.0, 1.0], [1.0, -1.0]])
    k = np.arange(256)
    m = np.ones((256, 256))
    for level in range(4):
        band = k >> 2 * (3 - level) & 3
        y, x = k // 16 >> level & 1, k % 16 >> level & 1
        m *= one[band >> 1][:, x] * one[band & 1][:, y]
    return m / 16


def kernel(**inputs):
    import numpy as np
    import concourse.bacc as bacc
    from concourse.bass_utils import run_bass_kernel_spmd

    a = {k: np.asarray(v) for k, v in inputs.items()}
    tok = {k[7:]: v for k, v in a.items() if k.startswith("L0_tok_")}
    c = np.ascontiguousarray
    dws = np.stack([tok[k].reshape(D, 9) for k in ("pl_dw", "pg_dw", "f1_dw", "f2_dw", "f3_dw")], 1)
    pws = np.stack([tok[k].reshape(D, D).T for k in ("pl_pw", "pg_pw", "pg_w2", "f1_pw", "f2_pw", "f3_pw")])
    vecs = np.stack([tok[k].reshape(D) for k in
                     ("pl_b", "pl_pwb", "pg_b1", "pg_pwb", "pg_b2", "alpha", "f1_pwb", "f2_pwb")])
    rows = np.stack([tok["f3_pwb"], tok["ln_g"], tok["ln_b"], a["L0_attn_gamma"], a["L0_attn_beta"],
                     a["L0_attn_b_out"], a["cls_tok"].reshape(D), tok["cls"].reshape(D)])
    wgu = np.concatenate([a["L0_ffn_Wg"].transpose(0, 2, 1), a["L0_ffn_Wu"].transpose(0, 2, 1)], 2)
    arrays = {
        "patches": c(a["x"].reshape(2, BH, C, G, PATCH, G, PATCH).transpose(2, 4, 6, 0, 3, 5, 1)
                     .reshape(KC, 128, NP_).transpose(1, 0, 2)),
        "plw": c(tok["pl_w"].reshape(D, KC, 128).transpose(2, 1, 0)),
        "w1t": c(tok["pg_w1"].reshape(D, 2, 128, C).transpose(2, 1, 3, 0).reshape(128, 2, C * D)),
        "haar": c(haar_matrix(np).astype(np.float32).reshape(2, 128, 256).transpose(1, 0, 2)),
        "ident": np.eye(128, dtype=np.float32),
        "vecs": c(vecs.reshape(8, 2, HD).transpose(2, 0, 1)),
        "dws": c(dws.reshape(2, HD, 5, 9).transpose(1, 0, 2, 3)),
        "pws": c(pws.reshape(6, 2, HD, D).transpose(2, 0, 1, 3)),
        "rows": c(rows),
        "sparsity": c(a["L0_attn_sparsity"].reshape(1)),
        "wqkv": c(a["L0_attn_w_qkv"].T),
        "wout": c(a["L0_attn_w_out"].T.reshape(HC, 128, D).transpose(1, 0, 2)),
        "router": c(a["L0_ffn_router_w"].T),
        "iota": c(np.tile(np.arange(E, dtype=np.float32), (128, 1))),
        "wgu": c(wgu),
        "wd": c(a["L0_ffn_Wd"].transpose(0, 2, 1).reshape(E, HC, 128, D).transpose(0, 2, 1, 3)),
    }
    nc = bacc.Bacc("TRN2", target_bir_lowering=False, num_devices=1)
    args = [nc.dram_tensor(k, v.shape, mybir.dt.from_np(v.dtype), kind="ExternalInput").ap() for k, v in arrays.items()]
    args.append(nc.dram_tensor("out", (B, KEYS, D), F32, kind="ExternalOutput").ap())
    build_tower(nc, *args)
    r = run_bass_kernel_spmd(nc, [arrays], core_ids=[0])
    return r.results[0]["out"]
```
